# Optimizing a Trainium2 kernel written in Bass

```python
import numpy as np
import jax
import jax.numpy as jnp

def _softmax(x, axis=-1):
    return jax.nn.softmax(x, axis=axis)

def _gelu(x):
    return jax.nn.gelu(x, approximate=True)

def _silu(x):
    return jax.nn.silu(x)

def _sigmoid(x):
    return jax.nn.sigmoid(x)

def _layernorm(x, axis=-1, eps=1e-05):
    m = jnp.mean(x, axis=axis, keepdims=True)
    v = jnp.var(x, axis=axis, keepdims=True)
    return (x - m) / jnp.sqrt(v + eps)

def _scatter_add(tgt, idx, src, axis=0):
    return tgt.at[idx].add(src)

def _segment_sum(src, seg, n):
    return jax.ops.segment_sum(src, seg, n)
kernel_name = 'mk_recurrent_d2_jaxref_r8_ea5fa5'

def setup_inputs(seed: int=0):
    np.random.seed(seed)
    _w = jnp.asarray

    def _L0_attn_setup():
        import jax, jax.numpy as jnp
        import numpy as np
        import math
        FACTOR = 1
        key = jax.random.key(seed)
        x = jax.random.normal(key, (8, 64, 512), dtype=jnp.float32)
        return {'x': x}
    _L0_attn_in = _L0_attn_setup()

    def _L0_ffn_setup():
        import jax, jax.numpy as jnp
        import numpy as np
        HID, INT, LAT, NE, K = (512, 1024, 256, 8, 2)
        LN_EPS = 1e-05

        def _layernorm(x, gamma, beta):
            mu = jnp.mean(x, axis=-1, keepdims=True)
            var = jnp.var(x, axis=-1, keepdims=True)
            return (x - mu) * jax.lax.rsqrt(var + LN_EPS) * gamma + beta
        key = jax.random.key(seed)
        ks = jax.random.split(key, 8)
        s = lambda d: 1.0 / np.sqrt(d)
        return {'hidden_states': jax.random.normal(ks[0], (4, 256, HID), jnp.float32), 'gate_w': jax.random.normal(ks[1], (HID, NE), jnp.float32) * s(HID), 'up_w': jax.random.normal(ks[2], (HID, INT), jnp.float32) * s(HID), 'down_w': jax.random.normal(ks[3], (INT, HID), jnp.float32) * s(INT), 'fc1_w': jax.random.normal(ks[4], (HID, LAT), jnp.float32) * s(HID), 'fc2_w': jax.random.normal(ks[5], (LAT, HID), jnp.float32) * s(LAT), 'expert_w': jax.random.normal(ks[6], (LAT, LAT), jnp.float32), 'ln_gamma': jnp.ones((HID,), jnp.float32), 'ln_beta': jnp.zeros((HID,), jnp.float32)}
    _L0_ffn_in = _L0_ffn_setup()

    def _L1_attn_setup():
        import jax, jax.numpy as jnp
        import numpy as np
        H_M, P_M, G_M, N_M, K_CONV, CHUNK = (128, 64, 8, 128, 4, 128)
        D_MODEL = 512
        D_INNER = H_M * P_M
        CONV_DIM = D_INNER + 2 * G_M * N_M
        PROJ_DIM = D_INNER + CONV_DIM + H_M
        EPS = 1e-05

        def segsum(x):
            l = x.shape[-1]
            xe = jnp.broadcast_to(x[..., None], x.shape + (l,))
            m1 = jnp.tril(jnp.ones((l, l), dtype=bool), -1)
            s = jnp.cumsum(jnp.where(m1, xe, 0.0), axis=-2)
            m2 = jnp.tril(jnp.ones((l, l), dtype=bool), 0)
            return jnp.where(m2, s, -jnp.inf)

        def causal_conv(x, w, bconv):
            k = w.shape[1]
            s = x.shape[1]
            xp = jnp.pad(x, ((0, 0), (k - 1, 0), (0, 0)))
            y = sum((xp[:, i:i + s, :] * w[:, i] for i in range(k)))
            return y + bconv
        key = jax.random.key(seed)
        ks = jax.random.split(key, 8)
        B_, S = (1, 256)
        sc = 0.02
        return {'x': jax.random.normal(ks[0], (B_, S, D_MODEL), dtype=jnp.float32), 'norm_w': jnp.ones((D_MODEL,), dtype=jnp.float32), 'in_proj_w': jax.random.normal(ks[1], (PROJ_DIM, D_MODEL), dtype=jnp.float32) * sc, 'conv_w': jax.random.normal(ks[2], (CONV_DIM, K_CONV), dtype=jnp.float32) * 0.2, 'conv_b': jnp.zeros((CONV_DIM,), dtype=jnp.float32), 'dt_bias': jax.random.uniform(ks[3], (H_M,), dtype=jnp.float32) * 0.1, 'A_log': jnp.log(1.0 + 15.0 * jax.random.uniform(ks[4], (H_M,), dtype=jnp.float32)), 'Dp': jnp.ones((H_M,), dtype=jnp.float32), 'gnorm_w': jnp.ones((D_INNER,), dtype=jnp.float32), 'out_proj_w': jax.random.normal(ks[5], (D_MODEL, D_INNER), dtype=jnp.float32) * sc}
    _L1_attn_in = _L1_attn_setup()

    def _L1_ffn_setup():
        import jax, jax.numpy as jnp
        import numpy as np
        H = 512
        I = 1792
        G = 128

        def dequant(q, s, g=G):
            O, In = q.shape
            return (q.reshape(O, In // g, g).astype(s.dtype) * s[:, :, None]).reshape(O, In)
        key = jax.random.key(seed)
        ks = jax.random.split(key, 7)
        x = jax.random.normal(ks[0], (2, 256, H), dtype=jnp.float32)

        def mk_qlinear(kq, ksc, out_d, in_d):
            q = jax.random.randint(kq, (out_d, in_d), -8, 8, dtype=jnp.int32)
            s = jax.random.uniform(ksc, (out_d, in_d // G), dtype=jnp.float32, minval=0.005, maxval=0.02)
            return (q, s)
        gate_q, gate_s = mk_qlinear(ks[1], ks[2], I, H)
        up_q, up_s = mk_qlinear(ks[3], ks[4], I, H)
        down_q, down_s = mk_qlinear(ks[5], ks[6], H, I)
        return {'x': x, 'gate_q': gate_q, 'gate_s': gate_s, 'up_q': up_q, 'up_s': up_s, 'down_q': down_q, 'down_s': down_s}
    _L1_ffn_in = _L1_ffn_setup()
    _d = {'L0_attn_x': _L0_attn_in['x'], 'L0_ffn_gate_w': _L0_ffn_in['gate_w'], 'L0_ffn_up_w': _L0_ffn_in['up_w'], 'L0_ffn_down_w': _L0_ffn_in['down_w'], 'L0_ffn_fc1_w': _L0_ffn_in['fc1_w'], 'L0_ffn_fc2_w': _L0_ffn_in['fc2_w'], 'L0_ffn_expert_w': _L0_ffn_in['expert_w'], 'L0_ffn_ln_gamma': _L0_ffn_in['ln_gamma'], 'L0_ffn_ln_beta': _L0_ffn_in['ln_beta'], 'L1_attn_norm_w': _L1_attn_in['norm_w'], 'L1_attn_in_proj_w': _L1_attn_in['in_proj_w'], 'L1_attn_conv_w': _L1_attn_in['conv_w'], 'L1_attn_conv_b': _L1_attn_in['conv_b'], 'L1_attn_dt_bias': _L1_attn_in['dt_bias'], 'L1_attn_A_log': _L1_attn_in['A_log'], 'L1_attn_Dp': _L1_attn_in['Dp'], 'L1_attn_gnorm_w': _L1_attn_in['gnorm_w'], 'L1_attn_out_proj_w': _L1_attn_in['out_proj_w'], 'L1_ffn_gate_q': _L1_ffn_in['gate_q'], 'L1_ffn_gate_s': _L1_ffn_in['gate_s'], 'L1_ffn_up_q': _L1_ffn_in['up_q'], 'L1_ffn_up_s': _L1_ffn_in['up_s'], 'L1_ffn_down_q': _L1_ffn_in['down_q'], 'L1_ffn_down_s': _L1_ffn_in['down_s']}
    _x0 = _d['L0_attn_x']
    _d['L0_attn_x'] = jax.random.normal(jax.random.fold_in(jax.random.key(seed), 1), (2, 512, 512), dtype=_x0.dtype)
    del _x0
    return _d

def reference(L0_attn_x, L0_ffn_gate_w, L0_ffn_up_w, L0_ffn_down_w, L0_ffn_fc1_w, L0_ffn_fc2_w, L0_ffn_expert_w, L0_ffn_ln_gamma, L0_ffn_ln_beta, L1_attn_norm_w, L1_attn_in_proj_w, L1_attn_conv_w, L1_attn_conv_b, L1_attn_dt_bias, L1_attn_A_log, L1_attn_Dp, L1_attn_gnorm_w, L1_attn_out_proj_w, L1_ffn_gate_q, L1_ffn_gate_s, L1_ffn_up_q, L1_ffn_up_s, L1_ffn_down_q, L1_ffn_down_s):

    def _L0_attn_ref(x):
        import jax, jax.numpy as jnp
        import numpy as np
        import math
        FACTOR = 1
        B, C, L = x.shape
        xh = x[:, None]
        f = jnp.fft.rfft(xh, axis=-1)
        corr = jnp.fft.irfft(f * jnp.conj(f), n=L, axis=-1)
        top_k = int(FACTOR * math.log(L))
        weights, delay = jax.lax.top_k(corr, top_k)
        tmp_corr = jax.nn.softmax(weights, axis=-1)
        init_index = jnp.arange(L)
        idx = (init_index[None, None, None, None, :] + delay[..., None]) % L
        pattern = jnp.take_along_axis(xh[:, :, :, None, :], idx, axis=-1)
        delays_agg = jnp.sum(pattern * tmp_corr[..., None], axis=-2)
        return delays_agg[:, 0]

    def _L0_ffn_ref(hidden_states, gate_w, up_w, down_w, fc1_w, fc2_w, expert_w, ln_gamma, ln_beta):
        import jax, jax.numpy as jnp
        import numpy as np
        HID, INT, LAT, NE, K = (512, 1024, 256, 8, 2)
        LN_EPS = 1e-05

        def _layernorm(x, gamma, beta):
            mu = jnp.mean(x, axis=-1, keepdims=True)
            var = jnp.var(x, axis=-1, keepdims=True)
            return (x - mu) * jax.lax.rsqrt(var + LN_EPS) * gamma + beta
        logits = jnp.einsum('bsh,he->bse', hidden_states, gate_w)
        routing_weights, selected_experts = jax.lax.top_k(logits, K)
        h = jax.nn.relu(jnp.einsum('bsh,hi->bsi', hidden_states, up_w)) ** 2
        shared_out = jnp.einsum('bsi,ih->bsh', h, down_w)
        x_latent = jnp.einsum('bsh,hl->bsl', hidden_states, fc1_w)
        expert_out = jnp.einsum('bsl,lm->bsm', x_latent, expert_w)
        moe_out = expert_out * jnp.sum(routing_weights, axis=-1, keepdims=True)
        routed_out = jnp.einsum('bsl,lh->bsh', moe_out, fc2_w)
        return _layernorm(shared_out + routed_out, ln_gamma, ln_beta)

    def _L1_attn_ref(x, norm_w, in_proj_w, conv_w, conv_b, dt_bias, A_log, Dp, gnorm_w, out_proj_w):
        import jax, jax.numpy as jnp
        import numpy as np
        H_M, P_M, G_M, N_M, K_CONV, CHUNK = (128, 64, 8, 128, 4, 128)
        D_MODEL = 512
        D_INNER = H_M * P_M
        CONV_DIM = D_INNER + 2 * G_M * N_M
        PROJ_DIM = D_INNER + CONV_DIM + H_M
        EPS = 1e-05

        def segsum(x):
            l = x.shape[-1]
            xe = jnp.broadcast_to(x[..., None], x.shape + (l,))
            m1 = jnp.tril(jnp.ones((l, l), dtype=bool), -1)
            s = jnp.cumsum(jnp.where(m1, xe, 0.0), axis=-2)
            m2 = jnp.tril(jnp.ones((l, l), dtype=bool), 0)
            return jnp.where(m2, s, -jnp.inf)

        def causal_conv(x, w, bconv):
            k = w.shape[1]
            s = x.shape[1]
            xp = jnp.pad(x, ((0, 0), (k - 1, 0), (0, 0)))
            y = sum((xp[:, i:i + s, :] * w[:, i] for i in range(k)))
            return y + bconv
        b, s, _ = x.shape
        residual = x
        h = x * jax.lax.rsqrt(jnp.mean(x * x, axis=-1, keepdims=True) + EPS) * norm_w
        proj = jnp.einsum('bsd,od->bso', h, in_proj_w)
        gate = proj[..., :D_INNER]
        hBC = proj[..., D_INNER:D_INNER + CONV_DIM]
        dt = proj[..., D_INNER + CONV_DIM:]
        hBC = jax.nn.silu(causal_conv(hBC, conv_w, conv_b))
        hid = hBC[..., :D_INNER].reshape(b, s, H_M, P_M)
        B = hBC[..., D_INNER:D_INNER + G_M * N_M].reshape(b, s, G_M, N_M)
        C = hBC[..., D_INNER + G_M * N_M:].reshape(b, s, G_M, N_M)
        dt = jax.nn.softplus(dt + dt_bias)
        A = -jnp.exp(A_log)
        pad = -s % CHUNK
        D_res = Dp[None, None, :, None] * hid
        hid_dt = hid * dt[..., None]
        A_full = A[None, None, :] * dt

        def padseq(t):
            return jnp.pad(t, [(0, 0), (0, pad)] + [(0, 0)] * (t.ndim - 2))
        hid_dt, A_full, Bp, Cp = (padseq(hid_dt), padseq(A_full), padseq(B), padseq(C))
        S = s + pad
        c, l = (S // CHUNK, CHUNK)
        hc = hid_dt.reshape(b, c, l, H_M, P_M)
        Ac = A_full.reshape(b, c, l, H_M).transpose(0, 3, 1, 2)
        rep = H_M // G_M
        Bh = jnp.repeat(Bp.reshape(b, c, l, G_M, N_M), rep, axis=3)
        Ch = jnp.repeat(Cp.reshape(b, c, l, G_M, N_M), rep, axis=3)
        A_cs = jnp.cumsum(Ac, axis=-1)
        L = jnp.exp(segsum(Ac))
        M = jnp.einsum('bcihn,bcjhn->bcijh', Ch, Bh) * jnp.transpose(L, (0, 2, 3, 4, 1))
        Y_diag = jnp.einsum('bcijh,bcjhp->bcihp', M, hc)
        decay_states = jnp.exp(A_cs[..., -1:] - A_cs)
        states = jnp.einsum('bclhn,bhcl,bclhp->bchpn', Bh, decay_states, hc)
        A_last = jnp.pad(A_cs[..., -1], ((0, 0), (0, 0), (1, 0)))
        decay_chunk = jnp.exp(segsum(A_last))
        states_cat = jnp.concatenate([jnp.zeros_like(states[:, :1]), states], axis=1)
        prev_states = jnp.einsum('bhij,bjhpn->bihpn', decay_chunk, states_cat)[:, :-1]
        Y_off = jnp.einsum('bclhn,bchpn,bhcl->bclhp', Ch, prev_states, jnp.exp(A_cs))
        y = (Y_diag + Y_off).reshape(b, S, H_M, P_M)[:, :s] + D_res
        y = y.reshape(b, s, D_INNER)
        yg = y * jax.nn.silu(gate)
        gsz = D_INNER // G_M
        ygr = yg.reshape(b, s, G_M, gsz)
        ygr = ygr * jax.lax.rsqrt(jnp.mean(ygr * ygr, axis=-1, keepdims=True) + EPS)
        y = ygr.reshape(b, s, D_INNER) * gnorm_w
        out = jnp.einsum('bsd,od->bso', y, out_proj_w)
        return residual + out

    def _L1_ffn_ref(x, gate_q, gate_s, up_q, up_s, down_q, down_s):
        import jax, jax.numpy as jnp
        import numpy as np
        H = 512
        I = 1792
        G = 128

        def dequant(q, s, g=G):
            O, In = q.shape
            return (q.reshape(O, In // g, g).astype(s.dtype) * s[:, :, None]).reshape(O, In)
        Wg = dequant(gate_q, gate_s)
        Wu = dequant(up_q, up_s)
        Wd = dequant(down_q, down_s)
        gate_score = jax.nn.silu(jnp.einsum('bsh,ih->bsi', x, Wg))
        intermediate = gate_score * jnp.einsum('bsh,ih->bsi', x, Wu)
        return jnp.einsum('bsi,hi->bsh', intermediate, Wd)
    x = L0_attn_x
    xn = _layernorm(x, axis=-1)
    s = _L0_attn_ref(xn)
    g = _silu(_L0_ffn_ref(xn, L0_ffn_gate_w, L0_ffn_up_w, L0_ffn_down_w, L0_ffn_fc1_w, L0_ffn_fc2_w, L0_ffn_expert_w, L0_ffn_ln_gamma, L0_ffn_ln_beta))
    x = x + s * g
    xn = _layernorm(x, axis=-1)
    s = _L1_attn_ref(xn, L1_attn_norm_w, L1_attn_in_proj_w, L1_attn_conv_w, L1_attn_conv_b, L1_attn_dt_bias, L1_attn_A_log, L1_attn_Dp, L1_attn_gnorm_w, L1_attn_out_proj_w)
    g = _silu(_L1_ffn_ref(xn, L1_ffn_gate_q, L1_ffn_gate_s, L1_ffn_up_q, L1_ffn_up_s, L1_ffn_down_q, L1_ffn_down_s))
    x = x + s * g
    return x

_drawn_inputs = setup_inputs


def setup_inputs(seed=0):
    import zlib

    import numpy as np

    out = dict(_drawn_inputs(seed))
    spreads = {'L0_ffn_ln_gamma': (1.0, 0.2),
     'L0_ffn_ln_beta': (0.0, 0.1),
     'L1_attn_norm_w': (1.0, 0.2),
     'L1_attn_conv_b': (0.0, 0.1),
     'L1_attn_Dp': (1.0, 0.2),
     'L1_attn_gnorm_w': (1.0, 0.2)}
    factors = {}
    for name, (base, spread) in spreads.items():
        noise = np.random.default_rng([zlib.crc32(name.encode()), seed]).standard_normal(out[name].shape)
        drawn = base * np.exp(spread * noise) if base else spread * noise
        out[name] = jnp.asarray(drawn.astype(out[name].dtype))
    for name, factor in factors.items():
        out[name] = (out[name] * factor).astype(out[name].dtype)
    return out
```

```python
from contextlib import ExitStack

import concourse.bass as bass
from concourse import mybir

F32 = mybir.dt.float32
U32 = mybir.dt.uint32
I32 = mybir.dt.int32
ALU = mybir.AluOpType
ACT = mybir.ActivationFunctionType

P = 128
T = 1024
NT = T // P
D = 512
KD = D // P
NB = 2
SEQ = T // NB
TB = SEQ // P
TOPK = 6
EPS = 1e-5
UP = 1024
KU = UP // P
LAT = 256
KL = LAT // P
NE = 8
HEADS = 128
HP = 64
GROUPS = 8
NST = 128
HG = HEADS // GROUPS
CG = HG * HP
KC = CG // P
DI = HEADS * HP
CONV = 4
INT = 1792
KI = INT // P
QC = 896
NQ = 3 * D * INT // P // QC


class Sems:

    def __init__(self, nc, ctx):
        self.nc, self.ctx = nc, ctx

    def __call__(self, name):
        return self.ctx.enter_context(self.nc.semaphore(name))


def chain_on(eng, sem):
    n = [0]

    def link(ins):
        n[0] += 1
        ins.then_inc(sem, 1)
        eng.wait_ge(sem, n[0])
    return link


def layer0(nc, a, x1, ident, x1_dram, table):
    with ExitStack() as ctx:
        sem = Sems(nc, ctx)

        def sb(name, shape, dt=F32):
            return ctx.enter_context(nc.sbuf_tensor(name, shape, dt))

        xn = sb("xn", [P, NT, D])
        xnT = sb("xnT", [P, KD, T])
        dft = sb("dft", [P, KD, D])
        idft = sb("idft", [P, KD, D])
        upw = sb("upw", [P, KD, UP])
        downw = sb("downw", [P, KU, D])
        fc1w = sb("fc1w", [P, KD, LAT])
        expw = sb("expw", [P, KL, LAT])
        fc2w = sb("fc2w", [P, KL, D])
        gatew = sb("gatew", [P, KD, NE])
        gamma = sb("gamma", [P, D])
        beta = sb("beta", [P, D])
        rowbase = sb("rowbase", [P, NT, 8], U32)
        power = sb("power", [P, KD, SEQ])
        hid = sb("hid", [P, KU, SEQ])
        latT = sb("latT", [P, KL, SEQ])
        exoT = sb("exoT", [P, KL, SEQ])
        shifted = sb("shifted", [P, TOPK, D])
        mixed = sb("mixed", [P, TB, D])
        routed = sb("routed", [P, 2, D])
        z = sb("z", [P, TB, D])
        stats = sb("stats", [P, NT, 6])
        mv = sb("mv", [P, NT, 2])
        std = sb("std", [P, NT])
        rstd = sb("rstd", [P, NT])
        zstats = sb("zstats", [P, NT, 6])
        zmv = sb("zmv", [P, NT, 2])
        zstd = sb("zstd", [P, NT])
        zrstd = sb("zrstd", [P, NT])
        top = sb("top", [P, NT, 8])
        delay = sb("delay", [P, NT, 8], U32)
        at = sb("at", [P, NT, 8], U32)
        negmax = sb("negmax", [P, NT])
        wexp = sb("wexp", [P, NT, 8])
        wsum = sb("wsum", [P, NT])
        wrec = sb("wrec", [P, NT])
        topl = sb("topl", [P, NT, 8])
        rsum = sb("rsum", [P, NT])
        ps_a = ctx.enter_context(nc.psum_tensor("ps_a", [P, 4, 512], F32))
        ps_d = ctx.enter_context(nc.psum_tensor("ps_d", [P, 4, 512], F32))

        x_loaded = [sem(f"x_loaded{t}") for t in range(NT)]
        ident_loaded = sem("ident_loaded")
        dft_loaded = sem("dft_loaded")
        idft_loaded = sem("idft_loaded")
        up_loaded = sem("up_loaded")
        small_loaded = sem("small_loaded")
        down_loaded = sem("down_loaded")
        rows_loaded = sem("rows_loaded")
        dve_chain = sem("dve_chain")
        act_chain = sem("act_chain")
        pool_chain = sem("pool_chain")
        var_ready = sem("var_ready")
        std_ready = sem("std_ready")
        xn_ready = sem("xn_ready")
        table_stored = sem("table_stored")
        pe_a = sem("pe_a")
        act_took = sem("act_took")
        pe_d = sem("pe_d")
        dve_took = sem("dve_took")
        squared = sem("squared")
        topk_ready = sem("topk_ready")
        weights_ready = sem("weights_ready")
        gathered = sem("gathered")
        mixed_ready = sem("mixed_ready")
        z_ready = sem("z_ready")
        zvar_ready = sem("zvar_ready")
        zstd_ready = sem("zstd_ready")
        zn_ready = sem("zn_ready")
        affine_ready = sem("affine_ready")
        silu_ready = sem("silu_ready")
        x1_ready = sem("x1_ready")
        x1_stored = sem("x1_stored")

        A_N, D_N = 2 * KD + KU + 2 * KL, 3 * TB

        def a_dft(n, m): return NT + A_N * n + m
        def a_up(n, m): return NT + A_N * n + KD + m
        def a_lat(n, m): return NT + A_N * n + KD + KU + m
        def a_exo(n, m): return NT + A_N * n + KD + KU + KL + m
        def a_rout(n, t): return NT + A_N * n + KD + KU + 2 * KL + t
        def d_corr(n, t): return D_N * n + t
        def d_log(n, t): return D_N * n + TB + t
        def d_shared(n, t): return D_N * n + 2 * TB + t

        block = ctx.enter_context(nc.Block())

        @block.sync
        def _(sp):
            x_view = a["x"].rearrange("(t p) d -> p t d", p=P)
            for t in range(NT):
                sp.dma_start(x1[:, t, :], x_view[:, t, :]).then_inc(x_loaded[t], 16)
            sp.dma_start(ident[:], a["ident"]).then_inc(ident_loaded, 16)
            sp.dma_start(dft[:], a["dft"]).then_inc(dft_loaded, 16)
            sp.dma_start(idft[:], a["idft"]).then_inc(idft_loaded, 16)
            sp.dma_start(rowbase[:], a["rowbase"]).then_inc(rows_loaded, 16)
            sp.dma_start(gamma[:], a["gamma"].to_broadcast((P, D))).then_inc(rows_loaded, 16)
            sp.dma_start(beta[:], a["beta"].to_broadcast((P, D))).then_inc(rows_loaded, 16)
            sp.dma_start(upw[:], a["up_w"].rearrange("(k p) n -> p k n", p=P)).then_inc(up_loaded, 16)
            sp.dma_start(fc1w[:], a["fc1_w"].rearrange("(k p) n -> p k n", p=P)).then_inc(small_loaded, 16)
            sp.dma_start(expw[:], a["expert_w"].rearrange("(k p) n -> p k n", p=P)).then_inc(small_loaded, 16)
            sp.dma_start(fc2w[:], a["fc2_w"].rearrange("(k p) n -> p k n", p=P)).then_inc(small_loaded, 16)
            sp.dma_start(gatew[:], a["gate_w"].rearrange("(k p) n -> p k n", p=P)).then_inc(small_loaded, 16)
            sp.dma_start(downw[:], a["down_w"].rearrange("(k p) n -> p k n", p=P)).then_inc(down_loaded, 16)
            for t in range(NT):
                sp.wait_ge(xn_ready, t + 1)
                for half in range(2):
                    sp.dma_start(table[t * P:(t + 1) * P, half * D:(half + 1) * D],
                                 xn[:, t, :]).then_inc(table_stored, 16)
            for t in range(NT):
                sp.wait_ge(x1_ready, t + 1)
                sp.dma_start(x1_dram[:, t, :], x1[:, t, :]).then_inc(x1_stored, 16)
            sp.wait_ge(x1_stored, 16 * NT)
            sp.wait_ge(table_stored, 32 * NT)

        @block.tensor
        def _(pe):
            def turn(eng_sem, i, base=4):
                if i >= base:
                    pe.wait_ge(eng_sem, i - base + 1)

            pe.wait_ge(ident_loaded, 16)
            for t in range(NT):
                pe.wait_ge(xn_ready, t + 1)
                turn(act_took, t)
                for k in range(KD):
                    mm = nc.tensor.transpose(ps_a[:, t % 4, k * P:(k + 1) * P],
                                             xn[:, t, k * P:(k + 1) * P], ident[:])
                mm.then_inc(pe_a, 1)
            pe.wait_ge(dft_loaded, 16)
            for n in range(NB):
                cols = slice(n * SEQ, (n + 1) * SEQ)
                pe.wait_ge(act_took, (n + 1) * TB)
                for m in range(KD):
                    i = a_dft(n, m)
                    turn(act_took, i)
                    for k in range(KD):
                        mm = nc.tensor.matmul(ps_a[:, i % 4, :], dft[:, k, m * P:(m + 1) * P],
                                              xnT[:, k, cols], start=(k == 0), stop=(k == KD - 1))
                    mm.then_inc(pe_a, 1)
                pe.wait_ge(up_loaded, 16)
                for m in range(KU):
                    i = a_up(n, m)
                    turn(act_took, i)
                    for k in range(KD):
                        mm = nc.tensor.matmul(ps_a[:, i % 4, :], upw[:, k, m * P:(m + 1) * P],
                                              xnT[:, k, cols], start=(k == 0), stop=(k == KD - 1))
                    mm.then_inc(pe_a, 1)
                pe.wait_ge(idft_loaded, 16)
                for t in range(TB):
                    i = d_corr(n, t)
                    turn(dve_took, i)
                    for k in range(KD):
                        mm = nc.tensor.matmul(ps_d[:, i % 4, :], power[:, k, t * P:(t + 1) * P],
                                              idft[:, k, :], start=(k == 0), stop=(k == KD - 1))
                    mm.then_inc(pe_d, 1)
                pe.wait_ge(small_loaded, 64)
                for m in range(KL):
                    i = a_lat(n, m)
                    turn(act_took, i)
                    for k in range(KD):
                        mm = nc.tensor.matmul(ps_a[:, i % 4, :], fc1w[:, k, m * P:(m + 1) * P],
                                              xnT[:, k, cols], start=(k == 0), stop=(k == KD - 1))
                    mm.then_inc(pe_a, 1)
                for t in range(TB):
                    i = d_log(n, t)
                    turn(dve_took, i)
                    for k in range(KD):
                        mm = nc.tensor.matmul(ps_d[:, i % 4, 0:NE],
                                              xnT[:, k, n * SEQ + t * P:n * SEQ + (t + 1) * P],
                                              gatew[:, k, :], start=(k == 0), stop=(k == KD - 1))
                    mm.then_inc(pe_d, 1)
                pe.wait_ge(act_took, a_lat(n, KL - 1) + 1)
                for m in range(KL):
                    i = a_exo(n, m)
                    for k in range(KL):
                        mm = nc.tensor.matmul(ps_a[:, i % 4, :], expw[:, k, m * P:(m + 1) * P],
                                              latT[:, k, :], start=(k == 0), stop=(k == KL - 1))
                    mm.then_inc(pe_a, 1)
                pe.wait_ge(down_loaded, 16)
                pe.wait_ge(squared, (n + 1) * KU)
                for t in range(TB):
                    i = d_shared(n, t)
                    turn(dve_took, i)
                    for k in range(KU):
                        mm = nc.tensor.matmul(ps_d[:, i % 4, :], hid[:, k, t * P:(t + 1) * P],
                                              downw[:, k, :], start=(k == 0), stop=(k == KU - 1))
                    mm.then_inc(pe_d, 1)
                    j = a_rout(n, t)
                    pe.wait_ge(act_took, max(a_exo(n, KL - 1) + 1, j - 3))
                    for k in range(KL):
                        mm = nc.tensor.matmul(ps_a[:, j % 4, :], exoT[:, k, t * P:(t + 1) * P],
                                              fc2w[:, k, :], start=(k == 0), stop=(k == KL - 1))
                    mm.then_inc(pe_a, 1)

        @block.scalar
        def _(act):
            act.wait_ge(var_ready, NT)
            nc.scalar.activation(std[:], mv[:, :, 1], ACT.Sqrt).then_inc(std_ready, 1)
            for t in range(NT):
                act.wait_ge(pe_a, t + 1)
                nc.scalar.activation(xnT[:, :, t * P:(t + 1) * P],
                                     ps_a[:, t % 4, :].rearrange("p (k c) -> p k c", k=KD),
                                     ACT.Copy).then_inc(act_took, 1)
            for n in range(NB):
                for m in range(KD):
                    i = a_dft(n, m)
                    act.wait_ge(pe_a, i + 1)
                    if n:
                        act.wait_ge(pe_d, d_corr(n - 1, TB - 1) + 1)
                    nc.scalar.activation(power[:, m, :], ps_a[:, i % 4, :], ACT.Square).then_inc(act_took, 1)
                for m in range(KU):
                    i = a_up(n, m)
                    act.wait_ge(pe_a, i + 1)
                    if n:
                        act.wait_ge(pe_d, d_shared(n - 1, TB - 1) + 1)
                    nc.scalar.activation(hid[:, m, :], ps_a[:, i % 4, :], ACT.Relu).then_inc(act_took, 1)
                for m in range(KL):
                    i = a_lat(n, m)
                    act.wait_ge(pe_a, i + 1)
                    nc.scalar.activation(latT[:, m, :], ps_a[:, i % 4, :], ACT.Copy).then_inc(act_took, 1)
                for m in range(KL):
                    i = a_exo(n, m)
                    act.wait_ge(pe_a, i + 1)
                    nc.scalar.activation(exoT[:, m, :], ps_a[:, i % 4, :], ACT.Copy).then_inc(act_took, 1)
                for t in range(TB):
                    g = n * TB + t
                    act.wait_ge(topk_ready, g + 1)
                    nc.scalar.activation(wexp[:, g, 0:TOPK], top[:, g, 0:TOPK], ACT.Exp, bias=negmax[:, g:g + 1],
                                         accum_out=wsum[:, g:g + 1]).then_inc(weights_ready, 1)
                for t in range(TB):
                    g, i = n * TB + t, a_rout(n, t)
                    act.wait_ge(pe_a, i + 1)
                    act.wait_ge(dve_took, d_log(n, TB - 1) + 1)
                    if t >= 2:
                        act.wait_ge(z_ready, g - 1)
                    nc.scalar.activation(routed[:, t % 2, :], ps_a[:, i % 4, :], ACT.Copy,
                                         scale=rsum[:, g:g + 1]).then_inc(act_took, 1)
                act.wait_ge(zvar_ready, (n + 1) * TB)
                nc.scalar.activation(zstd[:, n * TB:(n + 1) * TB], zmv[:, n * TB:(n + 1) * TB, 1],
                                     ACT.Sqrt).then_inc(zstd_ready, 1)
                for t in range(TB):
                    act.wait_ge(affine_ready, n * TB + t + 1)
                    nc.scalar.activation(z[:, t, :], z[:, t, :], ACT.Silu).then_inc(silu_ready, 1)

        @block.vector
        def _(dve):
            link = chain_on(dve, dve_chain)
            for t in range(NT):
                dve.wait_ge(x_loaded[t], 16)
                link(nc.vector.bn_stats(stats[:, t, :], x1[:, t, :]))
                link(nc.vector.bn_aggr(mv[:, t, :], stats[:, t, :]))
                nc.vector.tensor_scalar(mv[:, t, 1:2], mv[:, t, 1:2], EPS, None, ALU.add).then_inc(var_ready, 1)
            dve.wait_ge(std_ready, 1)
            link(nc.vector.reciprocal(rstd[:], std[:]))
            for t in range(NT):
                nc.vector.tensor_scalar(xn[:, t, :], x1[:, t, :], mv[:, t, 0:1], rstd[:, t:t + 1],
                                        ALU.subtract, ALU.mult).then_inc(xn_ready, 1)
            dve.wait_ge(rows_loaded, 48)
            for n in range(NB):
                for t in range(TB):
                    g, i = n * TB + t, d_corr(n, t)
                    dve.wait_ge(pe_d, i + 1)
                    link(nc.vector.max(top[:, g, :], ps_d[:, i % 4, :]))
                    nc.vector.max_index(delay[:, g, :], top[:, g, :], ps_d[:, i % 4, :]).then_inc(dve_took, 1)
                    dve.wait_ge(dve_took, i + 1)
                    link(nc.vector.tensor_tensor(at[:, g, :], delay[:, g, :], rowbase[:, g, :], ALU.add))
                    nc.vector.tensor_scalar(negmax[:, g:g + 1], top[:, g, 0:1], -1.0, None,
                                            ALU.mult).then_inc(topk_ready, 1)
                for t in range(TB):
                    g, i = n * TB + t, d_log(n, t)
                    dve.wait_ge(pe_d, i + 1)
                    link(nc.vector.max(topl[:, g, :], ps_d[:, i % 4, 0:NE]))
                    nc.vector.tensor_tensor(rsum[:, g:g + 1], topl[:, g, 0:1], topl[:, g, 1:2],
                                            ALU.add).then_inc(dve_took, 1)
                for t in range(TB):
                    g = n * TB + t
                    dve.wait_ge(weights_ready, g + 1)
                    link(nc.vector.reciprocal(wrec[:, g:g + 1], wsum[:, g:g + 1]))
                    link(nc.vector.tensor_scalar(wexp[:, g, 0:TOPK], wexp[:, g, 0:TOPK], wrec[:, g:g + 1], None,
                                                 ALU.mult))
                    dve.wait_ge(gathered, 16 * TOPK * (g + 1))
                    link(nc.vector.tensor_scalar(mixed[:, t, :], shifted[:, 0, :], wexp[:, g, 0:1], None, ALU.mult))
                    for j in range(1, TOPK):
                        add = nc.vector.scalar_tensor_tensor(mixed[:, t, :], shifted[:, j, :], wexp[:, g, j:j + 1],
                                                             mixed[:, t, :], ALU.mult, ALU.add)
                        if j < TOPK - 1:
                            link(add)
                    add.then_inc(mixed_ready, 1)
                for t in range(TB):
                    g, i = n * TB + t, d_shared(n, t)
                    dve.wait_ge(pe_d, i + 1)
                    dve.wait_ge(act_took, a_rout(n, t) + 1)
                    nc.vector.tensor_tensor(z[:, t, :], ps_d[:, i % 4, :], routed[:, t % 2, :],
                                            ALU.add).then_inc(z_ready, 1)
                    dve.wait_ge(z_ready, g + 1)
                    nc.vector.bn_stats(zstats[:, g, :], z[:, t, :]).then_inc(dve_took, 1)
                    dve.wait_ge(dve_took, i + 1)
                    link(nc.vector.bn_aggr(zmv[:, g, :], zstats[:, g, :]))
                    nc.vector.tensor_scalar(zmv[:, g, 1:2], zmv[:, g, 1:2], EPS, None,
                                            ALU.add).then_inc(zvar_ready, 1)
                dve.wait_ge(zstd_ready, n + 1)
                link(nc.vector.reciprocal(zrstd[:, n * TB:(n + 1) * TB], zstd[:, n * TB:(n + 1) * TB]))
                for t in range(TB):
                    g = n * TB + t
                    nc.vector.tensor_scalar(z[:, t, :], z[:, t, :], zmv[:, g, 0:1], zrstd[:, g:g + 1],
                                            ALU.subtract, ALU.mult).then_inc(zn_ready, 1)
                for t in range(TB):
                    g = n * TB + t
                    dve.wait_ge(silu_ready, g + 1)
                    dve.wait_ge(mixed_ready, g + 1)
                    link(nc.vector.tensor_tensor(mixed[:, t, :], mixed[:, t, :], z[:, t, :], ALU.mult))
                    nc.vector.tensor_tensor(x1[:, g, :], x1[:, g, :], mixed[:, t, :], ALU.add).then_inc(x1_ready, 1)
                dve.wait_ge(x1_ready, (n + 1) * TB)

        @block.gpsimd
        def _(pool):
            link = chain_on(pool, pool_chain)
            pool.wait_ge(rows_loaded, 48)
            for n in range(NB):
                for m in range(KU):
                    pool.wait_ge(act_took, a_up(n, m) + 1)
                    nc.gpsimd.tensor_tensor(hid[:, m, :], hid[:, m, :], hid[:, m, :], ALU.mult).then_inc(squared, 1)
                for t in range(TB):
                    g = n * TB + t
                    pool.wait_ge(table_stored, 32 * NT)
                    pool.wait_ge(topk_ready, g + 1)
                    if g:
                        pool.wait_ge(mixed_ready, g)
                    for j in range(TOPK):
                        nc.gpsimd.indirect_dma_start(
                            shifted[:, j, :], None, table.rearrange("r (c o) -> (r c) o", o=1),
                            bass.IndirectOffsetOnAxis(ap=at[:, g, j:j + 1], axis=0)).then_inc(gathered, 16)
                for t in range(TB):
                    g = n * TB + t
                    pool.wait_ge(zn_ready, g + 1)
                    link(nc.gpsimd.tensor_tensor(z[:, t, :], z[:, t, :], gamma[:], ALU.mult))
                    nc.gpsimd.tensor_tensor(z[:, t, :], z[:, t, :], beta[:], ALU.add).then_inc(affine_ready, 1)


def mixer_inputs(nc, a, xn, ident, ones, hT, xnT, dt_l, dd_l, nacs_l, chunk_decay, acs_dram):
    with ExitStack() as ctx:
        sem = Sems(nc, ctx)

        def sb(name, shape, dt=F32):
            return ctx.enter_context(nc.sbuf_tensor(name, shape, dt))

        stats = sb("m_stats", [P, NT, 6])
        mv = sb("m_mv", [P, NT, 2])
        std = sb("m_std", [P, NT])
        rstd = sb("m_rstd", [P, NT])
        square = sb("m_square", [P, D])
        meansq = sb("m_meansq", [P, NT])
        rms = sb("m_rms", [P, NT])
        rrms = sb("m_rrms", [P, NT])
        h = sb("m_h", [P, 2, D])
        normw = sb("m_normw", [P, KD])
        wdt = sb("m_wdt", [P, KD, HEADS])
        dtb = sb("m_dtb", [P, 1])
        alog = sb("m_alog", [P, 1])
        aexp = sb("m_aexp", [P, 1])
        v = sb("m_v", [P, T])
        av = sb("m_av", [P, T])
        e = sb("m_e", [P, T])
        u1 = sb("m_u1", [P, T])
        ln = sb("m_ln", [P, T])
        z = sb("m_z", [P, T])
        dt = sb("m_dt", [P, T])
        step = sb("m_step", [P, T])
        acs = sb("m_acs", [P, T])
        decay = sb("m_decay", [P, T])
        lastdecay = sb("m_lastdecay", [P, 4])
        diag = sb("m_diag", [P, 4, HEADS])
        ps = ctx.enter_context(nc.psum_tensor("m_ps", [P, 8, 512], F32))

        loaded = sem("m_loaded")
        dve_chain = sem("m_dve_chain")
        act_chain = sem("m_act_chain")
        var_ready = sem("m_var_ready")
        std_ready = sem("m_std_ready")
        xn_ready = sem("m_xn_ready")
        meansq_ready = sem("m_meansq_ready")
        meansq_eps = sem("m_meansq_eps")
        rms_ready = sem("m_rms_ready")
        h_ready = sem("m_h_ready")
        xn_turned = sem("m_xn_turned")
        h_turned = sem("m_h_turned")
        xnT_ready = sem("m_xnT_ready")
        hT_ready = sem("m_hT_ready")
        dt_proj = sem("m_dt_proj")
        v_ready = sem("m_v_ready")
        e_ready = sem("m_e_ready")
        u1_ready = sem("m_u1_ready")
        ln_ready = sem("m_ln_ready")
        dt_ready = sem("m_dt_ready")
        aexp_ready = sem("m_aexp_ready")
        acs_ready = sem("m_acs_ready")
        decay_ready = sem("m_decay_ready")
        lastdecay_ready = sem("m_lastdecay_ready")
        dd_ready = sem("m_dd_ready")
        diag_ready = sem("m_diag_ready")
        turned = sem("m_turned")
        acs_stored = sem("m_acs_stored")
        ones_ready = sem("m_ones_ready")

        block = ctx.enter_context(nc.Block())

        @block.sync
        def _(sp):
            sp.dma_start(normw[:], a["norm_w"]).then_inc(loaded, 16)
            sp.dma_start(wdt[:], a["w_dt"]).then_inc(loaded, 16)
            sp.dma_start(dtb[:], a["dt_bias"]).then_inc(loaded, 16)
            sp.dma_start(alog[:], a["a_log"]).then_inc(loaded, 16)
            sp.wait_ge(acs_ready, NT)
            sp.dma_start(acs_dram, acs[:]).then_inc(acs_stored, 16)
            sp.wait_ge(acs_stored, 16)

        @block.gpsimd
        def _(pool):
            nc.gpsimd.memset(ones[:], 1.0).then_inc(ones_ready, 1)
            pool.wait_ge(ones_ready, 1)

        @block.tensor
        def _(pe):
            for t in range(NT):
                pe.wait_ge(xn_ready, t + 1)
                if t >= 2:
                    pe.wait_ge(xnT_ready, t - 1)
                for k in range(KD):
                    mm = nc.tensor.transpose(ps[:, t % 2, k * P:(k + 1) * P], xn[:, t, k * P:(k + 1) * P], ident[:])
                mm.then_inc(xn_turned, 1)
                pe.wait_ge(h_ready, t + 1)
                if t >= 2:
                    pe.wait_ge(hT_ready, t - 1)
                for k in range(KD):
                    mm = nc.tensor.transpose(ps[:, 2 + t % 2, k * P:(k + 1) * P],
                                             h[:, t % 2, k * P:(k + 1) * P], ident[:])
                mm.then_inc(h_turned, 1)
            pe.wait_ge(loaded, 64)
            pe.wait_ge(hT_ready, NT)
            for n in range(NB):
                for k in range(KD):
                    mm = nc.tensor.matmul(ps[:, 4 + n, :], wdt[:, k, :], hT[:, k, n * SEQ:(n + 1) * SEQ],
                                          start=(k == 0), stop=(k == KD - 1))
                mm.then_inc(dt_proj, 1)
            pe.wait_ge(xnT_ready, NT)
            pe.wait_ge(dt_ready, 1)
            for t in range(NT):
                mm = nc.tensor.transpose(ps[:, t // 4, (t % 4) * P:(t % 4 + 1) * P], dt[:, t * P:(t + 1) * P], ident[:])
            mm.then_inc(turned, 1)
            pe.wait_ge(acs_ready, NT)
            for t in range(NT):
                mm = nc.tensor.transpose(ps[:, 2 + t // 4, (t % 4) * P:(t % 4 + 1) * P], acs[:, t * P:(t + 1) * P],
                                         ident[:])
            mm.then_inc(turned, 1)
            pe.wait_ge(dd_ready, 1)
            for t in range(NT):
                mm = nc.tensor.transpose(ps[:, 6 + t // 4, (t % 4) * P:(t % 4 + 1) * P], decay[:, t * P:(t + 1) * P],
                                         ident[:])
            mm.then_inc(turned, 1)
            pe.wait_ge(diag_ready, 4)
            pe.wait_ge(ones_ready, 1)
            pe.wait_ge(v_ready, NB)
            mm = nc.tensor.matmul(ps[:, 4, :], ones[:], diag[:].rearrange("p c h -> p (c h)"), start=True, stop=True)
            mm.then_inc(turned, 1)

        @block.scalar
        def _(act):
            act.wait_ge(var_ready, NT)
            nc.scalar.activation(std[:], mv[:, :, 1], ACT.Sqrt).then_inc(std_ready, 1)
            for t in range(NT):
                act.wait_ge(xn_ready, t + 1)
                if t:
                    act.wait_ge(meansq_ready, t)
                nc.scalar.activation(square[:], xn[:, t, :], ACT.Square,
                                     accum_out=meansq[:, t:t + 1]).then_inc(meansq_ready, 1)
            act.wait_ge(meansq_eps, 1)
            nc.scalar.activation(rms[:], meansq[:], ACT.Sqrt).then_inc(rms_ready, 1)
            for t in range(NT):
                act.wait_ge(xn_turned, t + 1)
                nc.scalar.activation(xnT[:, :, t * P:(t + 1) * P],
                                     ps[:, t % 2, :].rearrange("p (k c) -> p k c", k=KD),
                                     ACT.Copy).then_inc(xnT_ready, 1)
            act.wait_ge(v_ready, NB)
            nc.scalar.activation(av[:], v[:], ACT.Abs).then_inc(act_chain, 1)
            act.wait_ge(act_chain, 1)
            nc.scalar.activation(e[:], av[:], ACT.Exp, scale=-1.0).then_inc(e_ready, 1)
            act.wait_ge(loaded, 64)
            nc.scalar.activation(aexp[:], alog[:], ACT.Exp).then_inc(aexp_ready, 1)
            act.wait_ge(u1_ready, 1)
            nc.scalar.activation(ln[:], u1[:], ACT.Ln).then_inc(ln_ready, 1)
            for t in range(NT):
                act.wait_ge(acs_ready, t + 1)
                last = acs[:, (t + 1) * P - 1:(t + 1) * P]
                nc.scalar.activation(decay[:, t * P:(t + 1) * P], acs[:, t * P:(t + 1) * P], ACT.Exp,
                                     bias=last, scale=-1.0).then_inc(decay_ready, 1)
            for i, t in enumerate((1, 2, 5, 6)):
                ins = nc.scalar.activation(lastdecay[:, i:i + 1], acs[:, (t + 1) * P - 1:(t + 1) * P], ACT.Exp)
            ins.then_inc(lastdecay_ready, 1)

        @block.vector
        def _(dve):
            link = chain_on(dve, dve_chain)
            for t in range(NT):
                link(nc.vector.bn_stats(stats[:, t, :], xn[:, t, :]))
                link(nc.vector.bn_aggr(mv[:, t, :], stats[:, t, :]))
                nc.vector.tensor_scalar(mv[:, t, 1:2], mv[:, t, 1:2], EPS, None, ALU.add).then_inc(var_ready, 1)
            dve.wait_ge(std_ready, 1)
            link(nc.vector.reciprocal(rstd[:], std[:]))
            for t in range(NT):
                nc.vector.tensor_scalar(xn[:, t, :], xn[:, t, :], mv[:, t, 0:1], rstd[:, t:t + 1],
                                        ALU.subtract, ALU.mult).then_inc(xn_ready, 1)
            dve.wait_ge(meansq_ready, NT)
            nc.vector.tensor_scalar(meansq[:], meansq[:], 1.0 / D, EPS, ALU.mult, ALU.add).then_inc(meansq_eps, 1)
            dve.wait_ge(rms_ready, 1)
            link(nc.vector.reciprocal(rrms[:], rms[:]))
            dve.wait_ge(loaded, 64)
            dve.wait_ge(xn_ready, NT)
            for t in range(NT + 1):
                if t < NT:
                    if t >= 2:
                        dve.wait_ge(h_turned, t - 1)
                    nc.vector.tensor_scalar(h[:, t % 2, :], xn[:, t, :], rrms[:, t:t + 1], None,
                                            ALU.mult).then_inc(h_ready, 1)
                if t:
                    s = t - 1
                    dve.wait_ge(h_turned, s + 1)
                    nc.vector.tensor_tensor(hT[:, :, s * P:(s + 1) * P],
                                            ps[:, 2 + s % 2, :].rearrange("p (k c) -> p k c", k=KD),
                                            normw[:].unsqueeze(2).to_broadcast((P, KD, P)),
                                            ALU.mult).then_inc(hT_ready, 1)
            for n in range(NB):
                dve.wait_ge(dt_proj, n + 1)
                nc.vector.tensor_scalar(v[:, n * SEQ:(n + 1) * SEQ], ps[:, 4 + n, :], dtb[:, 0:1], None,
                                        ALU.add).then_inc(v_ready, 1)
            dve.wait_ge(e_ready, 1)
            nc.vector.tensor_scalar(u1[:], e[:], 1.0, None, ALU.add).then_inc(u1_ready, 1)
            dve.wait_ge(u1_ready, 1)
            link(nc.vector.tensor_scalar(av[:], u1[:], -1.0, None, ALU.add))
            link(nc.vector.tensor_scalar(z[:], av[:], 0.0, None, ALU.is_equal))
            link(nc.vector.tensor_tensor(av[:], av[:], z[:], ALU.add))
            link(nc.vector.reciprocal(step[:], av[:]))
            link(nc.vector.tensor_tensor(step[:], step[:], e[:], ALU.mult))
            link(nc.vector.tensor_tensor(z[:], z[:], e[:], ALU.mult))
            dve.wait_ge(ln_ready, 1)
            link(nc.vector.tensor_tensor(ln[:], ln[:], step[:], ALU.mult))
            link(nc.vector.tensor_tensor(ln[:], ln[:], z[:], ALU.add))
            nc.vector.scalar_tensor_tensor(dt[:], v[:], 0.0, ln[:], ALU.max, ALU.add).then_inc(dt_ready, 1)
            dve.wait_ge(dt_ready, 1)
            dve.wait_ge(aexp_ready, 1)
            link(nc.vector.tensor_scalar(step[:], dt[:], aexp[:, 0:1], -1.0, ALU.mult, ALU.mult))
            link(nc.vector.memset(u1[:], 1.0))
            for t in range(NT):
                c = slice(t * P, (t + 1) * P)
                nc.vector.tensor_tensor_scan(acs[:, c], u1[:, c], step[:, c], 0.0, ALU.mult,
                                             ALU.add).then_inc(acs_ready, 1)
            dve.wait_ge(decay_ready, NT)
            nc.vector.tensor_tensor(decay[:], decay[:], dt[:], ALU.mult).then_inc(dd_ready, 1)
            dve.wait_ge(lastdecay_ready, 1)
            for i in range(4):
                nc.vector.tensor_scalar(diag[:, i, :], ident[:], lastdecay[:, i:i + 1], None,
                                        ALU.mult).then_inc(diag_ready, 1)

            def banks(b):
                return ps[:, b:b + 2, :].rearrange("p b (t h) -> p (b t) h", t=4)
            dve.wait_ge(turned, 1)
            nc.vector.tensor_copy(dt_l[:], banks(0))
            dve.wait_ge(turned, 2)
            nc.vector.tensor_scalar(nacs_l[:], banks(2), -1.0, None, ALU.mult)
            dve.wait_ge(turned, 3)
            nc.vector.tensor_copy(dd_l[:], banks(6))
            dve.wait_ge(turned, 4)
            link(nc.vector.tensor_copy(chunk_decay[:].rearrange("p c h -> p (c h)"), ps[:, 4, :]))


def layer1_ffn(nc, a, xnT, g_dram):
    with ExitStack() as ctx:
        sem = Sems(nc, ctx)

        def sb(name, shape, dt=F32):
            return ctx.enter_context(nc.sbuf_tensor(name, shape, dt))

        w = sb("f_w", [P, NQ, QC])
        q = sb("f_q", [P, 2, QC], I32)
        s = sb("f_s", [P, 2, QC])
        gated = sb("f_gated", [P, 2, SEQ])
        inner = sb("f_inner", [P, KI, SEQ])
        g = sb("f_g", [P, 2, D])
        ps_gate = ctx.enter_context(nc.psum_tensor("f_ps_gate", [P, 2, 512], F32))
        ps_up = ctx.enter_context(nc.psum_tensor("f_ps_up", [P, 2, 512], F32))
        ps_out = ctx.enter_context(nc.psum_tensor("f_ps_out", [P, 2, 512], F32))

        piece_loaded = [sem("f_piece_loaded0"), sem("f_piece_loaded1")]
        dequantised = sem("f_dequantised")
        gate_done = sem("f_gate_done")
        up_done = sem("f_up_done")
        gate_silu = sem("f_gate_silu")
        inner_ready = sem("f_inner_ready")
        out_done = sem("f_out_done")
        g_ready = sem("f_g_ready")
        g_stored = [sem("f_g_stored0"), sem("f_g_stored1")]

        flat = w[:].rearrange("p n c -> p (n c)")
        w_gate = flat[:, 0:KD * INT].rearrange("p (k n) -> p k n", k=KD)
        w_up = flat[:, KD * INT:2 * KD * INT].rearrange("p (k n) -> p k n", k=KD)
        w_down = flat[:, 2 * KD * INT:].rearrange("p (k n) -> p k n", k=KI)
        block = ctx.enter_context(nc.Block())

        @block.sync
        def _(sp):
            for i in range(NQ):
                if i >= 2:
                    sp.wait_ge(dequantised, i - 1)
                sp.dma_start(q[:, i % 2, :], a["q"][i]).then_inc(piece_loaded[i % 2], 16)
                sp.dma_start(s[:, i % 2, :], a["s"][i:i + 1, :].to_broadcast((P, QC))).then_inc(
                    piece_loaded[i % 2], 16)
            for j in range(NT):
                sp.wait_ge(g_ready, j + 1)
                sp.dma_start(g_dram[:, j, :], g[:, j % 2, :]).then_inc(g_stored[j % 2], 16)
            for slot in g_stored:
                sp.wait_ge(slot, 16 * NT // 2)

        @block.tensor
        def _(pe):
            for n in range(NB):
                for m in range(KI):
                    j = n * KI + m
                    if n == 0:
                        pe.wait_ge(dequantised, 4 * KD)
                    if j >= 2:
                        pe.wait_ge(gate_silu, j - 1)
                        pe.wait_ge(inner_ready, j - 1)
                    for wt, bank, done in ((w_gate, ps_gate, gate_done), (w_up, ps_up, up_done)):
                        for k in range(KD):
                            mm = nc.tensor.matmul(bank[:, j % 2, :], wt[:, k, m * P:(m + 1) * P],
                                                  xnT[:, k, n * SEQ:(n + 1) * SEQ],
                                                  start=(k == 0), stop=(k == KD - 1))
                        mm.then_inc(done, 1)
                pe.wait_ge(dequantised, NQ)
                pe.wait_ge(inner_ready, (n + 1) * KI)
                for t in range(TB):
                    j = n * TB + t
                    if j >= 2:
                        pe.wait_ge(g_ready, j - 1)
                    for k in range(KI):
                        mm = nc.tensor.matmul(ps_out[:, j % 2, :], inner[:, k, t * P:(t + 1) * P], w_down[:, k, :],
                                              start=(k == 0), stop=(k == KI - 1))
                    mm.then_inc(out_done, 1)

        @block.scalar
        def _(act):
            for n in range(NB):
                for m in range(KI):
                    j = n * KI + m
                    act.wait_ge(gate_done, j + 1)
                    if j >= 2:
                        act.wait_ge(inner_ready, j - 1)
                    nc.scalar.activation(gated[:, j % 2, :], ps_gate[:, j % 2, :], ACT.Silu).then_inc(gate_silu, 1)
                for t in range(TB):
                    j = n * TB + t
                    act.wait_ge(out_done, j + 1)
                    if j >= 2:
                        act.wait_ge(g_stored[j % 2], 16 * (j // 2))
                    nc.scalar.activation(g[:, j % 2, :], ps_out[:, j % 2, :], ACT.Silu).then_inc(g_ready, 1)

        @block.vector
        def _(dve):
            for i in range(NQ):
                dve.wait_ge(piece_loaded[i % 2], 32 * (i // 2 + 1))
                nc.vector.tensor_tensor(w[:, i, :], q[:, i % 2, :], s[:, i % 2, :], ALU.mult).then_inc(dequantised, 1)
            for n in range(NB):
                if n:
                    dve.wait_ge(out_done, n * TB)
                for m in range(KI):
                    j = n * KI + m
                    dve.wait_ge(up_done, j + 1)
                    dve.wait_ge(gate_silu, j + 1)
                    nc.vector.tensor_tensor(inner[:, m, :], gated[:, j % 2, :], ps_up[:, j % 2, :],
                                            ALU.mult).then_inc(inner_ready, 1)


STATE_ORDER = [("T", 0), ("T", 1), ("ST", 0), ("T", 2), ("ST", 1), ("T", 3), ("ST", 2)]
S_JOBS = ([("CB", 0, 0)] + [(kind, c, half) for kind, c in STATE_ORDER for half in range(2)]
          + [(kind, k, 0) for k in range(KC) for kind in ("DIAG", "OFF")])
JOBS = ([("P", j) for j in range(KC + 2)] + [("OP", j) for j in range(TB + 1)]
        + [("S", j) for j in range(len(S_JOBS))])
NP_, NOP, NS_ = KC + 2, TB + 1, len(S_JOBS)
BANKS = 6
WIN_SLOTS = 3
R_SLOTS = 4
L_SLOTS = 4
CV_SLOTS = 2
CHUNKS_IN = (2 * KC + 2) // 2


def mixer(nc, a, acc, ident, ones, hT, dt_l, dd_l, nacs_l, chunk_decay, acs_dram, x1_dram, g_dram, out):
    with ExitStack() as ctx:
        sem = Sems(nc, ctx)

        def sb(name, shape, dt=F32):
            return ctx.enter_context(nc.sbuf_tensor(name, shape, dt))

        par = sb("s_par", [P, GROUPS, 66])
        mask = sb("s_mask", [P, P])
        conv_w = sb("s_conv_w", [P, 2, KC + 2, CONV])
        conv_b = sb("s_conv_b", [P, 2, KC + 2])
        skip = sb("s_skip", [P, 2, KC])
        gnorm = sb("s_gnorm", [P, 2, KC])
        dtg = sb("s_dtg", [P, 2, TB, HG])
        ddg = sb("s_ddg", [P, 2, TB, HG])
        nacg = sb("s_nacg", [P, 2, TB, HG])
        cdg = sb("s_cdg", [P, 2, 2, HG])
        win = sb("s_win", [P, WIN_SLOTS, 2, KD, P])
        wo = sb("s_wo", [P, KC, D])
        cv = sb("s_cv", [P, CV_SLOTS, SEQ])
        bT = sb("s_bT", [P, SEQ])
        cT = sb("s_cT", [P, SEQ])
        hid = sb("s_hid", [P, KC, SEQ])
        gate = sb("s_gate", [P, KC, SEQ])
        yT = sb("s_yT", [P, KC, SEQ])
        b_l = sb("s_b_l", [P, TB - 1, NST])
        cbt = sb("s_cbt", [P, TB, P])
        hdt = sb("s_hdt", [P, TB, CG])
        hdd = sb("s_hdd", [P, 2, CG])
        state = sb("s_state", [P, TB - 1, CG])
        carried = sb("s_carried", [P, CG])
        rows = sb("s_rows", [P, R_SLOTS, SEQ])
        lm = sb("s_lm", [P, L_SLOTS, SEQ])
        scale = sb("s_scale", [P, 2, 3 * P])
        ysum = sb("s_ysum", [P, 2, SEQ])
        yoff = sb("s_yoff", [P, 2, 3 * P])
        ssq = sb("s_ssq", [P, SEQ])
        meansq = sb("s_meansq", [P, TB])
        rms = sb("s_rms", [P, TB])
        rrms = sb("s_rrms", [P, TB])
        ps = ctx.enter_context(nc.psum_tensor("s_ps", [P, BANKS, 512], F32))
        ps_a = ctx.enter_context(nc.psum_tensor("s_ps_a", [P, 2, 512], F32))

        par_loaded = sem("s_par_loaded")
        params = sem("s_params")
        win_loaded = [sem(f"s_win_loaded{i}") for i in range(WIN_SLOTS)]
        wo_loaded = sem("s_wo_loaded")
        wo_scaled = sem("s_wo_scaled")
        rows_loaded = [sem(f"s_rows_loaded{i}") for i in range(R_SLOTS)]
        done = {"P": sem("s_p_done"), "OP": sem("s_op_done"), "S": sem("s_s_done")}
        took = {"P": sem("s_p_took"), "OP": sem("s_op_took"), "S": sem("s_s_took")}
        gate_done = sem("s_gate_done")
        gate_took = sem("s_gate_took")
        b_turned = sem("s_b_turned")
        b_took = sem("s_b_took")
        tap_ready = sem("s_tap_ready")
        conv_chain = sem("s_conv_chain")
        hbc_ready = sem("s_hbc_ready")
        diff_ready = sem("s_diff_ready")
        exp_ready = sem("s_exp_ready")
        scale_ready = sem("s_scale_ready")
        m_ready = sem("s_m_ready")
        carried_ready = sem("s_carried_ready")
        y_ready = sem("s_y_ready")
        pool_chain = sem("s_pool_chain")
        sq_ready = sem("s_sq_ready")
        ssq_ready = sem("s_ssq_ready")
        op_chain = sem("s_op_chain")
        rms_ready = sem("s_rms_ready")

        per = {"P": NP_, "OP": NOP, "S": NS_}

        def bank_free(pe, u, stage, j, first):
            pos, v = JOBS.index((stage, j)) - BANKS, u
            while True:
                if pos < 0:
                    if first:
                        return
                    pos, v = pos + len(JOBS) // BANKS * BANKS + BANKS, v - 1
                    if pos >= len(JOBS):
                        pos -= BANKS
                st, jj = JOBS[pos]
                if st == "OP":
                    if first:
                        pos -= BANKS
                        continue
                    v = v - 1
                pe.wait_ge(took[st], v * per[st] + jj + 1)
                return

        def bank(stage, j):
            return ps[:, JOBS.index((stage, j)) % BANKS, :]

        def tile_of(j):
            return bT[:] if j == 0 else cT[:] if j == 1 else hid[:, j - 2, :]

        def sp_in(sp, u, g, b, first):
            for c in range(CHUNKS_IN):
                slot = c % WIN_SLOTS
                if not (first and c < WIN_SLOTS):
                    last, v = (c - WIN_SLOTS, u) if c >= WIN_SLOTS else (c - WIN_SLOTS + CHUNKS_IN, u - 1)
                    if last == 0:
                        sp.wait_ge(done["P"], v * NP_ + 2)
                    else:
                        sp.wait_ge(gate_done, v * KC + last)
                sp.dma_start(win[:, slot].rearrange("p a k o -> p (a k o)"),
                             a["w_in"][bass.ds(g * CHUNKS_IN + c, 1), :, :].rearrange("o p n -> (o p) n")
                             ).then_inc(win_loaded[slot], 16)

        def sp_scan(sp, u, g, b, first):
            if b == 0:
                if not first:
                    sp.wait_ge(done["OP"], u * NOP)
                sp.dma_start(wo[:].rearrange("p k o -> p (k o)"),
                             a["w_out"][bass.ds(g, 1), :, :].rearrange("o p n -> (o p) n")).then_inc(wo_loaded, 16)
            for h in range(HG):
                if not (first and h < R_SLOTS):
                    sp.wait_ge(diff_ready, u * HG + h - R_SLOTS + 1)
                    sp.wait_ge(scale_ready, u * HG + h - R_SLOTS + 1)
                sp.dma_start(rows[:, h % R_SLOTS, :],
                             acs_dram[bass.ds(g * HG + h, 1), b * SEQ:(b + 1) * SEQ].to_broadcast((P, SEQ))
                             ).then_inc(rows_loaded[h % R_SLOTS], 16)

        def pe_in(pe, u, g, b, first):
            for j in range(2 * KC + 2):
                c, slot = j // 2, (j // 2) % WIN_SLOTS
                if j % 2 == 0:
                    pe.wait_ge(win_loaded[slot], 16 * (u * (CHUNKS_IN // WIN_SLOTS) + c // WIN_SLOTS + 1))
                gated = j >= 2 and j % 2 == 1
                if gated:
                    n = (j - 3) // 2
                    out_ = ps_a[:, n % 2, :]
                    if n >= 2:
                        pe.wait_ge(gate_took, u * KC + n - 1)
                    elif not first:
                        pe.wait_ge(gate_took, u * KC - n)
                        if n == 0:
                            pe.wait_ge(b_took, u)
                else:
                    n = j if j < 2 else 2 + (j - 2) // 2
                    out_ = bank("P", n)
                    bank_free(pe, u, "P", n, first)
                for k in range(KD):
                    mm = nc.tensor.matmul(out_, win[:, slot, j % 2, k, :], hT[:, k, b * SEQ:(b + 1) * SEQ],
                                          start=(k == 0), stop=(k == KD - 1))
                mm.then_inc(gate_done if gated else done["P"], 1)

        def pe_out(pe, u, g, b, last):
            def own_bank_free(j):
                if last:
                    pe.wait_ge(took["S"], (u + 1) * NS_)
                else:
                    bank_free(pe, u + 1, "OP", j, False)
            own_bank_free(0)
            pe.wait_ge(ssq_ready, (u + 1) * (KC - 1))
            for t in range(TB):
                mm = nc.tensor.matmul(bank("OP", 0)[:, t:t + 1], ssq[:, t * P:(t + 1) * P], ones[:, 0:1],
                                      start=True, stop=True)
            mm.then_inc(done["OP"], 1)
            pe.wait_ge(wo_scaled, (g + 1) * KC)
            for t in range(TB):
                own_bank_free(1 + t)
                for k in range(KC):
                    mm = nc.tensor.matmul(bank("OP", 1 + t), yT[:, k, t * P:(t + 1) * P], wo[:, k, :],
                                          start=(k == 0), stop=(k == KC - 1))
                mm.then_inc(done["OP"], 1)

        def pe_scan(pe, u, g, b, first):
            for j, (kind, c, half) in enumerate(S_JOBS):
                bank_free(pe, u, "S", j, first)
                dst = bank("S", j)
                if kind == "CB":
                    pe.wait_ge(hbc_ready, u * NP_ + 2)
                    for i in range(TB):
                        mm = nc.tensor.matmul(dst[:, i * P:(i + 1) * P], bT[:, i * P:(i + 1) * P],
                                              cT[:, i * P:(i + 1) * P], start=True, stop=True)
                    mm.then_inc(done["S"], 1)
                    pe.wait_ge(gate_took, (u + 1) * KC)
                    for i in range(TB - 1):
                        mm = nc.tensor.transpose(ps_a[:, 0, i * P:(i + 1) * P], bT[:, i * P:(i + 1) * P], ident[:])
                    mm.then_inc(b_turned, 1)
                elif kind == "T":
                    if c == 0:
                        pe.wait_ge(hbc_ready, u * NP_ + 2 + 4 * (half + 1))
                    for i in range(4):
                        mm = nc.tensor.transpose(dst[:, i * P:(i + 1) * P],
                                                 hid[:, 4 * half + i, c * P:(c + 1) * P], ident[:])
                    mm.then_inc(done["S"], 1)
                elif kind == "ST":
                    pe.wait_ge(took["S"], u * NS_ + S_JOBS.index(("T", c, half)) + 1)
                    pe.wait_ge(b_took, u + 1)
                    nc.tensor.matmul(dst, b_l[:, c, :], hdd[:, c % 2, half * 512:(half + 1) * 512],
                                     start=True, stop=True).then_inc(done["S"], 1)
                elif kind == "DIAG":
                    pe.wait_ge(m_ready, u * HG + 2 * c + 2)
                    if c == 0:
                        pe.wait_ge(took["S"], u * NS_ + S_JOBS.index(("T", TB - 1, 1)) + 1)
                    for e in range(2):
                        h = 2 * c + e
                        for i in range(TB):
                            mm = nc.tensor.matmul(dst[e * HP:(e + 1) * HP, i * P:(i + 1) * P],
                                                  hdt[:, i, h * HP:(h + 1) * HP],
                                                  lm[:, h % L_SLOTS, i * P:(i + 1) * P], start=True, stop=True)
                    mm.then_inc(done["S"], 1)
                else:
                    if c == 0:
                        pe.wait_ge(took["S"], u * NS_ + S_JOBS.index(("ST", TB - 2, 1)) + 1)
                    for i in range(TB - 1):
                        mm = nc.tensor.matmul(dst[:, i * P:(i + 1) * P], state[:, i, c * P:(c + 1) * P],
                                              cT[:, (i + 1) * P:(i + 2) * P], start=True, stop=True)
                    mm.then_inc(done["S"], 1)

        def act_in(act, u, g, b, first):
            def silu_of(j):
                act.wait_ge(took["P"], u * NP_ + j + 1)
                if not first and j >= 2:
                    act.wait_ge(took["S"], (u - 1) * NS_ + S_JOBS.index(("DIAG", j - 2, 0)) + 1)
                if not first and j < 2:
                    act.wait_ge(done["S"], u * NS_)
                nc.scalar.activation(tile_of(j), cv[:, j % CV_SLOTS, :], ACT.Silu).then_inc(hbc_ready, 1)
            act.wait_ge(params, u + 1)
            for j in range(NP_):
                act.wait_ge(done["P"], u * NP_ + j + 1)
                if j >= CV_SLOTS:
                    act.wait_ge(hbc_ready, u * NP_ + j - CV_SLOTS + 1)
                elif not first:
                    act.wait_ge(hbc_ready, u * NP_)
                nc.scalar.activation(cv[:, j % CV_SLOTS, :], bank("P", j), ACT.Identity,
                                     bias=conv_b[:, b, j:j + 1], scale=conv_w[:, b, j, 3:4]).then_inc(tap_ready, 1)
                if j:
                    silu_of(j - 1)
                if j >= 2:
                    act.wait_ge(gate_done, u * KC + j - 1)
                    if not first:
                        act.wait_ge(y_ready, (u - 1) * KC + j - 1)
                    nc.scalar.activation(gate[:, j - 2, :], ps_a[:, (j - 2) % 2, :], ACT.Silu).then_inc(gate_took, 1)
            silu_of(NP_ - 1)

        def act_out(act, u, g, b, last):
            act.wait_ge(took["OP"], u * NOP + 1)
            nc.scalar.activation(rms[:], meansq[:], ACT.Sqrt).then_inc(rms_ready, 1)

        def act_scan(act, u, g, b, first):
            act.wait_ge(b_turned, u + 1)
            nc.scalar.activation(b_l[:].rearrange("p c n -> p (c n)"), ps_a[:, 0, 0:3 * P], ACT.Copy).then_inc(b_took, 1)

            def exps(k):
                for h in (2 * k, 2 * k + 1):
                    act.wait_ge(diff_ready, u * HG + h + 1)
                    nc.scalar.activation(lm[:, h % L_SLOTS, :], lm[:, h % L_SLOTS, :], ACT.Exp).then_inc(exp_ready, 1)
                for e in range(2):
                    h = 2 * k + e
                    if k >= 2:
                        act.wait_ge(took["S"], u * NS_ + S_JOBS.index(("OFF", k - 2, 0)) + 1)
                    elif not first:
                        act.wait_ge(took["S"], (u - 1) * NS_ + S_JOBS.index(("OFF", KC - 2 + k, 0)) + 1)
                    act.wait_ge(rows_loaded[h % R_SLOTS], 16 * (u * (HG // R_SLOTS) + h // R_SLOTS + 1))
                    nc.scalar.activation(scale[e * HP:(e + 1) * HP, k % 2, :],
                                         rows[e * HP:(e + 1) * HP, h % R_SLOTS, P:], ACT.Exp).then_inc(scale_ready, 1)

            def square(k):
                act.wait_ge(y_ready, u * KC + k + 1)
                nc.scalar.activation(ysum[:, k % 2, :], yT[:, k, :], ACT.Square).then_inc(sq_ready, 1)
            exps(0)
            exps(1)
            for k in range(KC):
                if k + 2 < KC:
                    exps(k + 2)
                square(k)

        def dve_in(dve, u, g, b, first):
            dve.wait_ge(params, u + 1)
            for j in range(NP_):
                dve.wait_ge(tap_ready, u * NP_ + j + 1)
                for d in (1, 2, 3):
                    dst = cv[:, j % CV_SLOTS, d:]
                    ins = nc.vector.scalar_tensor_tensor(dst, bank("P", j)[:, 0:SEQ - d],
                                                         conv_w[:, b, j, 3 - d:4 - d], dst, ALU.mult, ALU.add)
                    if d < 3:
                        ins.then_inc(conv_chain, 1)
                        dve.wait_ge(conv_chain, (u * NP_ + j) * 2 + d)
                ins.then_inc(took["P"], 1)

        def dve_out(dve, u, g, b, last):
            dve.wait_ge(done["OP"], u * NOP + 1)
            nc.vector.tensor_scalar(meansq[:], bank("OP", 0)[:, 0:TB], 1.0 / CG, EPS, ALU.mult,
                                    ALU.add).then_inc(took["OP"], 1)
            dve.wait_ge(rms_ready, u + 1)
            nc.vector.reciprocal(rrms[:], rms[:]).then_inc(op_chain, 1)
            dve.wait_ge(op_chain, u + 1)
            for t in range(TB):
                dve.wait_ge(done["OP"], u * NOP + 2 + t)
                nc.vector.scalar_tensor_tensor(acc[:, b * TB + t, :], bank("OP", 1 + t), rrms[:, t:t + 1],
                                               acc[:, b * TB + t, :], ALU.mult, ALU.add).then_inc(took["OP"], 1)

        def dve_scan(dve, u, g, b, first):
            def diff_of(h):
                dve.wait_ge(rows_loaded[h % R_SLOTS], 16 * (u * (HG // R_SLOTS) + h // R_SLOTS + 1))
                for i in range(TB):
                    cols = slice(i * P, (i + 1) * P)
                    ins = nc.vector.tensor_scalar(lm[:, h % L_SLOTS, cols], rows[:, h % R_SLOTS, cols],
                                                  nacg[:, b, i, h:h + 1], 0.0, ALU.add, ALU.min)
                ins.then_inc(diff_ready, 1)

            def m_of(h):
                dve.wait_ge(exp_ready, u * HG + h + 1)
                nc.vector.tensor_tensor(lm[:, h % L_SLOTS, :], lm[:, h % L_SLOTS, :],
                                        cbt[:].rearrange("p c i -> p (c i)"), ALU.mult).then_inc(m_ready, 1)
            if not first:
                dve.wait_ge(done["S"], u * NS_)
            for h in range(L_SLOTS):
                diff_of(h)
            for j, (kind, c, half) in enumerate(S_JOBS):
                if kind == "DIAG":
                    if c + 1 < KC:
                        m_of(2 * c + 2)
                        m_of(2 * c + 3)
                dve.wait_ge(done["S"], u * NS_ + j + 1)
                src = bank("S", j)
                heads = slice(8 * half, 8 * half + 8)
                if kind == "CB":
                    nc.vector.tensor_tensor(cbt[:], src.rearrange("p (c i) -> p c i", c=TB),
                                            mask[:].unsqueeze(1).to_broadcast((P, TB, P)),
                                            ALU.mult).then_inc(took["S"], 1)
                    dve.wait_ge(took["S"], u * NS_ + 1)
                    m_of(0)
                    m_of(1)
                elif kind == "T":
                    by_head = src.rearrange("p (h c) -> p h c", h=8)
                    if c < TB - 1:
                        if c == 2:
                            dve.wait_ge(done["S"], u * NS_ + S_JOBS.index(("ST", 0, half)) + 1)
                        nc.vector.tensor_tensor(hdd[:, c % 2, half * 512:(half + 1) * 512].rearrange(
                            "p (h c) -> p h c", h=8), by_head,
                            ddg[:, b, c, heads].unsqueeze(2).to_broadcast((P, 8, HP)), ALU.mult)
                    nc.vector.tensor_tensor(hdt[:, c, half * 512:(half + 1) * 512].rearrange(
                        "p (h c) -> p h c", h=8), by_head,
                        dtg[:, b, c, heads].unsqueeze(2).to_broadcast((P, 8, HP)), ALU.mult).then_inc(took["S"], 1)
                elif kind == "ST":
                    dst = state[:, c, half * 512:(half + 1) * 512]
                    if c == 0:
                        nc.vector.tensor_copy(dst, src).then_inc(took["S"], 1)
                    else:
                        dve.wait_ge(carried_ready, u * 4 + 2 * (c - 1) + half + 1)
                        nc.vector.tensor_tensor(dst, src, carried[:, half * 512:(half + 1) * 512],
                                                ALU.add).then_inc(took["S"], 1)
                elif kind == "DIAG":
                    if c >= 2:
                        dve.wait_ge(ssq_ready, u * (KC - 1) + max(c - 2, 1))
                    elif not first:
                        dve.wait_ge(ssq_ready, u * (KC - 1))
                    nc.vector.scalar_tensor_tensor(ysum[:, c % 2, :], hid[:, c, :], skip[:, b, c:c + 1], src,
                                                   ALU.mult, ALU.add).then_inc(took["S"], 1)
                    if c + 2 < KC:
                        diff_of(2 * c + 4)
                        diff_of(2 * c + 5)
                else:
                    dve.wait_ge(scale_ready, u * HG + 2 * c + 2)
                    nc.vector.tensor_tensor(yoff[:, c % 2, :], src[:, 0:3 * P], scale[:, c % 2, :],
                                            ALU.mult).then_inc(took["S"], 1)
            if b == 0:
                dve.wait_ge(wo_loaded, 16 * (g + 1))
                for k in range(KC):
                    nc.vector.tensor_scalar(wo[:, k, :], wo[:, k, :], gnorm[:, b, k:k + 1], None,
                                            ALU.mult).then_inc(wo_scaled, 1)

        def pool_in(pool, u, g, b, first):
            gs = bass.ds(g, 1)
            hs = bass.ds(g * HG, HG)
            nc.gpsimd.tensor_copy(conv_w[:, b].rearrange("p t k -> p (t k)"), par[:, gs, 0:40].rearrange("p g c -> p (g c)"))
            nc.gpsimd.tensor_copy(conv_b[:, b], par[:, gs, 40:50].rearrange("p g c -> p (g c)"))
            nc.gpsimd.tensor_copy(skip[:, b], par[:, gs, 50:58].rearrange("p g c -> p (g c)"))
            nc.gpsimd.tensor_copy(gnorm[:, b], par[:, gs, 58:66].rearrange("p g c -> p (g c)"))
            nc.gpsimd.tensor_copy(dtg[:, b], dt_l[:, b * TB:(b + 1) * TB, hs])
            nc.gpsimd.tensor_copy(ddg[:, b], dd_l[:, b * TB:(b + 1) * TB, hs])
            nc.gpsimd.tensor_copy(nacg[:, b], nacs_l[:, b * TB:(b + 1) * TB, hs])
            nc.gpsimd.tensor_copy(cdg[:, b], chunk_decay[:, 2 * b:2 * b + 2, hs]).then_inc(params, 1)

        def pool_scan(pool, u, g, b, first):
            pool.wait_ge(params, u + 1)
            for c in (1, 2):
                for half in range(2):
                    cols = slice(half * 512, (half + 1) * 512)
                    pool.wait_ge(took["S"], u * NS_ + S_JOBS.index(("ST", c - 1, half)) + 1)
                    nc.gpsimd.tensor_tensor(carried[:, cols].rearrange("p (h c) -> p h c", h=8),
                                            state[:, c - 1, cols].rearrange("p (h c) -> p h c", h=8),
                                            cdg[:, b, c - 1, 8 * half:8 * half + 8].unsqueeze(2).to_broadcast((P, 8, HP)),
                                            ALU.mult).then_inc(carried_ready, 1)

            def add_square(k):
                pool.wait_ge(sq_ready, u * KC + k + 1)
                if k > 1:
                    pool.wait_ge(ssq_ready, u * (KC - 1) + k - 1)
                elif not first:
                    pool.wait_ge(done["OP"], (u - 1) * NOP + 1)
                nc.gpsimd.tensor_tensor(ssq[:], ysum[:, 0, :] if k == 1 else ssq[:], ysum[:, k % 2, :],
                                        ALU.add).then_inc(ssq_ready, 1)
            for k in range(KC):
                if k > 1:
                    add_square(k - 1)
                pool.wait_ge(took["S"], u * NS_ + S_JOBS.index(("OFF", k, 0)) + 1)
                nc.gpsimd.tensor_tensor(ysum[:, k % 2, P:], ysum[:, k % 2, P:], yoff[:, k % 2, :],
                                        ALU.add).then_inc(pool_chain, 1)
                pool.wait_ge(pool_chain, u * KC + k + 1)
                if not first:
                    pool.wait_ge(done["OP"], u * NOP)
                nc.gpsimd.tensor_tensor(yT[:, k, :], ysum[:, k % 2, :], gate[:, k, :], ALU.mult).then_inc(y_ready, 1)
            add_square(KC - 1)

        def schedule(eng, stage_in, stage_out, stage_scan):
            def unit(g, b, first=False):
                u = 2 * g + b
                if stage_in:
                    stage_in(eng, u, g, b, first)
                if stage_out and not first:
                    stage_out(eng, u - 1, g - 1 if b == 0 else g, 1 - b, False)
                if stage_scan:
                    stage_scan(eng, u, g, b, first)
            unit(0, 0, True)
            with eng.Fori(0, GROUPS - 1) as g:
                unit(g, 1)
                unit(g + 1, 0)
            unit(GROUPS - 1, 1)
            if stage_out:
                stage_out(eng, 2 * GROUPS - 1, GROUPS - 1, 1, True)

        with nc.Block() as block:
            @block.sync
            def _(sp):
                sp.dma_start(par[:], a["par"]).then_inc(par_loaded, 16)
                sp.dma_start(mask[:], a["mask"]).then_inc(par_loaded, 16)
                schedule(sp, sp_in, None, sp_scan)

            @block.tensor
            def _(pe):
                schedule(pe, pe_in, pe_out, pe_scan)

            @block.scalar
            def _(act):
                schedule(act, act_in, act_out, act_scan)

            @block.vector
            def _(dve):
                dve.wait_ge(par_loaded, 32)
                schedule(dve, dve_in, dve_out, dve_scan)

            @block.gpsimd
            def _(pool):
                pool.wait_ge(par_loaded, 32)
                schedule(pool, pool_in, None, pool_scan)

        x1_back = sem("s_x1_back")
        g_back = sem("s_g_back")
        product_ready = sem("s_product_ready")
        out_ready = sem("s_out_ready")
        out_stored = sem("s_out_stored")
        with nc.Block() as block:
            @block.sync
            def _(sp):
                sp.dma_start(hid[:], x1_dram).then_inc(x1_back, 16)
                sp.dma_start(gate[:], g_dram).then_inc(g_back, 16)
                for t in range(NT):
                    sp.wait_ge(out_ready, t + 1)
                    sp.dma_start(out[:, t, :], acc[:, t, :]).then_inc(out_stored, 16)
                sp.wait_ge(out_stored, 16 * NT)

            @block.vector
            def _(dve):
                dve.wait_ge(x1_back, 16)
                dve.wait_ge(g_back, 16)
                for t in range(NT):
                    nc.vector.tensor_tensor(acc[:, t, :], acc[:, t, :], gate[:, t, :], ALU.mult).then_inc(product_ready, 1)
                for t in range(NT):
                    dve.wait_ge(product_ready, t + 1)
                    nc.vector.tensor_tensor(acc[:, t, :], acc[:, t, :], hid[:, t, :], ALU.add).then_inc(out_ready, 1)


def program(nc, a, out):
    with ExitStack() as ctx:
        def sb(name, shape, dt=F32):
            return ctx.enter_context(nc.sbuf_tensor(name, shape, dt))

        def dram(name, shape):
            return nc.dram_tensor(name, shape, F32, kind="Internal").ap()

        xs = sb("xs", [P, NT, D])
        ident = sb("ident", [P, P])
        table = dram("table", [T, 2 * D])
        x1_dram = dram("x1_dram", [P, NT, D])
        g_dram = dram("g_dram", [P, NT, D])
        acs_dram = dram("acs_dram", [HEADS, T])
        layer0(nc, a, xs, ident, x1_dram, table)
        ones = sb("ones", [P, P])
        hT = sb("hT", [P, KD, T])
        dt_l = sb("dt_l", [P, NT, HEADS])
        dd_l = sb("dd_l", [P, NT, HEADS])
        nacs_l = sb("nacs_l", [P, NT, HEADS])
        chunk_decay = sb("chunk_decay", [P, 4, HEADS])
        with nc.sbuf_tensor("xnT1", [P, KD, T], F32) as xnT:
            mixer_inputs(nc, a, xs, ident, ones, hT, xnT, dt_l, dd_l, nacs_l, chunk_decay, acs_dram)
            layer1_ffn(nc, a, xnT, g_dram)
        mixer(nc, a, xs, ident, ones, hT, dt_l, dd_l, nacs_l, chunk_decay, acs_dram, x1_dram, g_dram,
              out.rearrange("(t p) d -> p t d", p=P))


def shape_tables(np):
    t = np.arange(D)
    f = np.arange(D // 2)
    ang = 2 * np.pi * ((t[:, None] * f[None, :]) % D) / D
    cos, sin = np.cos(ang), np.sin(ang)
    sin[:, 0] = np.cos(np.pi * t)
    dft = np.concatenate([cos, sin], 1)
    weight = np.full(D // 2, 2.0 / D)
    weight[0] = 1.0 / D
    tau = np.minimum(t, D - t)
    ci = np.cos(2 * np.pi * ((f[:, None] * tau[None, :]) % D) / D) * weight[:, None]
    si = ci.copy()
    si[0] = np.cos(np.pi * tau) / D
    idft = np.concatenate([ci, si], 0)

    def lay(m):
        return np.ascontiguousarray(m.reshape(KD, P, -1).transpose(1, 0, 2)).astype(np.float32)
    row = np.arange(T).reshape(NT, P).T[:, :, None] * (2 * D)
    return {"ident": np.eye(P, dtype=np.float32), "mask": np.triu(np.ones((P, P), np.float32)), "dft": lay(dft), "idft": lay(idft),
            "rowbase": np.broadcast_to(row, (P, NT, 8)).astype(np.uint32)}


def kernel(**inputs):
    import numpy as np
    import concourse.bacc as bacc
    from concourse.bass_utils import run_bass_kernel_spmd

    def c(v):
        return np.ascontiguousarray(v)

    i = {k: np.asarray(v) for k, v in inputs.items()}
    arrays = {
        "x": c(i["L0_attn_x"].reshape(T, D)),
        "gate_w": c(i["L0_ffn_gate_w"]), "up_w": c(i["L0_ffn_up_w"]), "down_w": c(i["L0_ffn_down_w"]),
        "fc1_w": c(i["L0_ffn_fc1_w"]), "fc2_w": c(i["L0_ffn_fc2_w"]), "expert_w": c(i["L0_ffn_expert_w"]),
        "gamma": c(i["L0_ffn_ln_gamma"].reshape(1, D)), "beta": c(i["L0_ffn_ln_beta"].reshape(1, D)),
    }
    w_in = i["L1_attn_in_proj_w"].reshape(-1, P, D)
    order = [t for g in range(GROUPS)
             for t in [2 * GROUPS * KC + g, (2 * KC + 1) * GROUPS + g]
             + [x for k in range(KC) for x in (GROUPS * KC + g * KC + k, g * KC + k)]]
    tiles = w_in[order].reshape(-1, 2, P, KD, P)
    arrays["w_in"] = c(tiles.transpose(0, 4, 1, 3, 2).reshape(-1, P, 2 * KD * P))
    arrays["w_dt"] = c(w_in[-1].reshape(P, KD, P).transpose(2, 1, 0))
    arrays["w_out"] = c(i["L1_attn_out_proj_w"].reshape(D, GROUPS, KC, P).transpose(1, 3, 2, 0).reshape(
        GROUPS, P, KC * D))
    arrays["norm_w"] = c(i["L1_attn_norm_w"].reshape(KD, P).T)
    arrays["dt_bias"] = c(i["L1_attn_dt_bias"].reshape(P, 1))
    arrays["a_log"] = c(i["L1_attn_A_log"].reshape(P, 1))
    cw, cb = i["L1_attn_conv_w"].reshape(-1, P, CONV), i["L1_attn_conv_b"].reshape(-1, P)
    skip = np.repeat(i["L1_attn_Dp"], HP).reshape(GROUPS, KC, P)
    gn = i["L1_attn_gnorm_w"].reshape(GROUPS, KC, P)
    par = []
    for g in range(GROUPS):
        own = [GROUPS * KC + g, GROUPS * KC + GROUPS + g] + [g * KC + k for k in range(KC)]
        par.append(np.concatenate([cw[own].transpose(1, 0, 2).reshape(P, -1), cb[own].T, skip[g].T, gn[g].T], 1))
    arrays["par"] = c(np.stack(par, 1))

    def blocks(m):
        return m.T.reshape(-1, P, m.shape[0]).transpose(1, 0, 2).reshape(P, -1)
    names = ("gate", "up", "down")
    arrays["q"] = c(np.concatenate([blocks(i[f"L1_ffn_{n}_q"]) for n in names], 1).reshape(P, NQ, QC).transpose(1, 0, 2))
    arrays["s"] = c(np.concatenate([i[f"L1_ffn_{n}_s"].T.reshape(-1) for n in names]).reshape(NQ, QC))
    arrays.update(shape_tables(np))
    nc = bacc.Bacc("TRN2", target_bir_lowering=False, num_devices=1)
    a = {k: nc.dram_tensor(f"in_{k}", v.shape, mybir.dt.from_np(v.dtype), kind="ExternalInput").ap()
         for k, v in arrays.items()}
    out = nc.dram_tensor("out", (T, D), F32, kind="ExternalOutput").ap()
    program(nc, a, out)
    r = run_bass_kernel_spmd(nc, [{f"in_{k}": v for k, v in arrays.items()}], core_ids=[0])
    return r.results[0]["out"].reshape(NB, SEQ, D)
```

```python
from contextlib import ExitStack

import concourse.bass as bass
from concourse import mybir

F32 = mybir.dt.float32
U32 = mybir.dt.uint32
I32 = mybir.dt.int32
F32R = mybir.dt.float32r
ALU = mybir.AluOpType
ACT = mybir.ActivationFunctionType

P = 128
T = 1024
NT = T // P
D = 512
KD = D // P
NB = 2
SEQ = T // NB
TB = SEQ // P
TOPK = 6
EPS = 1e-5
UP = 1024
KU = UP // P
LAT = 256
KL = LAT // P
NE = 8
HEADS = 128
HP = 64
GROUPS = 8
NST = 128
HG = HEADS // GROUPS
CG = HG * HP
KC = CG // P
DI = HEADS * HP
CONV = 4
INT = 1792
KI = INT // P
QC = 896
GROUP_N = 3 * NT * HG + 4 * HG
NQ = 3 * D * INT // P // QC


class Sems:

    def __init__(self, nc, ctx):
        self.nc, self.ctx = nc, ctx

    def __call__(self, name):
        return self.ctx.enter_context(self.nc.semaphore(name))


def chain_on(eng, sem):
    n = [0]

    def link(ins):
        n[0] += 1
        ins.then_inc(sem, 1)
        eng.wait_ge(sem, n[0])
    return link


def three_passes(nc, dst, l_hi, l_lo, r_hi, r_lo, start, stop):
    nc.tensor.matmul(dst, l_hi, r_hi, start=start, stop=False)
    nc.tensor.matmul(dst, l_hi, r_lo, start=False, stop=False)
    return nc.tensor.matmul(dst, l_lo, r_hi, start=False, stop=stop)


def layer0(nc, a, x1, ident, x1_dram, table):
    with ExitStack() as ctx:
        sem = Sems(nc, ctx)

        def sb(name, shape, dt=F32):
            return ctx.enter_context(nc.sbuf_tensor(name, shape, dt))

        xn = sb("xn", [P, NT, D])
        xnT = sb("xnT", [P, KD, T])
        dft = sb("dft", [P, KD, D])
        idft = sb("idft", [P, KD, D])
        upw = sb("upw", [P, KD, UP])
        downw = sb("downw", [P, KU, D])
        fc1w = sb("fc1w", [P, KD, LAT])
        expw = sb("expw", [P, KL, LAT])
        fc2w = sb("fc2w", [P, KL, D])
        gatew = sb("gatew", [P, KD, NE])
        gamma = sb("gamma", [P, D])
        beta = sb("beta", [P, D])
        rowbase = sb("rowbase", [P, NT, 8], U32)
        power = sb("power", [P, KD, SEQ])
        hid = sb("hid", [P, KU, SEQ])
        latT = sb("latT", [P, KL, SEQ])
        exoT = sb("exoT", [P, KL, SEQ])
        shifted = sb("shifted", [P, TOPK, D])
        mixed = sb("mixed", [P, TB, D])
        routed = sb("routed", [P, 2, D])
        z = sb("z", [P, TB, D])
        stats = sb("stats", [P, NT, 6])
        mv = sb("mv", [P, NT, 2])
        std = sb("std", [P, NT])
        rstd = sb("rstd", [P, NT])
        zstats = sb("zstats", [P, NT, 6])
        zmv = sb("zmv", [P, NT, 2])
        zstd = sb("zstd", [P, NT])
        zrstd = sb("zrstd", [P, NT])
        top = sb("top", [P, NT, 8])
        delay = sb("delay", [P, NT, 8], U32)
        at = sb("at", [P, NT, 8], U32)
        negmax = sb("negmax", [P, NT])
        wexp = sb("wexp", [P, NT, 8])
        wsum = sb("wsum", [P, NT])
        wrec = sb("wrec", [P, NT])
        topl = sb("topl", [P, NT, 8])
        rsum = sb("rsum", [P, NT])
        ps_a = ctx.enter_context(nc.psum_tensor("ps_a", [P, 4, 512], F32))
        ps_d = ctx.enter_context(nc.psum_tensor("ps_d", [P, 4, 512], F32))

        x_loaded = [sem(f"x_loaded{t}") for t in range(NT)]
        ident_loaded = sem("ident_loaded")
        dft_loaded = sem("dft_loaded")
        idft_loaded = sem("idft_loaded")
        up_loaded = sem("up_loaded")
        small_loaded = sem("small_loaded")
        down_loaded = sem("down_loaded")
        rows_loaded = sem("rows_loaded")
        dve_chain = sem("dve_chain")
        act_chain = sem("act_chain")
        pool_chain = sem("pool_chain")
        var_ready = sem("var_ready")
        std_ready = sem("std_ready")
        xn_ready = sem("xn_ready")
        table_stored = sem("table_stored")
        pe_a = sem("pe_a")
        act_took = sem("act_took")
        pe_d = sem("pe_d")
        dve_took = sem("dve_took")
        squared = sem("squared")
        topk_ready = sem("topk_ready")
        weights_ready = sem("weights_ready")
        gathered = sem("gathered")
        mixed_ready = sem("mixed_ready")
        z_ready = sem("z_ready")
        zvar_ready = sem("zvar_ready")
        zstd_ready = sem("zstd_ready")
        zn_ready = sem("zn_ready")
        affine_ready = sem("affine_ready")
        silu_ready = sem("silu_ready")
        x1_ready = sem("x1_ready")
        x1_stored = sem("x1_stored")

        A_N, D_N = 2 * KD + KU + 2 * KL, 3 * TB

        def a_dft(n, m): return NT + A_N * n + m
        def a_up(n, m): return NT + A_N * n + KD + m
        def a_lat(n, m): return NT + A_N * n + KD + KU + m
        def a_exo(n, m): return NT + A_N * n + KD + KU + KL + m
        def a_rout(n, t): return NT + A_N * n + KD + KU + 2 * KL + t
        def d_corr(n, t): return D_N * n + t
        def d_log(n, t): return D_N * n + TB + t
        def d_shared(n, t): return D_N * n + 2 * TB + t

        block = ctx.enter_context(nc.Block())

        @block.sync
        def _(sp):
            x_view = a["x"].rearrange("(t p) d -> p t d", p=P)
            for t in range(NT):
                sp.dma_start(x1[:, t, :], x_view[:, t, :]).then_inc(x_loaded[t], 16)
            sp.dma_start(ident[:], a["ident"]).then_inc(ident_loaded, 16)
            sp.dma_start(dft[:], a["dft"]).then_inc(dft_loaded, 16)
            sp.dma_start(idft[:], a["idft"]).then_inc(idft_loaded, 16)
            sp.dma_start(rowbase[:], a["rowbase"]).then_inc(rows_loaded, 16)
            sp.dma_start(gamma[:], a["gamma"].to_broadcast((P, D))).then_inc(rows_loaded, 16)
            sp.dma_start(beta[:], a["beta"].to_broadcast((P, D))).then_inc(rows_loaded, 16)
            sp.dma_start(upw[:], a["up_w"].rearrange("(k p) n -> p k n", p=P)).then_inc(up_loaded, 16)
            sp.dma_start(fc1w[:], a["fc1_w"].rearrange("(k p) n -> p k n", p=P)).then_inc(small_loaded, 16)
            sp.dma_start(expw[:], a["expert_w"].rearrange("(k p) n -> p k n", p=P)).then_inc(small_loaded, 16)
            sp.dma_start(fc2w[:], a["fc2_w"].rearrange("(k p) n -> p k n", p=P)).then_inc(small_loaded, 16)
            sp.dma_start(gatew[:], a["gate_w"].rearrange("(k p) n -> p k n", p=P)).then_inc(small_loaded, 16)
            sp.dma_start(downw[:], a["down_w"].rearrange("(k p) n -> p k n", p=P)).then_inc(down_loaded, 16)
            for t in range(NT):
                sp.wait_ge(xn_ready, t + 1)
                for half in range(2):
                    sp.dma_start(table[t * P:(t + 1) * P, half * D:(half + 1) * D],
                                 xn[:, t, :]).then_inc(table_stored, 16)
            for t in range(NT):
                sp.wait_ge(x1_ready, t + 1)
                sp.dma_start(x1_dram[:, t, :], x1[:, t, :]).then_inc(x1_stored, 16)
            sp.wait_ge(x1_stored, 16 * NT)
            sp.wait_ge(table_stored, 32 * NT)

        @block.tensor
        def _(pe):
            def turn(eng_sem, i, base=4):
                if i >= base:
                    pe.wait_ge(eng_sem, i - base + 1)

            pe.wait_ge(ident_loaded, 16)
            for t in range(NT):
                pe.wait_ge(xn_ready, t + 1)
                turn(act_took, t)
                for k in range(KD):
                    mm = nc.tensor.transpose(ps_a[:, t % 4, k * P:(k + 1) * P],
                                             xn[:, t, k * P:(k + 1) * P], ident[:])
                mm.then_inc(pe_a, 1)
            pe.wait_ge(dft_loaded, 16)
            for n in range(NB):
                cols = slice(n * SEQ, (n + 1) * SEQ)
                pe.wait_ge(act_took, (n + 1) * TB)
                for m in range(KD):
                    i = a_dft(n, m)
                    turn(act_took, i)
                    for k in range(KD):
                        mm = nc.tensor.matmul(ps_a[:, i % 4, :], dft[:, k, m * P:(m + 1) * P],
                                              xnT[:, k, cols], start=(k == 0), stop=(k == KD - 1))
                    mm.then_inc(pe_a, 1)
                pe.wait_ge(up_loaded, 16)
                for m in range(KU):
                    i = a_up(n, m)
                    turn(act_took, i)
                    for k in range(KD):
                        mm = nc.tensor.matmul(ps_a[:, i % 4, :], upw[:, k, m * P:(m + 1) * P],
                                              xnT[:, k, cols], start=(k == 0), stop=(k == KD - 1))
                    mm.then_inc(pe_a, 1)
                pe.wait_ge(idft_loaded, 16)
                for t in range(TB):
                    i = d_corr(n, t)
                    turn(dve_took, i)
                    for k in range(KD):
                        mm = nc.tensor.matmul(ps_d[:, i % 4, :], power[:, k, t * P:(t + 1) * P],
                                              idft[:, k, :], start=(k == 0), stop=(k == KD - 1))
                    mm.then_inc(pe_d, 1)
                pe.wait_ge(small_loaded, 64)
                for m in range(KL):
                    i = a_lat(n, m)
                    turn(act_took, i)
                    for k in range(KD):
                        mm = nc.tensor.matmul(ps_a[:, i % 4, :], fc1w[:, k, m * P:(m + 1) * P],
                                              xnT[:, k, cols], start=(k == 0), stop=(k == KD - 1))
                    mm.then_inc(pe_a, 1)
                for t in range(TB):
                    i = d_log(n, t)
                    turn(dve_took, i)
                    for k in range(KD):
                        mm = nc.tensor.matmul(ps_d[:, i % 4, 0:NE],
                                              xnT[:, k, n * SEQ + t * P:n * SEQ + (t + 1) * P],
                                              gatew[:, k, :], start=(k == 0), stop=(k == KD - 1))
                    mm.then_inc(pe_d, 1)
                pe.wait_ge(act_took, a_lat(n, KL - 1) + 1)
                for m in range(KL):
                    i = a_exo(n, m)
                    for k in range(KL):
                        mm = nc.tensor.matmul(ps_a[:, i % 4, :], expw[:, k, m * P:(m + 1) * P],
                                              latT[:, k, :], start=(k == 0), stop=(k == KL - 1))
                    mm.then_inc(pe_a, 1)
                pe.wait_ge(down_loaded, 16)
                pe.wait_ge(squared, (n + 1) * KU)
                for t in range(TB):
                    i = d_shared(n, t)
                    turn(dve_took, i)
                    for k in range(KU):
                        mm = nc.tensor.matmul(ps_d[:, i % 4, :], hid[:, k, t * P:(t + 1) * P],
                                              downw[:, k, :], start=(k == 0), stop=(k == KU - 1))
                    mm.then_inc(pe_d, 1)
                    j = a_rout(n, t)
                    pe.wait_ge(act_took, max(a_exo(n, KL - 1) + 1, j - 3))
                    for k in range(KL):
                        mm = nc.tensor.matmul(ps_a[:, j % 4, :], exoT[:, k, t * P:(t + 1) * P],
                                              fc2w[:, k, :], start=(k == 0), stop=(k == KL - 1))
                    mm.then_inc(pe_a, 1)

        @block.scalar
        def _(act):
            act.wait_ge(var_ready, NT)
            nc.scalar.activation(std[:], mv[:, :, 1], ACT.Sqrt).then_inc(std_ready, 1)
            for t in range(NT):
                act.wait_ge(pe_a, t + 1)
                nc.scalar.activation(xnT[:, :, t * P:(t + 1) * P],
                                     ps_a[:, t % 4, :].rearrange("p (k c) -> p k c", k=KD),
                                     ACT.Copy).then_inc(act_took, 1)
            for n in range(NB):
                for m in range(KD):
                    i = a_dft(n, m)
                    act.wait_ge(pe_a, i + 1)
                    if n:
                        act.wait_ge(pe_d, d_corr(n - 1, TB - 1) + 1)
                    nc.scalar.activation(power[:, m, :], ps_a[:, i % 4, :], ACT.Square).then_inc(act_took, 1)
                for m in range(KU):
                    i = a_up(n, m)
                    act.wait_ge(pe_a, i + 1)
                    if n:
                        act.wait_ge(pe_d, d_shared(n - 1, TB - 1) + 1)
                    nc.scalar.activation(hid[:, m, :], ps_a[:, i % 4, :], ACT.Relu).then_inc(act_took, 1)
                for m in range(KL):
                    i = a_lat(n, m)
                    act.wait_ge(pe_a, i + 1)
                    nc.scalar.activation(latT[:, m, :], ps_a[:, i % 4, :], ACT.Copy).then_inc(act_took, 1)
                for m in range(KL):
                    i = a_exo(n, m)
                    act.wait_ge(pe_a, i + 1)
                    nc.scalar.activation(exoT[:, m, :], ps_a[:, i % 4, :], ACT.Copy).then_inc(act_took, 1)
                for t in range(TB):
                    g = n * TB + t
                    act.wait_ge(topk_ready, g + 1)
                    nc.scalar.activation(wexp[:, g, 0:TOPK], top[:, g, 0:TOPK], ACT.Exp, bias=negmax[:, g:g + 1],
                                         accum_out=wsum[:, g:g + 1]).then_inc(weights_ready, 1)
                for t in range(TB):
                    g, i = n * TB + t, a_rout(n, t)
                    act.wait_ge(pe_a, i + 1)
                    act.wait_ge(dve_took, d_log(n, TB - 1) + 1)
                    if t >= 2:
                        act.wait_ge(z_ready, g - 1)
                    nc.scalar.activation(routed[:, t % 2, :], ps_a[:, i % 4, :], ACT.Copy,
                                         scale=rsum[:, g:g + 1]).then_inc(act_took, 1)
                act.wait_ge(zvar_ready, (n + 1) * TB)
                nc.scalar.activation(zstd[:, n * TB:(n + 1) * TB], zmv[:, n * TB:(n + 1) * TB, 1],
                                     ACT.Sqrt).then_inc(zstd_ready, 1)
                for t in range(TB):
                    act.wait_ge(affine_ready, n * TB + t + 1)
                    nc.scalar.activation(z[:, t, :], z[:, t, :], ACT.Silu).then_inc(silu_ready, 1)

        @block.vector
        def _(dve):
            link = chain_on(dve, dve_chain)
            for t in range(NT):
                dve.wait_ge(x_loaded[t], 16)
                link(nc.vector.bn_stats(stats[:, t, :], x1[:, t, :]))
                link(nc.vector.bn_aggr(mv[:, t, :], stats[:, t, :]))
                nc.vector.tensor_scalar(mv[:, t, 1:2], mv[:, t, 1:2], EPS, None, ALU.add).then_inc(var_ready, 1)
            dve.wait_ge(std_ready, 1)
            link(nc.vector.reciprocal(rstd[:], std[:]))
            for t in range(NT):
                nc.vector.tensor_scalar(xn[:, t, :], x1[:, t, :], mv[:, t, 0:1], rstd[:, t:t + 1],
                                        ALU.subtract, ALU.mult).then_inc(xn_ready, 1)
            dve.wait_ge(rows_loaded, 48)
            for n in range(NB):
                for t in range(TB):
                    g, i = n * TB + t, d_corr(n, t)
                    dve.wait_ge(pe_d, i + 1)
                    link(nc.vector.max(top[:, g, :], ps_d[:, i % 4, :]))
                    nc.vector.max_index(delay[:, g, :], top[:, g, :], ps_d[:, i % 4, :]).then_inc(dve_took, 1)
                    dve.wait_ge(dve_took, i + 1)
                    link(nc.vector.tensor_tensor(at[:, g, :], delay[:, g, :], rowbase[:, g, :], ALU.add))
                    nc.vector.tensor_scalar(negmax[:, g:g + 1], top[:, g, 0:1], -1.0, None,
                                            ALU.mult).then_inc(topk_ready, 1)
                for t in range(TB):
                    g, i = n * TB + t, d_log(n, t)
                    dve.wait_ge(pe_d, i + 1)
                    link(nc.vector.max(topl[:, g, :], ps_d[:, i % 4, 0:NE]))
                    nc.vector.tensor_tensor(rsum[:, g:g + 1], topl[:, g, 0:1], topl[:, g, 1:2],
                                            ALU.add).then_inc(dve_took, 1)
                for t in range(TB):
                    g = n * TB + t
                    dve.wait_ge(weights_ready, g + 1)
                    link(nc.vector.reciprocal(wrec[:, g:g + 1], wsum[:, g:g + 1]))
                    link(nc.vector.tensor_scalar(wexp[:, g, 0:TOPK], wexp[:, g, 0:TOPK], wrec[:, g:g + 1], None,
                                                 ALU.mult))
                    dve.wait_ge(gathered, 16 * TOPK * (g + 1))
                    link(nc.vector.tensor_scalar(mixed[:, t, :], shifted[:, 0, :], wexp[:, g, 0:1], None, ALU.mult))
                    for j in range(1, TOPK):
                        add = nc.vector.scalar_tensor_tensor(mixed[:, t, :], shifted[:, j, :], wexp[:, g, j:j + 1],
                                                             mixed[:, t, :], ALU.mult, ALU.add)
                        if j < TOPK - 1:
                            link(add)
                    add.then_inc(mixed_ready, 1)
                for t in range(TB):
                    g, i = n * TB + t, d_shared(n, t)
                    dve.wait_ge(pe_d, i + 1)
                    dve.wait_ge(act_took, a_rout(n, t) + 1)
                    nc.vector.tensor_tensor(z[:, t, :], ps_d[:, i % 4, :], routed[:, t % 2, :],
                                            ALU.add).then_inc(z_ready, 1)
                    dve.wait_ge(z_ready, g + 1)
                    nc.vector.bn_stats(zstats[:, g, :], z[:, t, :]).then_inc(dve_took, 1)
                    dve.wait_ge(dve_took, i + 1)
                    link(nc.vector.bn_aggr(zmv[:, g, :], zstats[:, g, :]))
                    nc.vector.tensor_scalar(zmv[:, g, 1:2], zmv[:, g, 1:2], EPS, None,
                                            ALU.add).then_inc(zvar_ready, 1)
                dve.wait_ge(zstd_ready, n + 1)
                link(nc.vector.reciprocal(zrstd[:, n * TB:(n + 1) * TB], zstd[:, n * TB:(n + 1) * TB]))
                for t in range(TB):
                    g = n * TB + t
                    nc.vector.tensor_scalar(z[:, t, :], z[:, t, :], zmv[:, g, 0:1], zrstd[:, g:g + 1],
                                            ALU.subtract, ALU.mult).then_inc(zn_ready, 1)
                for t in range(TB):
                    g = n * TB + t
                    dve.wait_ge(silu_ready, g + 1)
                    dve.wait_ge(mixed_ready, g + 1)
                    link(nc.vector.tensor_tensor(mixed[:, t, :], mixed[:, t, :], z[:, t, :], ALU.mult))
                    nc.vector.tensor_tensor(x1[:, g, :], x1[:, g, :], mixed[:, t, :], ALU.add).then_inc(x1_ready, 1)
                dve.wait_ge(x1_ready, (n + 1) * TB)

        @block.gpsimd
        def _(pool):
            link = chain_on(pool, pool_chain)
            pool.wait_ge(rows_loaded, 48)
            for n in range(NB):
                for m in range(KU):
                    pool.wait_ge(act_took, a_up(n, m) + 1)
                    nc.gpsimd.tensor_tensor(hid[:, m, :], hid[:, m, :], hid[:, m, :], ALU.mult).then_inc(squared, 1)
                for t in range(TB):
                    g = n * TB + t
                    pool.wait_ge(table_stored, 32 * NT)
                    pool.wait_ge(topk_ready, g + 1)
                    if g:
                        pool.wait_ge(mixed_ready, g)
                    for j in range(TOPK):
                        nc.gpsimd.indirect_dma_start(
                            shifted[:, j, :], None, table.rearrange("r (c o) -> (r c) o", o=1),
                            bass.IndirectOffsetOnAxis(ap=at[:, g, j:j + 1], axis=0)).then_inc(gathered, 16)
                for t in range(TB):
                    g = n * TB + t
                    pool.wait_ge(zn_ready, g + 1)
                    link(nc.gpsimd.tensor_tensor(z[:, t, :], z[:, t, :], gamma[:], ALU.mult))
                    nc.gpsimd.tensor_tensor(z[:, t, :], z[:, t, :], beta[:], ALU.add).then_inc(affine_ready, 1)


def mixer_inputs(nc, a, xn, ident, ones, h_hi, h_lo, xnT, group_dram, acs_dram):
    with ExitStack() as ctx:
        sem = Sems(nc, ctx)

        def sb(name, shape, dt=F32):
            return ctx.enter_context(nc.sbuf_tensor(name, shape, dt))

        stats = sb("m_stats", [P, NT, 6])
        mv = sb("m_mv", [P, NT, 2])
        std = sb("m_std", [P, NT])
        rstd = sb("m_rstd", [P, NT])
        square = sb("m_square", [P, D])
        meansq = sb("m_meansq", [P, NT])
        rms = sb("m_rms", [P, NT])
        rrms = sb("m_rrms", [P, NT])
        h = sb("m_h", [P, 2, D])
        normw = sb("m_normw", [P, KD])
        wdt = sb("m_wdt", [P, KD, HEADS])
        wdt_hi = sb("m_wdt_hi", [P, KD, HEADS], F32R)
        wdt_lo = sb("m_wdt_lo", [P, KD, HEADS], F32R)
        dtb = sb("m_dtb", [P, 1])
        alog = sb("m_alog", [P, 1])
        aexp = sb("m_aexp", [P, 1])
        v = sb("m_v", [P, T])
        av = sb("m_av", [P, T])
        e = sb("m_e", [P, T])
        u1 = sb("m_u1", [P, T])
        ln = sb("m_ln", [P, T])
        z = sb("m_z", [P, T])
        dt = sb("m_dt", [P, T])
        step = sb("m_step", [P, T])
        acs = sb("m_acs", [P, T])
        decay = sb("m_decay", [P, T])
        lastdecay = sb("m_lastdecay", [P, 4])
        diag = sb("m_diag", [P, 4, HEADS])
        hw = sb("m_hw", [P, 2, KD, P])
        group = sb("m_group", [P, GROUPS, GROUP_N])
        ps = ctx.enter_context(nc.psum_tensor("m_ps", [P, 8, 512], F32))

        loaded = sem("m_loaded")
        dve_chain = sem("m_dve_chain")
        act_chain = sem("m_act_chain")
        var_ready = sem("m_var_ready")
        std_ready = sem("m_std_ready")
        xn_ready = sem("m_xn_ready")
        meansq_ready = sem("m_meansq_ready")
        meansq_eps = sem("m_meansq_eps")
        rms_ready = sem("m_rms_ready")
        h_ready = sem("m_h_ready")
        xn_turned = sem("m_xn_turned")
        h_turned = sem("m_h_turned")
        xnT_ready = sem("m_xnT_ready")
        hT_ready = sem("m_hT_ready")
        dt_proj = sem("m_dt_proj")
        v_ready = sem("m_v_ready")
        e_ready = sem("m_e_ready")
        u1_ready = sem("m_u1_ready")
        ln_ready = sem("m_ln_ready")
        dt_ready = sem("m_dt_ready")
        aexp_ready = sem("m_aexp_ready")
        acs_ready = sem("m_acs_ready")
        decay_ready = sem("m_decay_ready")
        lastdecay_ready = sem("m_lastdecay_ready")
        dd_ready = sem("m_dd_ready")
        diag_ready = sem("m_diag_ready")
        turned = sem("m_turned")
        acs_stored = sem("m_acs_stored")
        ones_ready = sem("m_ones_ready")
        wdt_split = sem("m_wdt_split")
        group_ready = sem("m_group_ready")
        hw_ready = sem("m_hw_ready")
        h_hi_ready = sem("m_h_hi_ready")

        block = ctx.enter_context(nc.Block())

        @block.sync
        def _(sp):
            sp.dma_start(normw[:], a["norm_w"]).then_inc(loaded, 16)
            sp.dma_start(wdt[:], a["w_dt"]).then_inc(loaded, 16)
            sp.dma_start(dtb[:], a["dt_bias"]).then_inc(loaded, 16)
            sp.dma_start(alog[:], a["a_log"]).then_inc(loaded, 16)
            sp.wait_ge(acs_ready, NT)
            sp.dma_start(acs_dram, acs[:]).then_inc(acs_stored, 16)
            sp.wait_ge(group_ready, 4)
            sp.dma_start(group_dram, group[:]).then_inc(acs_stored, 16)
            sp.wait_ge(acs_stored, 32)

        @block.gpsimd
        def _(pool):
            nc.gpsimd.memset(ones[:], 1.0).then_inc(ones_ready, 1)
            pool.wait_ge(loaded, 64)
            nc.gpsimd.tensor_copy(wdt_hi[:], wdt[:]).then_inc(wdt_split, 1)
            pool.wait_ge(wdt_split, 1)
            nc.gpsimd.tensor_tensor(wdt_lo[:], wdt[:], wdt_hi[:].bitcast(F32), ALU.subtract).then_inc(wdt_split, 1)

        @block.tensor
        def _(pe):
            for t in range(NT):
                pe.wait_ge(xn_ready, t + 1)
                if t >= 2:
                    pe.wait_ge(xnT_ready, t - 1)
                for k in range(KD):
                    mm = nc.tensor.transpose(ps[:, t % 2, k * P:(k + 1) * P], xn[:, t, k * P:(k + 1) * P], ident[:])
                mm.then_inc(xn_turned, 1)
                pe.wait_ge(h_ready, t + 1)
                if t >= 2:
                    pe.wait_ge(hT_ready, t - 1)
                for k in range(KD):
                    mm = nc.tensor.transpose(ps[:, 2 + t % 2, k * P:(k + 1) * P],
                                             h[:, t % 2, k * P:(k + 1) * P], ident[:])
                mm.then_inc(h_turned, 1)
            pe.wait_ge(wdt_split, 2)
            pe.wait_ge(hT_ready, NT)
            for n in range(NB):
                for k in range(KD):
                    cols = slice(n * SEQ, (n + 1) * SEQ)
                    mm = three_passes(nc, ps[:, 4 + n, :], wdt_hi[:, k, :], wdt_lo[:, k, :], h_hi[:, k, cols],
                                      h_lo[:, k, cols], k == 0, k == KD - 1)
                mm.then_inc(dt_proj, 1)
            pe.wait_ge(xnT_ready, NT)
            pe.wait_ge(dt_ready, 1)
            for t in range(NT):
                mm = nc.tensor.transpose(ps[:, t // 4, (t % 4) * P:(t % 4 + 1) * P], dt[:, t * P:(t + 1) * P], ident[:])
            mm.then_inc(turned, 1)
            pe.wait_ge(acs_ready, NT)
            for t in range(NT):
                mm = nc.tensor.transpose(ps[:, 2 + t // 4, (t % 4) * P:(t % 4 + 1) * P], acs[:, t * P:(t + 1) * P],
                                         ident[:])
            mm.then_inc(turned, 1)
            pe.wait_ge(dd_ready, 1)
            for t in range(NT):
                mm = nc.tensor.transpose(ps[:, 6 + t // 4, (t % 4) * P:(t % 4 + 1) * P], decay[:, t * P:(t + 1) * P],
                                         ident[:])
            mm.then_inc(turned, 1)
            pe.wait_ge(diag_ready, 4)
            pe.wait_ge(ones_ready, 1)
            pe.wait_ge(v_ready, NB)
            mm = nc.tensor.matmul(ps[:, 4, :], ones[:], diag[:].rearrange("p c h -> p (c h)"), start=True, stop=True)
            mm.then_inc(turned, 1)

        @block.scalar
        def _(act):
            act.wait_ge(var_ready, NT)
            nc.scalar.activation(std[:], mv[:, :, 1], ACT.Sqrt).then_inc(std_ready, 1)
            for t in range(NT):
                act.wait_ge(xn_ready, t + 1)
                if t:
                    act.wait_ge(meansq_ready, t)
                nc.scalar.activation(square[:], xn[:, t, :], ACT.Square,
                                     accum_out=meansq[:, t:t + 1]).then_inc(meansq_ready, 1)
            act.wait_ge(meansq_eps, 1)
            nc.scalar.activation(rms[:], meansq[:], ACT.Sqrt).then_inc(rms_ready, 1)
            for t in range(NT):
                act.wait_ge(xn_turned, t + 1)
                nc.scalar.activation(xnT[:, :, t * P:(t + 1) * P],
                                     ps[:, t % 2, :].rearrange("p (k c) -> p k c", k=KD),
                                     ACT.Copy).then_inc(xnT_ready, 1)
            act.wait_ge(v_ready, NB)
            nc.scalar.activation(av[:], v[:], ACT.Abs).then_inc(act_chain, 1)
            act.wait_ge(act_chain, 1)
            nc.scalar.activation(e[:], av[:], ACT.Exp, scale=-1.0).then_inc(e_ready, 1)
            act.wait_ge(loaded, 64)
            nc.scalar.activation(aexp[:], alog[:], ACT.Exp).then_inc(aexp_ready, 1)
            act.wait_ge(u1_ready, 1)
            nc.scalar.activation(ln[:], u1[:], ACT.Ln).then_inc(ln_ready, 1)
            for t in range(NT):
                act.wait_ge(acs_ready, t + 1)
                last = acs[:, (t + 1) * P - 1:(t + 1) * P]
                nc.scalar.activation(decay[:, t * P:(t + 1) * P], acs[:, t * P:(t + 1) * P], ACT.Exp,
                                     bias=last, scale=-1.0).then_inc(decay_ready, 1)
            for i, t in enumerate((1, 2, 5, 6)):
                ins = nc.scalar.activation(lastdecay[:, i:i + 1], acs[:, (t + 1) * P - 1:(t + 1) * P], ACT.Exp)
            ins.then_inc(lastdecay_ready, 1)

        @block.vector
        def _(dve):
            link = chain_on(dve, dve_chain)
            for t in range(NT):
                link(nc.vector.bn_stats(stats[:, t, :], xn[:, t, :]))
                link(nc.vector.bn_aggr(mv[:, t, :], stats[:, t, :]))
                nc.vector.tensor_scalar(mv[:, t, 1:2], mv[:, t, 1:2], EPS, None, ALU.add).then_inc(var_ready, 1)
            dve.wait_ge(std_ready, 1)
            link(nc.vector.reciprocal(rstd[:], std[:]))
            for t in range(NT):
                nc.vector.tensor_scalar(xn[:, t, :], xn[:, t, :], mv[:, t, 0:1], rstd[:, t:t + 1],
                                        ALU.subtract, ALU.mult).then_inc(xn_ready, 1)
            dve.wait_ge(meansq_ready, NT)
            nc.vector.tensor_scalar(meansq[:], meansq[:], 1.0 / D, EPS, ALU.mult, ALU.add).then_inc(meansq_eps, 1)
            dve.wait_ge(rms_ready, 1)
            link(nc.vector.reciprocal(rrms[:], rms[:]))
            dve.wait_ge(loaded, 64)
            dve.wait_ge(xn_ready, NT)
            for t in range(NT + 1):
                if t < NT:
                    if t >= 2:
                        dve.wait_ge(h_turned, t - 1)
                    nc.vector.tensor_scalar(h[:, t % 2, :], xn[:, t, :], rrms[:, t:t + 1], None,
                                            ALU.mult).then_inc(h_ready, 1)
                if t:
                    s = t - 1
                    dve.wait_ge(h_turned, s + 1)
                    nc.vector.tensor_tensor(hw[:, s % 2], ps[:, 2 + s % 2, :].rearrange("p (k c) -> p k c", k=KD),
                                            normw[:].unsqueeze(2).to_broadcast((P, KD, P)),
                                            ALU.mult).then_inc(hw_ready, 1)
                    dve.wait_ge(hw_ready, s + 1)
                    nc.vector.tensor_copy(h_hi[:, :, s * P:(s + 1) * P], hw[:, s % 2]).then_inc(h_hi_ready, 1)
                    dve.wait_ge(h_hi_ready, s + 1)
                    nc.vector.tensor_tensor(h_lo[:, :, s * P:(s + 1) * P], hw[:, s % 2],
                                            h_hi[:, :, s * P:(s + 1) * P].bitcast(F32),
                                            ALU.subtract).then_inc(hT_ready, 1)
            for n in range(NB):
                dve.wait_ge(dt_proj, n + 1)
                nc.vector.tensor_scalar(v[:, n * SEQ:(n + 1) * SEQ], ps[:, 4 + n, :], dtb[:, 0:1], None,
                                        ALU.add).then_inc(v_ready, 1)
            dve.wait_ge(e_ready, 1)
            nc.vector.tensor_scalar(u1[:], e[:], 1.0, None, ALU.add).then_inc(u1_ready, 1)
            dve.wait_ge(u1_ready, 1)
            link(nc.vector.tensor_scalar(av[:], u1[:], -1.0, None, ALU.add))
            link(nc.vector.tensor_scalar(z[:], av[:], 0.0, None, ALU.is_equal))
            link(nc.vector.tensor_tensor(av[:], av[:], z[:], ALU.add))
            link(nc.vector.reciprocal(step[:], av[:]))
            link(nc.vector.tensor_tensor(step[:], step[:], e[:], ALU.mult))
            link(nc.vector.tensor_tensor(z[:], z[:], e[:], ALU.mult))
            dve.wait_ge(ln_ready, 1)
            link(nc.vector.tensor_tensor(ln[:], ln[:], step[:], ALU.mult))
            link(nc.vector.tensor_tensor(ln[:], ln[:], z[:], ALU.add))
            nc.vector.scalar_tensor_tensor(dt[:], v[:], 0.0, ln[:], ALU.max, ALU.add).then_inc(dt_ready, 1)
            dve.wait_ge(dt_ready, 1)
            dve.wait_ge(aexp_ready, 1)
            link(nc.vector.tensor_scalar(step[:], dt[:], aexp[:, 0:1], -1.0, ALU.mult, ALU.mult))
            link(nc.vector.memset(u1[:], 1.0))
            for t in range(NT):
                c = slice(t * P, (t + 1) * P)
                nc.vector.tensor_tensor_scan(acs[:, c], u1[:, c], step[:, c], 0.0, ALU.mult,
                                             ALU.add).then_inc(acs_ready, 1)
            dve.wait_ge(decay_ready, NT)
            nc.vector.tensor_tensor(decay[:], decay[:], dt[:], ALU.mult).then_inc(dd_ready, 1)
            dve.wait_ge(lastdecay_ready, 1)
            for i in range(4):
                nc.vector.tensor_scalar(diag[:, i, :], ident[:], lastdecay[:, i:i + 1], None,
                                        ALU.mult).then_inc(diag_ready, 1)

            def banks(b):
                return ps[:, b:b + 2, :].rearrange("p b (t g h) -> p (b t) g h", t=4, g=GROUPS)

            def part(i):
                return group[:, :, i * NT * HG:(i + 1) * NT * HG].rearrange("p g (t h) -> p t g h", t=NT)
            dve.wait_ge(turned, 1)
            nc.vector.tensor_copy(part(0), banks(0)).then_inc(group_ready, 1)
            dve.wait_ge(turned, 2)
            nc.vector.tensor_copy(part(2), banks(2)).then_inc(group_ready, 1)
            dve.wait_ge(turned, 3)
            nc.vector.tensor_copy(part(1), banks(6)).then_inc(group_ready, 1)
            dve.wait_ge(turned, 4)
            nc.vector.tensor_copy(group[:, :, 3 * NT * HG:].rearrange("p g (c h) -> p c g h", c=4),
                                  ps[:, 4, :].rearrange("p (c g h) -> p c g h", c=4, g=GROUPS)).then_inc(group_ready, 1)


def layer1_ffn(nc, a, xnT, g_dram):
    with ExitStack() as ctx:
        sem = Sems(nc, ctx)

        def sb(name, shape, dt=F32):
            return ctx.enter_context(nc.sbuf_tensor(name, shape, dt))

        w = sb("f_w", [P, NQ, QC])
        q = sb("f_q", [P, 2, QC], I32)
        s = sb("f_s", [P, 2, QC])
        gated = sb("f_gated", [P, 2, SEQ])
        inner = sb("f_inner", [P, KI, SEQ])
        g = sb("f_g", [P, 2, D])
        ps_gate = ctx.enter_context(nc.psum_tensor("f_ps_gate", [P, 2, 512], F32))
        ps_up = ctx.enter_context(nc.psum_tensor("f_ps_up", [P, 2, 512], F32))
        ps_out = ctx.enter_context(nc.psum_tensor("f_ps_out", [P, 2, 512], F32))

        piece_loaded = [sem("f_piece_loaded0"), sem("f_piece_loaded1")]
        dequantised = sem("f_dequantised")
        gate_done = sem("f_gate_done")
        up_done = sem("f_up_done")
        gate_silu = sem("f_gate_silu")
        inner_ready = sem("f_inner_ready")
        out_done = sem("f_out_done")
        g_ready = sem("f_g_ready")
        g_stored = [sem("f_g_stored0"), sem("f_g_stored1")]

        flat = w[:].rearrange("p n c -> p (n c)")
        w_gate = flat[:, 0:KD * INT].rearrange("p (k n) -> p k n", k=KD)
        w_up = flat[:, KD * INT:2 * KD * INT].rearrange("p (k n) -> p k n", k=KD)
        w_down = flat[:, 2 * KD * INT:].rearrange("p (k n) -> p k n", k=KI)
        block = ctx.enter_context(nc.Block())

        @block.sync
        def _(sp):
            for i in range(NQ):
                if i >= 2:
                    sp.wait_ge(dequantised, i - 1)
                sp.dma_start(q[:, i % 2, :], a["q"][i]).then_inc(piece_loaded[i % 2], 16)
                sp.dma_start(s[:, i % 2, :], a["s"][i:i + 1, :].to_broadcast((P, QC))).then_inc(
                    piece_loaded[i % 2], 16)
            for j in range(NT):
                sp.wait_ge(g_ready, j + 1)
                sp.dma_start(g_dram[:, j, :], g[:, j % 2, :]).then_inc(g_stored[j % 2], 16)
            for slot in g_stored:
                sp.wait_ge(slot, 16 * NT // 2)

        @block.tensor
        def _(pe):
            for n in range(NB):
                for m in range(KI):
                    j = n * KI + m
                    if n == 0:
                        pe.wait_ge(dequantised, 4 * KD)
                    if j >= 2:
                        pe.wait_ge(gate_silu, j - 1)
                        pe.wait_ge(inner_ready, j - 1)
                    for wt, bank, done in ((w_gate, ps_gate, gate_done), (w_up, ps_up, up_done)):
                        for k in range(KD):
                            mm = nc.tensor.matmul(bank[:, j % 2, :], wt[:, k, m * P:(m + 1) * P],
                                                  xnT[:, k, n * SEQ:(n + 1) * SEQ],
                                                  start=(k == 0), stop=(k == KD - 1))
                        mm.then_inc(done, 1)
                pe.wait_ge(dequantised, NQ)
                pe.wait_ge(inner_ready, (n + 1) * KI)
                for t in range(TB):
                    j = n * TB + t
                    if j >= 2:
                        pe.wait_ge(g_ready, j - 1)
                    for k in range(KI):
                        mm = nc.tensor.matmul(ps_out[:, j % 2, :], inner[:, k, t * P:(t + 1) * P], w_down[:, k, :],
                                              start=(k == 0), stop=(k == KI - 1))
                    mm.then_inc(out_done, 1)

        @block.scalar
        def _(act):
            for n in range(NB):
                for m in range(KI):
                    j = n * KI + m
                    act.wait_ge(gate_done, j + 1)
                    if j >= 2:
                        act.wait_ge(inner_ready, j - 1)
                    nc.scalar.activation(gated[:, j % 2, :], ps_gate[:, j % 2, :], ACT.Silu).then_inc(gate_silu, 1)
                for t in range(TB):
                    j = n * TB + t
                    act.wait_ge(out_done, j + 1)
                    if j >= 2:
                        act.wait_ge(g_stored[j % 2], 16 * (j // 2))
                    nc.scalar.activation(g[:, j % 2, :], ps_out[:, j % 2, :], ACT.Silu).then_inc(g_ready, 1)

        @block.vector
        def _(dve):
            for i in range(NQ):
                dve.wait_ge(piece_loaded[i % 2], 32 * (i // 2 + 1))
                nc.vector.tensor_tensor(w[:, i, :], q[:, i % 2, :], s[:, i % 2, :], ALU.mult).then_inc(dequantised, 1)
            for n in range(NB):
                if n:
                    dve.wait_ge(out_done, n * TB)
                for m in range(KI):
                    j = n * KI + m
                    dve.wait_ge(up_done, j + 1)
                    dve.wait_ge(gate_silu, j + 1)
                    nc.vector.tensor_tensor(inner[:, m, :], gated[:, j % 2, :], ps_up[:, j % 2, :],
                                            ALU.mult).then_inc(inner_ready, 1)


BC_SLOT = 2
LOADS = [("HG", k) for k in range(BC_SLOT)] + [("BC", 0)] + [("HG", k) for k in range(BC_SLOT, KC)]
NLOAD = len(LOADS)
CONVS = [2 + k for k in range(BC_SLOT)] + [0, 1] + [2 + k for k in range(BC_SLOT, KC)]
NCONV = len(CONVS)


def slot_jobs(k):
    def ahead(i):
        return i // KC, i % KC
    jobs = [("CB", 1, 0), ("BT", 1, 0)] if k == 5 else []
    jobs += [("ST", *ahead(k + 1)), ("DIAG", 0, k), ("OFF", 0, k), ("T", *ahead(k + 2))]
    if k == BC_SLOT:
        jobs += [("H", 1, CONVS.index(0)), ("H", 1, CONVS.index(1))]
    return jobs + [("G", 1, k), ("H", 1, CONVS.index(2 + k))]


JOBS = [job for k in range(KC) for job in slot_jobs(k)]
PER = {"ST": KC, "DIAG": KC, "OFF": KC, "H": NCONV, "T": KC, "G": KC, "CB": 1, "BT": 1}
BANKS = 4
assert len(JOBS) % BANKS == 0


def mixer(nc, a, acc, ident, ones, h_hi, h_lo, group_dram, acs_dram, x1_dram, g_dram, out):
    with ExitStack() as ctx:
        sem = Sems(nc, ctx)

        def sb(name, shape, dt=F32):
            return ctx.enter_context(nc.sbuf_tensor(name, shape, dt))

        mask = sb("s_mask", [P, P])
        par = sb("s_par", [P, 2, 66])
        steps = sb("s_steps", [P, 2, 3, TB, HG])
        cdecay = sb("s_cdecay", [P, 2, 2, HG])
        skip4 = sb("s_skip4", [P, 2, KC])
        w_raw = sb("s_w_raw", [P, 2, 2 * KD * P])
        w_hi = sb("s_w_hi", [P, 2, 2 * KD * P], F32R)
        w_lo = sb("s_w_lo", [P, 2, 2 * KD * P], F32R)
        wo_raw = sb("s_wo_raw", [P, 2, D])
        wo_hi = sb("s_wo_hi", [P, 2, D], F32R)
        wo_lo = sb("s_wo_lo", [P, 2, D], F32R)
        cv = sb("s_cv", [P, 2, SEQ])
        th = sb("s_th", [P, 2, SEQ])
        tg = sb("s_tg", [P, SEQ])
        bT = sb("s_bT", [P, 2, SEQ])
        cT = sb("s_cT", [P, 2, SEQ])
        hid = sb("s_hid", [P, KC, SEQ])
        gate = sb("s_gate", [P, KC, SEQ])
        b_l = sb("s_b_l", [P, 2, TB - 1, NST])
        cbt = sb("s_cbt", [P, 2, TB, P])
        hdt = sb("s_hdt", [P, 2, TB, P])
        hdd = sb("s_hdd", [P, 2, TB - 1, P])
        state = sb("s_state", [P, 2, TB - 1, P])
        rows = sb("s_rows", [P, 4, SEQ])
        lm = sb("s_lm", [P, 4, SEQ])
        scale = sb("s_scale", [P, 2, 3 * P])
        ysum = sb("s_ysum", [P, 2, SEQ])
        yoff = sb("s_yoff", [P, 2, 3 * P])
        y_hi = sb("s_y_hi", [P, 2, SEQ], F32R)
        y_lo = sb("s_y_lo", [P, 2, SEQ], F32R)
        sq = sb("s_sq", [P, 2, SEQ])
        ssq = sb("s_ssq", [P, SEQ])
        meansq = sb("s_meansq", [P, TB])
        rms = sb("s_rms", [P, TB])
        rrms = sb("s_rrms", [P, TB])
        ps = ctx.enter_context(nc.psum_tensor("s_ps", [P, BANKS, 512], F32))
        ps_o = ctx.enter_context(nc.psum_tensor("s_ps_o", [P, TB, 512], F32))

        mask_loaded = sem("s_mask_loaded")
        par_loaded = [sem(f"s_par_loaded{b}") for b in range(2)]
        w_loaded = [sem(f"s_w_loaded{b}") for b in range(2)]
        wo_loaded = [sem(f"s_wo_loaded{b}") for b in range(2)]
        rows_loaded = [sem(f"s_rows_loaded{i}") for i in range(4)]
        done = {kind: sem(f"s_{kind.lower()}_done") for kind in PER}
        took = {kind: sem(f"s_{kind.lower()}_took") for kind in PER}
        ssq_done = sem("s_ssq_done")
        ssq_took = sem("s_ssq_took")
        op_done = sem("s_op_done")
        op_took = sem("s_op_took")
        w_hi_ready = sem("s_w_hi_ready")
        w_lo_ready = sem("s_w_lo_ready")
        wo_hi_ready = sem("s_wo_hi_ready")
        wo_lo_ready = sem("s_wo_lo_ready")
        skip_ready = sem("s_skip_ready")
        tap_ready = sem("s_tap_ready")
        conv_chain = sem("s_conv_chain")
        th_ready = sem("s_th_ready")
        tile_ready = sem("s_tile_ready")
        tg_ready = sem("s_tg_ready")
        state_chain = sem("s_state_chain")
        diff_ready = sem("s_diff_ready")
        exp_ready = sem("s_exp_ready")
        scale_ready = sem("s_scale_ready")
        m_ready = sem("s_m_ready")
        pool_chain = sem("s_pool_chain")
        y_ready = sem("s_y_ready")
        y_hi_ready = sem("s_y_hi_ready")
        y_lo_ready = sem("s_y_lo_ready")
        sq_ready = sem("s_sq_ready")
        ssq_ready = sem("s_ssq_ready")
        rms_ready = sem("s_rms_ready")
        rrms_ready = sem("s_rrms_ready")

        class Unit:

            def __init__(self, g, b, first=False, last=False):
                self.g, self.b, self.u, self.first, self.last = g, b, 2 * g + b, first, last

            def ahead(self, n):
                if n == 1:
                    return Unit(self.g + self.b, 1 - self.b)
                return self if n == 0 else Unit(self.g - 1 + self.b, 1 - self.b)

            def at(self, per, i):
                return self.u * per + i + 1

        def exists(un, job):
            return not (job[1] == 1 and un.last)

        def bank_free(pe, un, job):
            pos, back = JOBS.index(job) - BANKS, 0
            while True:
                if pos < 0:
                    if un.first:
                        for kind, n in (("H", NCONV), ("G", KC), ("T", 2), ("ST", 1)):
                            pe.wait_ge(took[kind], n)
                        return
                    pos = (JOBS.index(job) % BANKS) + (len(JOBS) - 1 - JOBS.index(job) % BANKS) // BANKS * BANKS
                    back = -1
                if back or exists(un, JOBS[pos]):
                    kind, ahead, i = JOBS[pos]
                    pe.wait_ge(took[kind], (un.u + back + ahead) * PER[kind] + i + 1)
                    return
                pos -= BANKS

        def bank(job):
            return ps[:, JOBS.index(job) % BANKS, :]

        def load_slot(v, c):
            return (v.b + c) % 2, NLOAD * v.g + (NLOAD * v.b + c) // 2 + 1

        def loads_of(k):
            return [c for c in range(NLOAD) if LOADS[c] == ("HG", k) or k == BC_SLOT and LOADS[c][0] == "BC"]

        def conv_tile(v, i):
            j = CONVS[i]
            return bT[:, v.b, :] if j == 0 else cT[:, v.b, :] if j == 1 else hid[:, j - 2, :]

        def first_tiles():
            n = {"H": 0, "G": 0}
            at = 0
            for c, (what, _) in enumerate(LOADS):
                for half in ((0, 1) if what == "BC" else (1, 0)):
                    kind = "G" if what == "HG" and half else "H"
                    yield kind, n[kind], c, half, ps[:, at % BANKS, :]
                    n[kind] += 1
                    at += 1

        def channel_tile_before(un, k):
            if (k == 0 and un.first) or (k and un.last):
                return None
            i = CONVS.index(2 + (k - 1) % KC)
            return un.ahead(1 if k else 0), i, bank(("H", 1, i))

        def sp_params(sp, v, wait):
            if wait is not None:
                sp.wait_ge(y_hi_ready, wait)
                sp.wait_ge(y_lo_ready, wait)
            sp.dma_start(par[:, v.b], a["par"][:, bass.ds(v.g, 1), :].rearrange("p g c -> p (g c)")
                         ).then_inc(par_loaded[v.b], 16)
            src = group_dram[:, bass.ds(v.g, 1), 0:3 * NT * HG].rearrange("p g (s t h) -> p (g s) (t h)", s=3, t=NT)
            sp.dma_start(steps[:, v.b].rearrange("p s t h -> p s (t h)"),
                         src[:, :, v.b * TB * HG:(v.b + 1) * TB * HG]).then_inc(par_loaded[v.b], 16)
            at = 3 * NT * HG + v.b * 2 * HG
            sp.dma_start(cdecay[:, v.b].rearrange("p c h -> p (c h)"),
                         group_dram[:, bass.ds(v.g, 1), at:at + 2 * HG].rearrange("p g c -> p (g c)")
                         ).then_inc(par_loaded[v.b], 16)

        def sp_load(sp, v, c, free=True):
            slot, _ = load_slot(v, c)
            if free:
                sp.wait_ge(w_lo_ready, v.u * NLOAD + c - 1)
            sp.dma_start(w_raw[:, slot, :], a["w_in"][bass.ds(v.g * NLOAD + c, 1), :, :].rearrange("o p n -> (o p) n")
                         ).then_inc(w_loaded[slot], 16)

        def sp_rows(sp, v, k, free=True):
            for h in (2 * k, 2 * k + 1):
                if free:
                    sp.wait_ge(diff_ready, v.u * HG + h - 3)
                    sp.wait_ge(scale_ready, v.u * HG + h - 3)
                sp.dma_start(rows[:, h % 4, :], acs_dram[bass.ds(v.g * HG + h, 1), v.b * SEQ:(v.b + 1) * SEQ]
                             .to_broadcast((P, SEQ))).then_inc(rows_loaded[h % 4], 16)

        def sp_first(sp):
            v = Unit(0, 0, first=True)
            sp.dma_start(mask[:], a["mask"]).then_inc(mask_loaded, 16)
            sp_params(sp, v, None)
            for c in range(NLOAD):
                sp_load(sp, v, c, free=c >= 2)
            for k in range(2):
                sp_rows(sp, v, k, free=False)

        def sp_unit(sp, un):
            for k in range(KC):
                if not (un.first and k < 2):
                    sp.wait_ge(wo_lo_ready, un.u * KC + k - 1)
                sp.dma_start(wo_raw[:, k % 2, :], a["w_out"][bass.ds(un.g * KC + k, 1), :, :]
                             .rearrange("o p n -> (o p) n")).then_inc(wo_loaded[k % 2], 16)
                n, i = (k + 2) // KC, (k + 2) % KC
                if not (n and un.last):
                    sp_rows(sp, un.ahead(n), i)
                if not un.last:
                    for c in loads_of(k):
                        sp_load(sp, un.ahead(1), c)
                if not un.last and k == 0:
                    sp_params(sp, un.ahead(1), None if un.first else un.u * KC)

        def pe_project(pe, v, c, half, dst, kind):
            slot, _ = load_slot(v, c)
            pe.wait_ge(w_hi_ready, v.at(NLOAD, c))
            pe.wait_ge(w_lo_ready, v.at(NLOAD, c))
            cols = slice(v.b * SEQ, (v.b + 1) * SEQ)
            for k in range(KD):
                at = slice((half * KD + k) * P, (half * KD + k + 1) * P)
                mm = three_passes(nc, dst, w_hi[:, slot, at], w_lo[:, slot, at], h_hi[:, k, cols], h_lo[:, k, cols],
                                  k == 0, k == KD - 1)
            mm.then_inc(done[kind], 1)

        def pe_cb(pe, v, dst):
            pe.wait_ge(tile_ready, v.at(NCONV, CONVS.index(1)))
            for i in range(TB):
                c = slice(i * P, (i + 1) * P)
                mm = nc.tensor.matmul(dst[:, c], bT[:, v.b, c], cT[:, v.b, c], start=True, stop=True)
            mm.then_inc(done["CB"], 1)

        def pe_bt(pe, v, dst):
            for i in range(TB - 1):
                c = slice(i * P, (i + 1) * P)
                mm = nc.tensor.transpose(dst[:, c], bT[:, v.b, c], ident[:])
            mm.then_inc(done["BT"], 1)

        def pe_turn(pe, v, k, dst):
            pe.wait_ge(tile_ready, v.at(NCONV, CONVS.index(2 + k)))
            for i in range(TB):
                c = slice(i * P, (i + 1) * P)
                mm = nc.tensor.transpose(dst[:, c], hid[:, k, c], ident[:])
            mm.then_inc(done["T"], 1)

        def pe_state(pe, v, k, dst):
            pe.wait_ge(took["BT"], v.at(1, 0))
            pe.wait_ge(took["T"], v.at(KC, k))
            for i in range(TB - 1):
                mm = nc.tensor.matmul(dst[:, i * P:(i + 1) * P], b_l[:, v.b, i, :], hdd[:, k % 2, i, :],
                                      start=True, stop=True)
            mm.then_inc(done["ST"], 1)

        def pe_op(pe, v, k, tiles):
            if tiles[0] == 0:
                for s in (wo_hi_ready, wo_lo_ready, y_hi_ready, y_lo_ready):
                    pe.wait_ge(s, v.at(KC, k))
            for t in tiles:
                c = slice(t * P, (t + 1) * P)
                mm = three_passes(nc, ps_o[:, t, :], y_hi[:, k % 2, c], y_lo[:, k % 2, c], wo_hi[:, k % 2, :],
                                  wo_lo[:, k % 2, :], k == 0, k == KC - 1)
            if tiles[-1] == TB - 1:
                mm.then_inc(op_done, 1)

        def pe_ssq(pe, v, dst):
            pe.wait_ge(ssq_ready, v.at(KC - 1, KC - 2))
            for t in range(TB):
                mm = nc.tensor.matmul(dst[:, 3 * P + t:3 * P + t + 1], ssq[:, t * P:(t + 1) * P], ones[:, 0:1], start=True, stop=True)
            mm.then_inc(ssq_done, 1)

        def pe_first(pe):
            v = Unit(0, 0, first=True)
            banks = [tile[:2] for tile in first_tiles()]
            for n, (kind, i, c, half, src) in enumerate(first_tiles()):
                if n >= BANKS:
                    pe.wait_ge(took[banks[n - BANKS][0]], banks[n - BANKS][1] + 1)
                pe_project(pe, v, c, half, src, kind)
            pe.wait_ge(took["H"], NCONV)
            pe.wait_ge(took["G"], KC)
            pe_cb(pe, v, ps[:, 0, :])
            pe_bt(pe, v, ps[:, 1, :])
            pe_turn(pe, v, 0, ps[:, 2, :])
            pe_turn(pe, v, 1, ps[:, 3, :])
            pe.wait_ge(took["CB"], 1)
            pe_state(pe, v, 0, ps[:, 0, :])

        def pe_unit(pe, un):
            prev = un.ahead(-1) if not un.first else None
            for k in range(KC):
                before = (un, k - 1) if k else (prev, KC - 1)
                for job in slot_jobs(k):
                    kind, n, i = job
                    if exists(un, job):
                        v = un.ahead(n)
                        dst = bank(job)
                        bank_free(pe, un, job)
                        if kind == "CB":
                            pe_cb(pe, v, dst)
                        elif kind == "BT":
                            pe_bt(pe, v, dst)
                        elif kind == "ST":
                            pe_state(pe, v, i, dst)
                        elif kind == "T":
                            pe_turn(pe, v, i, dst)
                        elif kind == "H":
                            j = CONVS[i]
                            c, half = (LOADS.index(("BC", 0)), j) if j < 2 else (LOADS.index(("HG", j - 2)), 0)
                            pe_project(pe, v, c, half, dst, "H")
                        elif kind == "G":
                            pe_project(pe, v, LOADS.index(("HG", i)), 1, dst, "G")
                        elif kind == "DIAG":
                            pe.wait_ge(m_ready, v.at(HG, 2 * k + 1))
                            pe.wait_ge(took["T"], v.at(KC, k))
                            for e in range(2):
                                for j in range(TB):
                                    c = slice(j * P, (j + 1) * P)
                                    mm = nc.tensor.matmul(dst[e * HP:(e + 1) * HP, c],
                                                          hdt[:, k % 2, j, e * HP:(e + 1) * HP],
                                                          lm[:, (2 * k + e) % 4, c], start=True, stop=True)
                            mm.then_inc(done["DIAG"], 1)
                        else:
                            if k == 0 and not un.first:
                                pe_ssq(pe, prev, dst)
                            pe.wait_ge(took["ST"], v.at(KC, k))
                            for j in range(TB - 1):
                                mm = nc.tensor.matmul(dst[:, j * P:(j + 1) * P], state[:, k % 2, j, :],
                                                      cT[:, un.b, (j + 1) * P:(j + 2) * P], start=True, stop=True)
                            mm.then_inc(done["OFF"], 1)
                    if before[0] is not None and kind in ("DIAG", "OFF"):
                        if kind == "DIAG" and before[1] == 0 and not (before[0].first):
                            pe.wait_ge(op_took, before[0].u * TB)
                        pe_op(pe, *before, (0, 1) if kind == "DIAG" else (2, 3))

        def pe_last(pe):
            v = Unit(GROUPS - 1, 1)
            pe_op(pe, v, KC - 1, (0, 1))
            pe_op(pe, v, KC - 1, (2, 3))
            pe.wait_ge(took["OFF"], v.at(KC, KC - 1))
            pe_ssq(pe, v, ps[:, 0, :])

        def act_w(act, v, c, first=False):
            slot, n = load_slot(v, c)
            act.wait_ge(w_loaded[slot], 16 * n)
            if not (first and c < 2):
                act_done(act, v, c - 2)
            nc.scalar.activation(w_hi[:, slot, :], w_raw[:, slot, :], ACT.Copy).then_inc(w_hi_ready, 1)

        def act_done(eng, v, c):
            u = v.u if c >= 0 else v.u - 1
            kind, k = LOADS[c % NLOAD]
            eng.wait_ge(done["H"], u * NCONV + CONVS.index(1 if kind == "BC" else 2 + k) + 1)

        def act_diff(act, v, k, first=False):
            if not first:
                act.wait_ge(done["DIAG"], v.u * KC + k - 1)
            for h in (2 * k, 2 * k + 1):
                act.wait_ge(rows_loaded[h % 4], 16 * (v.u * (HG // 4) + h // 4 + 1))
                for i in range(TB):
                    c = slice(i * P, (i + 1) * P)
                    ins = nc.scalar.activation(lm[:, h % 4, c], rows[:, h % 4, c], ACT.Relu,
                                               bias=steps[:, v.b, 2, i, h:h + 1], scale=-1.0)
                ins.then_inc(diff_ready, 1)

        def act_exps(act, v, k):
            for h in (2 * k, 2 * k + 1):
                act.wait_ge(diff_ready, v.at(HG, h))
                nc.scalar.activation(lm[:, h % 4, :], lm[:, h % 4, :], ACT.Exp, scale=-1.0).then_inc(exp_ready, 1)

        def act_scale(act, v, k, first=False):
            if not first:
                act.wait_ge(took["OFF"], v.u * KC + k - 1)
            for h in (2 * k, 2 * k + 1):
                e = h % 2
                nc.scalar.activation(scale[e * HP:(e + 1) * HP, k % 2, :], rows[e * HP:(e + 1) * HP, h % 4, P:],
                                     ACT.Exp).then_inc(scale_ready, 1)

        def act_tap(act, v, i, src):
            j = CONVS[i]
            act.wait_ge(done["H"], v.at(NCONV, i))
            act.wait_ge(par_loaded[v.b], 48 * (v.g + 1))
            if not v.first or i >= 2:
                act.wait_ge(tile_ready, v.u * NCONV + i - 1)
            nc.scalar.activation(cv[:, i % 2, :], src, ACT.Identity,
                                 bias=par[:, v.b, 40 + j:41 + j],
                                 scale=par[:, v.b, 4 * j + 3:4 * j + 4]).then_inc(tap_ready, 1)

        def act_tanh(act, v, i):
            act.wait_ge(took["H"], v.at(NCONV, i))
            nc.scalar.activation(th[:, i % 2, :], cv[:, i % 2, :], ACT.Tanh, scale=0.5).then_inc(th_ready, 1)

        def act_gate(act, v, k, src):
            act.wait_ge(done["G"], v.at(KC, k))
            if not v.first or k:
                act.wait_ge(took["G"], v.u * KC + k)
            nc.scalar.activation(tg[:], src, ACT.Tanh, scale=0.5).then_inc(tg_ready, 1)

        def act_y(act, un, k):
            act.wait_ge(y_ready, un.at(KC, k))
            if not (un.first and k < 2):
                act.wait_ge(op_done, un.u * KC + k - 1)
            nc.scalar.activation(y_hi[:, k % 2, :], ysum[:, k % 2, :], ACT.Copy,
                                 scale=par[:, un.b, 58 + k:59 + k]).then_inc(y_hi_ready, 1)

        def act_sq(act, un, k):
            if k >= 2:
                act.wait_ge(ssq_ready, un.u * (KC - 1) + max(k - 2, 1))
            elif not un.first:
                act.wait_ge(ssq_ready, un.u * (KC - 1))
            nc.scalar.activation(sq[:, k % 2, :], ysum[:, k % 2, :], ACT.Square).then_inc(sq_ready, 1)

        def act_wo(act, un, k):
            act.wait_ge(wo_loaded[k % 2], 16 * (un.u * (KC // 2) + k // 2 + 1))
            if not (un.first and k < 2):
                act.wait_ge(op_done, un.u * KC + k - 1)
            nc.scalar.activation(wo_hi[:, k % 2, :], wo_raw[:, k % 2, :], ACT.Copy).then_inc(wo_hi_ready, 1)

        def act_rms(act, v):
            act.wait_ge(ssq_took, v.at(1, 0))
            nc.scalar.activation(rms[:], meansq[:], ACT.Sqrt).then_inc(rms_ready, 1)

        def act_first(act):
            v = Unit(0, 0, first=True)
            seen = -1
            act.wait_ge(par_loaded[0], 48)
            for kind, i, c, half, src in first_tiles():
                if c > seen:
                    act_w(act, v, c, True)
                    seen = c
                if kind == "H":
                    act_tap(act, v, i, src)
                    act_tanh(act, v, i)
                else:
                    act_gate(act, v, i, src)
            for k in range(2):
                act_diff(act, v, k, True)
                act_exps(act, v, k)
                act_scale(act, v, k, True)

        def act_unit(act, un):
            v = un.ahead(1)
            for k in range(KC):
                before = channel_tile_before(un, k)
                if before:
                    act_tap(act, *before)
                if not un.last:
                    for c in loads_of(k):
                        act_w(act, v, c)
                n, i = (k + 2) // KC, (k + 2) % KC
                more = not (n and un.last)
                if more:
                    act_diff(act, un.ahead(n), i)
                if before:
                    act_tanh(act, *before[:2])
                if k == 0 and not un.first:
                    act_rms(act, un.ahead(-1))
                if more:
                    act_exps(act, un.ahead(n), i)
                    act_scale(act, un.ahead(n), i)
                act_wo(act, un, k)
                act_y(act, un, k)
                if not un.last:
                    if k == BC_SLOT:
                        for j in (0, 1):
                            i = CONVS.index(j)
                            act_tap(act, v, i, bank(("H", 1, i)))
                            act_tanh(act, v, i)
                    act_gate(act, v, k, bank(("G", 1, k)))
                act_sq(act, un, k)

        def dve_state(dve, v, k, src, c):
            if c == 0:
                dve.wait_ge(done["ST"], v.at(KC, k))
                if k >= 2 or not v.first:
                    dve.wait_ge(done["OFF"], v.u * KC + k - 1)
                nc.vector.tensor_copy(state[:, k % 2, 0, :], src[:, 0:P]).then_inc(state_chain, 1)
                return
            dve.wait_ge(state_chain, (v.u * KC + k) * 2 + c)
            for e in range(2):
                h, cols = 2 * k + e, slice(e * HP, (e + 1) * HP)
                ins = nc.vector.scalar_tensor_tensor(
                    state[:, k % 2, c, cols], state[:, k % 2, c - 1, cols], cdecay[:, v.b, c - 1, h:h + 1],
                    src[:, c * P + e * HP:c * P + (e + 1) * HP], ALU.mult, ALU.add)
            ins.then_inc(state_chain if c == 1 else took["ST"], 1)

        def dve_turn(dve, v, k, src):
            dve.wait_ge(done["T"], v.at(KC, k))
            pair = slice(2 * k, 2 * k + 2)
            by_head = src.rearrange("p (c h e) -> p c h e", c=TB, h=2)
            nc.vector.tensor_tensor(hdd[:, k % 2].rearrange("p c (h e) -> p c h e", h=2), by_head[:, 0:TB - 1],
                                    steps[:, v.b, 1, 0:TB - 1, pair].unsqueeze(3).to_broadcast((P, TB - 1, 2, HP)),
                                    ALU.mult)
            nc.vector.tensor_tensor(hdt[:, k % 2].rearrange("p c (h e) -> p c h e", h=2), by_head,
                                    steps[:, v.b, 0, :, pair].unsqueeze(3).to_broadcast((P, TB, 2, HP)),
                                    ALU.mult).then_inc(took["T"], 1)

        def dve_m(dve, v, h):
            dve.wait_ge(exp_ready, v.at(HG, h))
            nc.vector.tensor_tensor(lm[:, h % 4, :], lm[:, h % 4, :], cbt[:, v.b].rearrange("p c i -> p (c i)"),
                                    ALU.mult).then_inc(m_ready, 1)

        def dve_conv(dve, v, i, src, d):
            j = CONVS[i]
            if d == 1:
                dve.wait_ge(tap_ready, v.at(NCONV, i))
            else:
                dve.wait_ge(conv_chain, (v.u * NCONV + i) * 2 + d - 1)
            dst = cv[:, i % 2, d:]
            nc.vector.scalar_tensor_tensor(dst, src[:, 0:SEQ - d], par[:, v.b, 4 * j + 3 - d:4 * j + 4 - d],
                                           dst, ALU.mult, ALU.add).then_inc(conv_chain if d < 3 else took["H"], 1)

        def dve_silu(dve, v, i):
            dve.wait_ge(th_ready, v.at(NCONV, i))
            nc.vector.scalar_tensor_tensor(conv_tile(v, i), th[:, i % 2, :], 1.0, cv[:, i % 2, :], ALU.add,
                                           ALU.mult).then_inc(tile_ready, 1)

        def dve_gate(dve, v, k, src):
            dve.wait_ge(tg_ready, v.at(KC, k))
            if not v.first:
                dve.wait_ge(y_ready, (v.u - 1) * KC + k + 1)
            nc.vector.scalar_tensor_tensor(gate[:, k, :], tg[:], 1.0, src, ALU.add, ALU.mult).then_inc(took["G"], 1)

        def dve_cb(dve, v, src):
            dve.wait_ge(done["CB"], v.at(1, 0))
            nc.vector.tensor_tensor(cbt[:, v.b], src.rearrange("p (c i) -> p c i", c=TB),
                                    mask[:].unsqueeze(1).to_broadcast((P, TB, P)), ALU.mult).then_inc(took["CB"], 1)

        def dve_bt(dve, v, src):
            dve.wait_ge(done["BT"], v.at(1, 0))
            nc.vector.tensor_copy(b_l[:, v.b].rearrange("p c n -> p (c n)"), src[:, 0:3 * P]).then_inc(took["BT"], 1)

        def dve_skip(dve, v):
            dve.wait_ge(par_loaded[v.b], 48 * (v.g + 1))
            nc.vector.tensor_scalar(skip4[:, v.b], par[:, v.b, 50:58], 4.0, None, ALU.mult).then_inc(skip_ready, 1)

        def dve_y_lo(dve, un, k):
            dve.wait_ge(y_hi_ready, un.at(KC, k))
            nc.vector.scalar_tensor_tensor(y_lo[:, k % 2, :], ysum[:, k % 2, :], par[:, un.b, 58 + k:59 + k],
                                           y_hi[:, k % 2, :].bitcast(F32), ALU.mult,
                                           ALU.subtract).then_inc(y_lo_ready, 1)

        def dve_ssq(dve, v, src):
            dve.wait_ge(ssq_done, v.at(1, 0))
            nc.vector.tensor_scalar(meansq[:], src[:, 3 * P:3 * P + TB], 1.0 / CG, 256 * EPS, ALU.mult,
                                    ALU.add).then_inc(ssq_took, 1)

        def dve_out(dve, v):
            dve.wait_ge(rms_ready, v.at(1, 0))
            nc.vector.reciprocal(rrms[:], rms[:]).then_inc(rrms_ready, 1)
            dve.wait_ge(rrms_ready, v.at(1, 0))
            dve.wait_ge(op_done, v.at(KC, KC - 1))
            for t in range(TB):
                nc.vector.scalar_tensor_tensor(acc[:, v.b * TB + t, :], ps_o[:, t, :], rrms[:, t:t + 1],
                                               acc[:, v.b * TB + t, :], ALU.mult, ALU.add).then_inc(op_took, 1)

        def dve_first(dve):
            v = Unit(0, 0, first=True)
            dve.wait_ge(mask_loaded, 16)
            dve_skip(dve, v)
            for kind, i, c, half, src in first_tiles():
                if kind == "H":
                    for d in (1, 2, 3):
                        dve_conv(dve, v, i, src, d)
                    dve_silu(dve, v, i)
                else:
                    dve_gate(dve, v, i, src)
            dve_cb(dve, v, ps[:, 0, :])
            dve_bt(dve, v, ps[:, 1, :])
            dve_turn(dve, v, 0, ps[:, 2, :])
            dve_turn(dve, v, 1, ps[:, 3, :])
            for c in range(TB - 1):
                dve_state(dve, v, 0, ps[:, 0, :], c)
            dve.wait_ge(took["CB"], 1)
            for h in range(2):
                dve_m(dve, v, h)

        def dve_unit(dve, un):
            for k in range(KC):
                v = un.ahead(1)
                after = un.ahead((k + 1) // KC), (k + 1) % KC
                more = k + 1 < KC or not un.last
                before = channel_tile_before(un, k)
                if k == 5 and not un.last:
                    dve_cb(dve, v, bank(("CB", 1, 0)))
                    dve_bt(dve, v, bank(("BT", 1, 0)))
                for c in range(TB - 1):
                    if more:
                        if c < 2:
                            dve_m(dve, after[0], 2 * after[1] + c)
                        dve_state(dve, *after, bank(("ST", (k + 1) // KC, after[1])), c)
                    if before:
                        dve_conv(dve, *before, c + 1)
                dve.wait_ge(done["DIAG"], un.at(KC, k))
                if not (un.first and k < 2):
                    dve.wait_ge(sq_ready, un.u * KC + k - 1)
                    dve.wait_ge(y_lo_ready, un.u * KC + k - 1)
                dve.wait_ge(skip_ready, un.at(1, 0))
                nc.vector.scalar_tensor_tensor(ysum[:, k % 2, :], hid[:, k, :], skip4[:, un.b, k:k + 1],
                                               bank(("DIAG", 0, k)), ALU.mult, ALU.add).then_inc(took["DIAG"], 1)
                dve.wait_ge(done["OFF"], un.at(KC, k))
                dve.wait_ge(scale_ready, un.at(HG, 2 * k + 1))
                if k == 0 and not un.first:
                    dve_ssq(dve, un.ahead(-1), bank(("OFF", 0, 0)))
                nc.vector.tensor_tensor(yoff[:, k % 2, :], bank(("OFF", 0, k))[:, 0:3 * P], scale[:, k % 2, :],
                                        ALU.mult).then_inc(took["OFF"], 1)
                if before:
                    dve_silu(dve, *before[:2])
                if k == 0 and not un.first:
                    dve_out(dve, un.ahead(-1))
                n, i = (k + 2) // KC, (k + 2) % KC
                if not (n and un.last):
                    dve_turn(dve, un.ahead(n), i, bank(("T", n, i)))
                if not un.last:
                    if k == BC_SLOT:
                        for j in (0, 1):
                            i = CONVS.index(j)
                            for d in (1, 2, 3):
                                dve_conv(dve, v, i, bank(("H", 1, i)), d)
                            dve_silu(dve, v, i)
                    if k == 3:
                        dve_skip(dve, v)
                    dve_gate(dve, v, k, bank(("G", 1, k)))
                dve_y_lo(dve, un, k)

        def dve_last(dve):
            v = Unit(GROUPS - 1, 1)
            dve_ssq(dve, v, ps[:, 0, :])
            dve_out(dve, v)

        def pool_w(pool, v, c):
            slot, _ = load_slot(v, c)
            pool.wait_ge(w_hi_ready, v.at(NLOAD, c))
            nc.gpsimd.tensor_tensor(w_lo[:, slot, :], w_raw[:, slot, :], w_hi[:, slot, :].bitcast(F32),
                                    ALU.subtract).then_inc(w_lo_ready, 1)

        def pool_sum(pool, un, k):
            pool.wait_ge(sq_ready, un.at(KC, k))
            if k > 1:
                pool.wait_ge(ssq_ready, un.u * (KC - 1) + k - 1)
            elif not un.first:
                pool.wait_ge(ssq_done, un.u)
            nc.gpsimd.tensor_tensor(ssq[:], sq[:, 0, :] if k == 1 else ssq[:], sq[:, k % 2, :],
                                    ALU.add).then_inc(ssq_ready, 1)

        def pool_first(pool):
            for c in range(NLOAD):
                pool_w(pool, Unit(0, 0), c)

        def pool_unit(pool, un):
            v = un.ahead(1)
            for k in range(KC):
                if k > 1:
                    pool_sum(pool, un, k - 1)
                elif k == 0 and not un.first:
                    pool_sum(pool, un.ahead(-1), KC - 1)
                if not un.last:
                    for c in loads_of(k):
                        pool_w(pool, v, c)
                pool.wait_ge(took["OFF"], un.at(KC, k))
                nc.gpsimd.tensor_tensor(ysum[:, k % 2, P:], ysum[:, k % 2, P:], yoff[:, k % 2, :],
                                        ALU.add).then_inc(pool_chain, 1)
                pool.wait_ge(pool_chain, un.at(KC, k))
                nc.gpsimd.tensor_tensor(ysum[:, k % 2, :], ysum[:, k % 2, :], gate[:, k, :],
                                        ALU.mult).then_inc(y_ready, 1)
                pool.wait_ge(wo_hi_ready, un.at(KC, k))
                nc.gpsimd.tensor_tensor(wo_lo[:, k % 2, :], wo_raw[:, k % 2, :], wo_hi[:, k % 2, :].bitcast(F32),
                                        ALU.subtract).then_inc(wo_lo_ready, 1)
            if un.last:
                pool_sum(pool, un, KC - 1)

        def schedule(eng, first, unit, last):
            first(eng)
            unit(eng, Unit(0, 0, first=True))
            with eng.Fori(0, GROUPS - 1) as g:
                unit(eng, Unit(g, 1))
                unit(eng, Unit(g + 1, 0))
            unit(eng, Unit(GROUPS - 1, 1, last=True))
            if last:
                last(eng)

        with nc.Block() as block:
            @block.sync
            def _(sp):
                schedule(sp, sp_first, sp_unit, None)

            @block.tensor
            def _(pe):
                schedule(pe, pe_first, pe_unit, pe_last)

            @block.scalar
            def _(act):
                schedule(act, act_first, act_unit, lambda e: act_rms(e, Unit(GROUPS - 1, 1)))

            @block.vector
            def _(dve):
                schedule(dve, dve_first, dve_unit, dve_last)

            @block.gpsimd
            def _(pool):
                schedule(pool, pool_first, pool_unit, None)

        x1_back = sem("s_x1_back")
        g_back = sem("s_g_back")
        product_ready = sem("s_product_ready")
        out_ready = sem("s_out_ready")
        out_stored = sem("s_out_stored")
        with nc.Block() as block:
            @block.sync
            def _(sp):
                sp.dma_start(hid[:], x1_dram).then_inc(x1_back, 16)
                sp.dma_start(gate[:], g_dram).then_inc(g_back, 16)
                for t in range(NT):
                    sp.wait_ge(out_ready, t + 1)
                    sp.dma_start(out[:, t, :], acc[:, t, :]).then_inc(out_stored, 16)
                sp.wait_ge(out_stored, 16 * NT)

            @block.vector
            def _(dve):
                dve.wait_ge(x1_back, 16)
                dve.wait_ge(g_back, 16)
                for t in range(NT):
                    nc.vector.tensor_tensor(acc[:, t, :], acc[:, t, :], gate[:, t, :], ALU.mult).then_inc(product_ready, 1)
                for t in range(NT):
                    dve.wait_ge(product_ready, t + 1)
                    nc.vector.tensor_tensor(acc[:, t, :], acc[:, t, :], hid[:, t, :], ALU.add).then_inc(out_ready, 1)


def program(nc, a, out):
    with ExitStack() as ctx:
        def sb(name, shape, dt=F32):
            return ctx.enter_context(nc.sbuf_tensor(name, shape, dt))

        def dram(name, shape):
            return nc.dram_tensor(name, shape, F32, kind="Internal").ap()

        xs = sb("xs", [P, NT, D])
        ident = sb("ident", [P, P])
        table = dram("table", [T, 2 * D])
        x1_dram = dram("x1_dram", [P, NT, D])
        g_dram = dram("g_dram", [P, NT, D])
        acs_dram = dram("acs_dram", [HEADS, T])
        group_dram = dram("group_dram", [P, GROUPS, GROUP_N])
        layer0(nc, a, xs, ident, x1_dram, table)
        ones = sb("ones", [P, P])
        h_hi = sb("h_hi", [P, KD, T], F32R)
        h_lo = sb("h_lo", [P, KD, T], F32R)
        with nc.sbuf_tensor("xnT1", [P, KD, T], F32) as xnT:
            mixer_inputs(nc, a, xs, ident, ones, h_hi, h_lo, xnT, group_dram, acs_dram)
            layer1_ffn(nc, a, xnT, g_dram)
        mixer(nc, a, xs, ident, ones, h_hi, h_lo, group_dram, acs_dram, x1_dram, g_dram,
              out.rearrange("(t p) d -> p t d", p=P))


def shape_tables(np):
    t = np.arange(D)
    f = np.arange(D // 2)
    ang = 2 * np.pi * ((t[:, None] * f[None, :]) % D) / D
    cos, sin = np.cos(ang), np.sin(ang)
    sin[:, 0] = np.cos(np.pi * t)
    dft = np.concatenate([cos, sin], 1)
    weight = np.full(D // 2, 2.0 / D)
    weight[0] = 1.0 / D
    tau = np.minimum(t, D - t)
    ci = np.cos(2 * np.pi * ((f[:, None] * tau[None, :]) % D) / D) * weight[:, None]
    si = ci.copy()
    si[0] = np.cos(np.pi * tau) / D
    idft = np.concatenate([ci, si], 0)

    def lay(m):
        return np.ascontiguousarray(m.reshape(KD, P, -1).transpose(1, 0, 2)).astype(np.float32)
    row = np.arange(T).reshape(NT, P).T[:, :, None] * (2 * D)
    return {"ident": np.eye(P, dtype=np.float32), "mask": np.triu(np.ones((P, P), np.float32)), "dft": lay(dft), "idft": lay(idft),
            "rowbase": np.broadcast_to(row, (P, NT, 8)).astype(np.uint32)}


def kernel(**inputs):
    import numpy as np
    import concourse.bacc as bacc
    from concourse.bass_utils import run_bass_kernel_spmd

    def c(v):
        return np.ascontiguousarray(v)

    i = {k: np.asarray(v) for k, v in inputs.items()}
    arrays = {
        "x": c(i["L0_attn_x"].reshape(T, D)),
        "gate_w": c(i["L0_ffn_gate_w"]), "up_w": c(i["L0_ffn_up_w"]), "down_w": c(i["L0_ffn_down_w"]),
        "fc1_w": c(i["L0_ffn_fc1_w"]), "fc2_w": c(i["L0_ffn_fc2_w"]), "expert_w": c(i["L0_ffn_expert_w"]),
        "gamma": c(i["L0_ffn_ln_gamma"].reshape(1, D)), "beta": c(i["L0_ffn_ln_beta"].reshape(1, D)),
    }
    w_in = i["L1_attn_in_proj_w"].reshape(-1, P, D)
    order = [t for g in range(GROUPS)
             for kind, k in LOADS
             for t in ((GROUPS * KC + g * KC + k, g * KC + k) if kind == "HG"
                       else (2 * GROUPS * KC + g, (2 * KC + 1) * GROUPS + g))]
    tiles = w_in[order].reshape(-1, 2, P, KD, P)
    arrays["w_in"] = c(tiles.transpose(0, 4, 1, 3, 2).reshape(-1, P, 2 * KD * P))
    arrays["w_dt"] = c(w_in[-1].reshape(P, KD, P).transpose(2, 1, 0))
    arrays["w_out"] = c(i["L1_attn_out_proj_w"].reshape(D, GROUPS, KC, P).transpose(1, 2, 3, 0).reshape(
        GROUPS * KC, P, D))
    arrays["norm_w"] = c(i["L1_attn_norm_w"].reshape(KD, P).T)
    arrays["dt_bias"] = c(i["L1_attn_dt_bias"].reshape(P, 1))
    arrays["a_log"] = c(i["L1_attn_A_log"].reshape(P, 1))
    cw, cb = i["L1_attn_conv_w"].reshape(-1, P, CONV), i["L1_attn_conv_b"].reshape(-1, P)
    skip = np.repeat(i["L1_attn_Dp"], HP).reshape(GROUPS, KC, P)
    gn = i["L1_attn_gnorm_w"].reshape(GROUPS, KC, P)
    par = []
    for g in range(GROUPS):
        own = [GROUPS * KC + g, GROUPS * KC + GROUPS + g] + [g * KC + k for k in range(KC)]
        par.append(np.concatenate([cw[own].transpose(1, 0, 2).reshape(P, -1), cb[own].T, skip[g].T, gn[g].T], 1))
    arrays["par"] = c(np.stack(par, 1))

    def blocks(m):
        return m.T.reshape(-1, P, m.shape[0]).transpose(1, 0, 2).reshape(P, -1)
    names = ("gate", "up", "down")
    arrays["q"] = c(np.concatenate([blocks(i[f"L1_ffn_{n}_q"]) for n in names], 1).reshape(P, NQ, QC).transpose(1, 0, 2))
    arrays["s"] = c(np.concatenate([i[f"L1_ffn_{n}_s"].T.reshape(-1) for n in names]).reshape(NQ, QC))
    arrays.update(shape_tables(np))
    nc = bacc.Bacc("TRN2", target_bir_lowering=False, num_devices=1)
    a = {k: nc.dram_tensor(f"in_{k}", v.shape, mybir.dt.from_np(v.dtype), kind="ExternalInput").ap()
         for k, v in arrays.items()}
    out = nc.dram_tensor("out", (T, D), F32, kind="ExternalOutput").ap()
    program(nc, a, out)
    r = run_bass_kernel_spmd(nc, [{f"in_{k}": v for k, v in arrays.items()}], core_ids=[0])
    return r.results[0]["out"].reshape(NB, SEQ, D)
```

```python
from contextlib import ExitStack

import concourse.bass as bass
from concourse import mybir

F32 = mybir.dt.float32
U32 = mybir.dt.uint32
I32 = mybir.dt.int32
F32R = mybir.dt.float32r
ALU = mybir.AluOpType
ACT = mybir.ActivationFunctionType

P = 128
T = 1024
NT = T // P
D = 512
KD = D // P
NB = 2
SEQ = T // NB
TB = SEQ // P
TOPK = 6
EPS = 1e-5
UP = 1024
KU = UP // P
LAT = 256
KL = LAT // P
NE = 8
HEADS = 128
HP = 64
GROUPS = 8
NST = 128
HG = HEADS // GROUPS
CG = HG * HP
KC = CG // P
DI = HEADS * HP
CONV = 4
INT = 1792
KI = INT // P
GU = 2 * KD * P
TURN_STEP = 6
GROUP_N = 3 * NT * HG + 4 * HG


class Sems:

    def __init__(self, nc, ctx):
        self.nc, self.ctx = nc, ctx

    def __call__(self, name):
        return self.ctx.enter_context(self.nc.semaphore(name))


def chain_on(eng, sem):
    n = [0]

    def link(ins):
        n[0] += 1
        ins.then_inc(sem, 1)
        eng.wait_ge(sem, n[0])
    return link


def three_passes(nc, dst, l_hi, l_lo, r_hi, r_lo, start, stop):
    nc.tensor.matmul(dst, l_hi, r_hi, start=start, stop=False)
    nc.tensor.matmul(dst, l_hi, r_lo, start=False, stop=False)
    return nc.tensor.matmul(dst, l_lo, r_hi, start=False, stop=stop)


def layer0(nc, a, x1, x1_mv, ident, x1_dram, x1_stored, table):
    with ExitStack() as ctx:
        sem = Sems(nc, ctx)

        def sb(name, shape, dt=F32):
            return ctx.enter_context(nc.sbuf_tensor(name, shape, dt))

        xn = sb("xn", [P, NT, D])
        xnT_hi, xnT_lo = sb("xnT_hi", [P, KD, T], F32R), sb("xnT_lo", [P, KD, T], F32R)
        dft_hi, dft_lo = sb("dft_hi", [P, KD, D], F32R), sb("dft_lo", [P, KD, D], F32R)
        upw_hi, upw_lo = sb("upw_hi", [P, KD, UP], F32R), sb("upw_lo", [P, KD, UP], F32R)
        fc1w_hi, fc1w_lo = sb("fc1w_hi", [P, KD, LAT], F32R), sb("fc1w_lo", [P, KD, LAT], F32R)
        gatew_hi, gatew_lo = sb("gatew_hi", [P, KD, NE], F32R), sb("gatew_lo", [P, KD, NE], F32R)
        idft = sb("idft", [P, KD, D])
        downw = sb("downw", [P, KU, D])
        expw = sb("expw", [P, KL, LAT])
        fc2w = sb("fc2w", [P, KL, D])
        gatew = sb("gatew", [P, KD, NE])
        gamma = sb("gamma", [P, D])
        beta = sb("beta", [P, D])
        rowbase = sb("rowbase", [P, NT, 8], U32)
        power = sb("power", [P, KD, SEQ])
        hid = xn
        latT = sb("latT", [P, KL, SEQ])
        exoT = sb("exoT", [P, KL, SEQ])
        shifted = sb("shifted", [P, 2, TOPK, D])
        mixed = sb("mixed", [P, TB, D])
        routed = latT
        z = power
        raw = shifted[:].rearrange("p i j d -> p (i j d)")
        dft = raw[:, 0:KD * D].rearrange("p (k n) -> p k n", k=KD)
        upw = raw[:, KD * D:].rearrange("p (k n) -> p k n", k=KD)
        fc1w = mixed[:, 0:KD * LAT // D, :].rearrange("p a d -> p (a d)").rearrange("p (k n) -> p k n", k=KD)
        stats = sb("stats", [P, NT, 6])
        mv = sb("mv", [P, NT, 2])
        std = sb("std", [P, NT])
        rstd = sb("rstd", [P, NT])
        zstats = sb("zstats", [P, NT, 6])
        zmv = sb("zmv", [P, NT, 2])
        zstd = sb("zstd", [P, NT])
        zrstd = sb("zrstd", [P, NT])
        top = sb("top", [P, NT, 8])
        delay = sb("delay", [P, NT, 8], U32)
        at = sb("at", [P, NT, 8], U32)
        negmax = sb("negmax", [P, NT])
        wexp = sb("wexp", [P, NT, 8])
        wsum = sb("wsum", [P, NT])
        wrec = sb("wrec", [P, NT])
        topl = sb("topl", [P, NT, 8])
        rsum = sb("rsum", [P, NT])
        ps_a = ctx.enter_context(nc.psum_tensor("ps_a", [P, 4, 512], F32))
        ps_d = ctx.enter_context(nc.psum_tensor("ps_d", [P, 4, 512], F32))

        x_loaded = [sem(f"x_loaded{t}") for t in range(NT)]
        ident_loaded = sem("ident_loaded")
        xn_lo_ready = sem("xn_lo_ready")
        dft_split = sem("dft_split")
        up_hi_ready = sem("up_hi_ready")
        up_lo_ready = sem("up_lo_ready")
        dft_loaded = sem("dft_loaded")
        idft_down_loaded = sem("idft_down_loaded")
        up_loaded = sem("up_loaded")
        small_loaded = sem("small_loaded")
        rows_loaded = sem("rows_loaded")
        dve_chain = sem("dve_chain")
        var_ready = sem("var_ready")
        std_ready = sem("std_ready")
        xn_ready = sem("xn_ready")
        table_stored = sem("table_stored")
        pe_a = sem("pe_a")
        act_took = sem("act_took")
        pe_d = sem("pe_d")
        dve_took = sem("dve_took")
        squared = sem("squared")
        topk_ready = sem("topk_ready")
        weights_ready = sem("weights_ready")
        gathered = [sem(f"gathered{i}") for i in range(2)]
        mixed_ready = sem("mixed_ready")
        z_ready = sem("z_ready")
        zvar_ready = sem("zvar_ready")
        zstd_ready = sem("zstd_ready")
        affine_ready = sem("affine_ready")
        silu_ready = sem("silu_ready")
        x1_ready = sem("x1_ready")

        A_N, D_N = 2 * KD + KU + 2 * KL, 3 * TB

        def a_dft(n, m): return NT + A_N * n + m
        def a_up(n, m): return NT + A_N * n + KD + m
        def a_lat(n, m): return NT + A_N * n + KD + KU + m
        def a_exo(n, m): return NT + A_N * n + KD + KU + KL + m
        def a_rout(n, t): return NT + A_N * n + KD + KU + 2 * KL + t
        def d_corr(n, t): return D_N * n + t
        def d_log(n, t): return D_N * n + TB + t
        def d_shared(n, t): return D_N * n + 2 * TB + t

        block = ctx.enter_context(nc.Block())

        @block.sync
        def _(sp):
            x_view = a["x"].rearrange("(t p) d -> p t d", p=P)
            for t in range(NT):
                sp.dma_start(x1[:, t, :], x_view[:, t, :]).then_inc(x_loaded[t], 16)
            sp.dma_start(ident[:], a["ident"]).then_inc(ident_loaded, 16)
            sp.dma_start(dft, a["dft"]).then_inc(dft_loaded, 16)
            sp.dma_start(upw, a["up_w"].rearrange("(k p) n -> p k n", p=P)).then_inc(up_loaded, 16)
            sp.dma_start(idft[:], a["idft"]).then_inc(idft_down_loaded, 16)
            sp.dma_start(rowbase[:], a["rowbase"]).then_inc(rows_loaded, 16)
            sp.dma_start(gamma[:], a["gamma"].to_broadcast((P, D))).then_inc(rows_loaded, 16)
            sp.dma_start(beta[:], a["beta"].to_broadcast((P, D))).then_inc(rows_loaded, 16)
            sp.dma_start(fc1w, a["fc1_w"].rearrange("(k p) n -> p k n", p=P)).then_inc(small_loaded, 16)
            sp.dma_start(expw[:], a["expert_w"].rearrange("(k p) n -> p k n", p=P)).then_inc(small_loaded, 16)
            sp.dma_start(fc2w[:], a["fc2_w"].rearrange("(k p) n -> p k n", p=P)).then_inc(small_loaded, 16)
            sp.dma_start(gatew[:], a["gate_w"].rearrange("(k p) n -> p k n", p=P)).then_inc(small_loaded, 16)
            sp.dma_start(downw[:], a["down_w"].rearrange("(k p) n -> p k n", p=P)).then_inc(idft_down_loaded, 16)
            for t in range(NT):
                sp.wait_ge(xn_ready, t + 1)
                for half in range(2):
                    sp.dma_start(table[t * P:(t + 1) * P, half * D:(half + 1) * D],
                                 xn[:, t, :]).then_inc(table_stored, 16)
            for t in range(NT):
                sp.wait_ge(x1_ready, t + 1)
                sp.dma_start(x1_dram[:, t, :], x1[:, t, :]).then_inc(x1_stored, 16)
            sp.wait_ge(table_stored, 32 * NT)

        @block.tensor
        def _(pe):
            def turn(eng_sem, i, base=4):
                if i >= base:
                    pe.wait_ge(eng_sem, i - base + 1)

            pe.wait_ge(ident_loaded, 16)
            for t in range(NT):
                pe.wait_ge(xn_ready, t + 1)
                turn(act_took, t)
                turn(xn_lo_ready, t)
                for k in range(KD):
                    mm = nc.tensor.transpose(ps_a[:, t % 4, k * P:(k + 1) * P],
                                             xn[:, t, k * P:(k + 1) * P], ident[:])
                mm.then_inc(pe_a, 1)
            pe.wait_ge(dft_split, 2)
            pe.wait_ge(xn_lo_ready, NT)
            for n in range(NB):
                cols = slice(n * SEQ, (n + 1) * SEQ)
                pe.wait_ge(act_took, (n + 1) * TB)
                for m in range(KD):
                    i = a_dft(n, m)
                    turn(act_took, i)
                    for k in range(KD):
                        at = slice(m * P, (m + 1) * P)
                        mm = three_passes(nc, ps_a[:, i % 4, :], dft_hi[:, k, at], dft_lo[:, k, at],
                                          xnT_hi[:, k, cols], xnT_lo[:, k, cols], k == 0, k == KD - 1)
                    mm.then_inc(pe_a, 1)
                pe.wait_ge(up_lo_ready, KD)
                for m in range(KU):
                    i = a_up(n, m)
                    turn(act_took, i)
                    for k in range(KD):
                        at = slice(m * P, (m + 1) * P)
                        mm = three_passes(nc, ps_a[:, i % 4, :], upw_hi[:, k, at], upw_lo[:, k, at],
                                          xnT_hi[:, k, cols], xnT_lo[:, k, cols], k == 0, k == KD - 1)
                    mm.then_inc(pe_a, 1)
                pe.wait_ge(idft_down_loaded, 32)
                for t in range(TB):
                    i = d_corr(n, t)
                    turn(dve_took, i)
                    for k in range(KD):
                        mm = nc.tensor.matmul(ps_d[:, i % 4, :], power[:, k, t * P:(t + 1) * P],
                                              idft[:, k, :], start=(k == 0), stop=(k == KD - 1))
                    mm.then_inc(pe_d, 1)
                pe.wait_ge(dft_split, 4)
                for m in range(KL):
                    i = a_lat(n, m)
                    turn(act_took, i)
                    for k in range(KD):
                        at = slice(m * P, (m + 1) * P)
                        mm = three_passes(nc, ps_a[:, i % 4, :], fc1w_hi[:, k, at], fc1w_lo[:, k, at],
                                          xnT_hi[:, k, cols], xnT_lo[:, k, cols], k == 0, k == KD - 1)
                    mm.then_inc(pe_a, 1)
                for t in range(TB):
                    i = d_log(n, t)
                    turn(dve_took, i)
                    for k in range(KD):
                        at = slice(n * SEQ + t * P, n * SEQ + (t + 1) * P)
                        mm = three_passes(nc, ps_d[:, i % 4, 0:NE], xnT_hi[:, k, at], xnT_lo[:, k, at],
                                          gatew_hi[:, k, :], gatew_lo[:, k, :], k == 0, k == KD - 1)
                    mm.then_inc(pe_d, 1)
                pe.wait_ge(act_took, a_lat(n, KL - 1) + 1)
                for m in range(KL):
                    i = a_exo(n, m)
                    for k in range(KL):
                        mm = nc.tensor.matmul(ps_a[:, i % 4, :], expw[:, k, m * P:(m + 1) * P],
                                              latT[:, k, :], start=(k == 0), stop=(k == KL - 1))
                    mm.then_inc(pe_a, 1)
                pe.wait_ge(squared, (n + 1) * KU)
                for t in range(TB):
                    i = d_shared(n, t)
                    turn(dve_took, i)
                    for k in range(KU):
                        mm = nc.tensor.matmul(ps_d[:, i % 4, :], hid[:, k, t * P:(t + 1) * P],
                                              downw[:, k, :], start=(k == 0), stop=(k == KU - 1))
                    mm.then_inc(pe_d, 1)
                    j = a_rout(n, t)
                    pe.wait_ge(act_took, max(a_exo(n, KL - 1) + 1, j - 3))
                    for k in range(KL):
                        mm = nc.tensor.matmul(ps_a[:, j % 4, :], exoT[:, k, t * P:(t + 1) * P],
                                              fc2w[:, k, :], start=(k == 0), stop=(k == KL - 1))
                    mm.then_inc(pe_a, 1)

        def up_hi(act, k):
            nc.scalar.activation(upw_hi[:, k, :], upw[:, k, :], ACT.Copy).then_inc(up_hi_ready, 1)

        @block.scalar
        def _(act):
            act.wait_ge(var_ready, NT)
            nc.scalar.activation(std[:], mv[:, :, 1], ACT.Sqrt).then_inc(std_ready, 1)
            act.wait_ge(dft_loaded, 16)
            nc.scalar.activation(dft_hi[:], dft, ACT.Copy).then_inc(dft_split, 1)
            for t in range(NT):
                act.wait_ge(pe_a, t + 1)
                nc.scalar.activation(xnT_hi[:, :, t * P:(t + 1) * P],
                                     ps_a[:, t % 4, :].rearrange("p (k c) -> p k c", k=KD),
                                     ACT.Copy).then_inc(act_took, 1)
            act.wait_ge(up_loaded, 16)
            for k in range(2):
                up_hi(act, k)
            for n in range(NB):
                for m in range(KD):
                    i = a_dft(n, m)
                    act.wait_ge(pe_a, i + 1)
                    if n:
                        act.wait_ge(x1_ready, (n - 1) * TB + m + 1)
                    nc.scalar.activation(power[:, m, :], ps_a[:, i % 4, :], ACT.Square).then_inc(act_took, 1)
                    if n == 0 and m + 2 < KD:
                        up_hi(act, m + 2)
                if n == 0:
                    act.wait_ge(small_loaded, 64)
                    nc.scalar.activation(fc1w_hi[:], fc1w, ACT.Copy).then_inc(up_hi_ready, 1)
                    nc.scalar.activation(gatew_hi[:], gatew[:], ACT.Copy).then_inc(up_hi_ready, 1)
                    act.wait_ge(table_stored, 32 * NT)
                for m in range(KU):
                    i = a_up(n, m)
                    act.wait_ge(pe_a, i + 1)
                    if n:
                        act.wait_ge(pe_d, d_shared(n - 1, TB - 1) + 1)
                    nc.scalar.activation(hid[:, m, :], ps_a[:, i % 4, :], ACT.Relu).then_inc(act_took, 1)
                for m in range(KL):
                    i = a_lat(n, m)
                    act.wait_ge(pe_a, i + 1)
                    nc.scalar.activation(latT[:, m, :], ps_a[:, i % 4, :], ACT.Copy).then_inc(act_took, 1)
                for m in range(KL):
                    i = a_exo(n, m)
                    act.wait_ge(pe_a, i + 1)
                    nc.scalar.activation(exoT[:, m, :], ps_a[:, i % 4, :], ACT.Copy).then_inc(act_took, 1)
                for t in range(TB):
                    g = n * TB + t
                    act.wait_ge(topk_ready, g + 1)
                    nc.scalar.activation(wexp[:, g, 0:TOPK], top[:, g, 0:TOPK], ACT.Exp, bias=negmax[:, g:g + 1],
                                         accum_out=wsum[:, g:g + 1]).then_inc(weights_ready, 1)
                for t in range(TB + 2):
                    g = n * TB + t
                    if t < TB:
                        i = a_rout(n, t)
                        act.wait_ge(pe_a, i + 1)
                        act.wait_ge(dve_took, d_log(n, TB - 1) + 1)
                        if t >= 2:
                            act.wait_ge(z_ready, g - 1)
                        nc.scalar.activation(routed[:, t % 2, :], ps_a[:, i % 4, :], ACT.Copy,
                                             scale=rsum[:, g:g + 1]).then_inc(act_took, 1)
                    if t >= 2:
                        act.wait_ge(affine_ready, g - 1)
                        nc.scalar.activation(z[:, t - 2, :], z[:, t - 2, :], ACT.Silu).then_inc(silu_ready, 1)
                    if 1 <= t <= TB:
                        act.wait_ge(zvar_ready, g)
                        nc.scalar.activation(zstd[:, g - 1:g], zmv[:, g - 1, 1:2], ACT.Sqrt).then_inc(zstd_ready, 1)

        @block.vector
        def _(dve):
            link = chain_on(dve, dve_chain)

            def xn_rest(t):
                c = slice(t * P, (t + 1) * P)
                dve.wait_ge(act_took, t + 1)
                nc.vector.tensor_tensor(xnT_lo[:, :, c], ps_a[:, t % 4, :].rearrange("p (k c) -> p k c", k=KD),
                                        xnT_hi[:, :, c].bitcast(F32), ALU.subtract).then_inc(xn_lo_ready, 1)
            for t in range(NT):
                dve.wait_ge(x_loaded[t], 16)
                link(nc.vector.bn_stats(stats[:, t, :], x1[:, t, :]))
                link(nc.vector.bn_aggr(mv[:, t, :], stats[:, t, :]))
                nc.vector.tensor_scalar(mv[:, t, 1:2], mv[:, t, 1:2], EPS, None, ALU.add).then_inc(var_ready, 1)
            dve.wait_ge(std_ready, 1)
            link(nc.vector.reciprocal(rstd[:], std[:]))
            for t in range(NT):
                nc.vector.tensor_scalar(xn[:, t, :], x1[:, t, :], mv[:, t, 0:1], rstd[:, t:t + 1],
                                        ALU.subtract, ALU.mult).then_inc(xn_ready, 1)
                if t >= 2:
                    xn_rest(t - 2)
            for t in (NT - 2, NT - 1):
                xn_rest(t)
            for k in range(KD):
                dve.wait_ge(up_hi_ready, k + 1)
                nc.vector.tensor_tensor(upw_lo[:, k, :], upw[:, k, :], upw_hi[:, k, :].bitcast(F32),
                                        ALU.subtract).then_inc(up_lo_ready, 1)
            dve.wait_ge(rows_loaded, 48)
            for n in range(NB):
                for t in range(TB):
                    g, i = n * TB + t, d_corr(n, t)
                    dve.wait_ge(pe_d, i + 1)
                    link(nc.vector.max(top[:, g, :], ps_d[:, i % 4, :]))
                    nc.vector.max_index(delay[:, g, :], top[:, g, :], ps_d[:, i % 4, :]).then_inc(dve_took, 1)
                    dve.wait_ge(dve_took, i + 1)
                    link(nc.vector.tensor_tensor(at[:, g, :], delay[:, g, :], rowbase[:, g, :], ALU.add))
                    nc.vector.tensor_scalar(negmax[:, g:g + 1], top[:, g, 0:1], -1.0, None,
                                            ALU.mult).then_inc(topk_ready, 1)
                for t in range(TB):
                    g, i = n * TB + t, d_log(n, t)
                    dve.wait_ge(pe_d, i + 1)
                    link(nc.vector.max(topl[:, g, :], ps_d[:, i % 4, 0:NE]))
                    nc.vector.tensor_tensor(rsum[:, g:g + 1], topl[:, g, 0:1], topl[:, g, 1:2],
                                            ALU.add).then_inc(dve_took, 1)
                for t in range(TB):
                    g = n * TB + t
                    dve.wait_ge(weights_ready, g + 1)
                    link(nc.vector.reciprocal(wrec[:, g:g + 1], wsum[:, g:g + 1]))
                    link(nc.vector.tensor_scalar(wexp[:, g, 0:TOPK], wexp[:, g, 0:TOPK], wrec[:, g:g + 1], None,
                                                 ALU.mult))
                    dve.wait_ge(gathered[g % 2], 16 * TOPK * (g // 2 + 1))
                    link(nc.vector.tensor_scalar(mixed[:, t, :], shifted[:, g % 2, 0, :], wexp[:, g, 0:1], None, ALU.mult))
                    for j in range(1, TOPK):
                        add = nc.vector.scalar_tensor_tensor(mixed[:, t, :], shifted[:, g % 2, j, :], wexp[:, g, j:j + 1],
                                                             mixed[:, t, :], ALU.mult, ALU.add)
                        if j < TOPK - 1:
                            link(add)
                    add.then_inc(mixed_ready, 1)
                for t in range(TB + 2):
                    g = n * TB + t
                    if t < TB:
                        i = d_shared(n, t)
                        dve.wait_ge(pe_d, i + 1)
                        dve.wait_ge(act_took, a_rout(n, t) + 1)
                        nc.vector.tensor_tensor(z[:, t, :], ps_d[:, i % 4, :], routed[:, t % 2, :],
                                                ALU.add).then_inc(z_ready, 1)
                        dve.wait_ge(z_ready, g + 1)
                        nc.vector.bn_stats(zstats[:, g, :], z[:, t, :]).then_inc(dve_took, 1)
                        dve.wait_ge(dve_took, i + 1)
                        link(nc.vector.bn_aggr(zmv[:, g, :], zstats[:, g, :]))
                        nc.vector.tensor_scalar(zmv[:, g, 1:2], zmv[:, g, 1:2], EPS, None,
                                                ALU.add).then_inc(zvar_ready, 1)
                    if 1 <= t <= TB:
                        u = g - 1
                        dve.wait_ge(zstd_ready, u + 1)
                        link(nc.vector.reciprocal(zrstd[:, u:u + 1], zstd[:, u:u + 1]))
                        link(nc.vector.scalar_tensor_tensor(z[:, t - 1, :], z[:, t - 1, :], zmv[:, u, 0:1], gamma[:],
                                                            ALU.subtract, ALU.mult))
                        nc.vector.scalar_tensor_tensor(z[:, t - 1, :], z[:, t - 1, :], zrstd[:, u:u + 1], beta[:],
                                                       ALU.mult, ALU.add).then_inc(affine_ready, 1)
                    if t >= 2:
                        u = g - 2
                        dve.wait_ge(silu_ready, u + 1)
                        dve.wait_ge(mixed_ready, u + 1)
                        link(nc.vector.tensor_tensor(mixed[:, t - 2, :], mixed[:, t - 2, :], z[:, t - 2, :], ALU.mult))
                        nc.vector.tensor_tensor(x1[:, u, :], x1[:, u, :], mixed[:, t - 2, :],
                                                ALU.add).then_inc(x1_ready, 1)
                        dve.wait_ge(x1_ready, u + 1)
                        link(nc.vector.bn_stats(stats[:, u, :], x1[:, u, :]))
                        link(nc.vector.bn_aggr(x1_mv[:, u, :], stats[:, u, :]))

        @block.gpsimd
        def _(pool):
            pool.wait_ge(dft_split, 1)
            nc.gpsimd.tensor_tensor(dft_lo[:], dft, dft_hi[:].bitcast(F32), ALU.subtract).then_inc(dft_split, 1)
            pool.wait_ge(up_hi_ready, KD + 1)
            nc.gpsimd.tensor_tensor(fc1w_lo[:], fc1w, fc1w_hi[:].bitcast(F32), ALU.subtract).then_inc(dft_split, 1)
            pool.wait_ge(up_hi_ready, KD + 2)
            nc.gpsimd.tensor_tensor(gatew_lo[:], gatew[:], gatew_hi[:].bitcast(F32),
                                    ALU.subtract).then_inc(dft_split, 1)
            for n in range(NB):
                for m in range(KU):
                    pool.wait_ge(act_took, a_up(n, m) + 1)
                    nc.gpsimd.tensor_tensor(hid[:, m, :], hid[:, m, :], hid[:, m, :], ALU.mult).then_inc(squared, 1)
                for t in range(TB):
                    g = n * TB + t
                    pool.wait_ge(table_stored, 32 * NT)
                    pool.wait_ge(topk_ready, g + 1)
                    if g >= 2:
                        pool.wait_ge(mixed_ready, g - 1)
                    for j in range(TOPK):
                        nc.gpsimd.indirect_dma_start(
                            shifted[:, g % 2, j, :], None, table.rearrange("r (c o) -> (r c) o", o=1),
                            bass.IndirectOffsetOnAxis(ap=at[:, g, j:j + 1], axis=0)).then_inc(gathered[g % 2], 16)


def layer1_inputs(nc, a, xn, mv, x1_stored, ident, ones, h_hi, h_lo, group_dram, acs_dram, g_dram):
    with ExitStack() as ctx:
        sem = Sems(nc, ctx)

        def sb(name, shape, dt=F32):
            return ctx.enter_context(nc.sbuf_tensor(name, shape, dt))

        var_eps = sb("m_var_eps", [P, NT])
        std = sb("m_std", [P, NT])
        rstd = sb("m_rstd", [P, NT])
        meansq = sb("m_meansq", [P, NT])
        rms = sb("m_rms", [P, NT])
        rrms = sb("m_rrms", [P, NT])
        normw = sb("m_normw", [P, KD])
        wdt = sb("m_wdt", [P, KD, HEADS])
        wdt_hi = sb("m_wdt_hi", [P, KD, HEADS], F32R)
        wdt_lo = sb("m_wdt_lo", [P, KD, HEADS], F32R)
        dtb = sb("m_dtb", [P, 1])
        alog = sb("m_alog", [P, 1])
        aexp = sb("m_aexp", [P, 1])
        dt = sb("m_dt", [P, T])
        acs = sb("m_acs", [P, T])
        decay = sb("m_decay", [P, T])
        lastdecay = sb("m_lastdecay", [P, 4])
        diag = sb("m_diag", [P, 4, HEADS])
        group = sb("m_group", [P, GROUPS, GROUP_N])
        xn_hi = sb("m_xn_hi", [P, KD, T], F32R)
        xn_lo = sb("m_xn_lo", [P, KD, T], F32R)
        gu_q, d_q = sb("f_gu_q", [P, 2, GU], I32), sb("f_d_q", [P, 3, D], I32)
        gu_w, d_w = sb("f_gu_w", [P, 2, GU]), sb("f_d_w", [P, 3, D])
        gu_hi, d_hi = sb("f_gu_hi", [P, 2, GU], F32R), sb("f_d_hi", [P, 2, D], F32R)
        gu_lo, d_lo = sb("f_gu_lo", [P, 2, GU], F32R), sb("f_d_lo", [P, 2, D], F32R)
        gated = sb("f_gated", [P, NB, SEQ])
        inner1 = sb("f_inner1", [P, KI, SEQ])
        in_hi = sb("f_in_hi", [P, 2, SEQ], F32R)
        in_lo = sb("f_in_lo", [P, 2, SEQ], F32R)
        g = gu_w[:].rearrange("p b (h d) -> p (b h) d", d=D)
        h = inner1[:, 0:2, :]
        hw = inner1[:, 2:4, :].rearrange("p b (k c) -> p b k c", k=KD)
        v = inner1[:, 6:8, :]
        av, e, u1, ln, z, step = (inner1[:, i, :] for i in range(8, 14))
        ps = ctx.enter_context(nc.psum_tensor("m_ps", [P, 8, 512], F32))

        loaded = sem("m_loaded")
        dve_chain = sem("m_dve_chain")
        act_chain = sem("m_act_chain")
        var_ready = sem("m_var_ready")
        std_ready = sem("m_std_ready")
        xn_ready = sem("m_xn_ready")
        meansq_ready = sem("m_meansq_ready")
        rms_ready = sem("m_rms_ready")
        h_ready = sem("m_h_ready")
        xn_turned = sem("m_xn_turned")
        h_turned = sem("m_h_turned")
        xn_hi_ready = sem("m_xn_hi_ready")
        xn_lo_ready = sem("m_xn_lo_ready")
        hw_ready = sem("m_hw_ready")
        h_hi_ready = sem("m_h_hi_ready")
        h_lo_ready = sem("m_h_lo_ready")
        ones_ready = sem("m_ones_ready")
        wdt_split = sem("m_wdt_split")
        dt_proj = sem("m_dt_proj")
        v_ready = sem("m_v_ready")
        e_ready = sem("m_e_ready")
        u1_ready = sem("m_u1_ready")
        ln_ready = sem("m_ln_ready")
        dt_ready = sem("m_dt_ready")
        aexp_ready = sem("m_aexp_ready")
        acs_ready = sem("m_acs_ready")
        decay_ready = sem("m_decay_ready")
        dd_ready = sem("m_dd_ready")
        diag_ready = sem("m_diag_ready")
        turned = sem("m_turned")
        group_ready = sem("m_group_ready")
        stored = sem("m_stored")
        gu_loaded = [sem(f"f_gu_loaded{i}") for i in range(2)]
        d_loaded = [sem(f"f_d_loaded{i}") for i in range(3)]
        gu_scaled, d_scaled = sem("f_gu_scaled"), sem("f_d_scaled")
        gu_hi_ready, d_hi_ready = sem("f_gu_hi_ready"), sem("f_d_hi_ready")
        gu_lo_ready, d_lo_ready = sem("f_gu_lo_ready"), sem("f_d_lo_ready")
        gate_up_done = [sem(f"f_gate_up_done{n}") for n in range(NB)]
        silu_ready = [sem(f"f_silu_ready{n}") for n in range(NB)]
        inner_ready = [sem(f"f_inner_ready{n}") for n in range(NB)]
        in_hi_ready = sem("f_in_hi_ready")
        in_lo_ready = sem("f_in_lo_ready")
        down_done = sem("f_down_done")
        g_ready = sem("f_g_ready")
        g_stored = [sem(f"f_g_stored{i}") for i in range(4)]


        def g_store(sp, j):
            sp.wait_ge(g_ready, j + 1)
            sp.dma_start(g_dram[:, j, :], g[:, j % 4, :]).then_inc(g_stored[j % 4], 16)

        def pe_gate_up(pe, m):
            pe.wait_ge(gu_lo_ready, m + 1)
            for n in range(NB):
                if m:
                    pe.wait_ge(inner_ready[n], m)
                for part in range(2):
                    for k in range(KD):
                        at = slice((part * KD + k) * P, (part * KD + k + 1) * P)
                        c = slice(n * SEQ, (n + 1) * SEQ)
                        mm = three_passes(nc, ps[:, 2 * n + part, :], gu_hi[:, m % 2, at], gu_lo[:, m % 2, at],
                                          xn_hi[:, k, c], xn_lo[:, k, c], k == 0, k == KD - 1)
                mm.then_inc(gate_up_done[n], 1)

        def pe_down(pe, i):
            m, first = i % KI, 4 if i < KI else 0
            pe.wait_ge(d_lo_ready, i + 1)
            pe.wait_ge(in_lo_ready, i + 1)
            if i == 0:
                pe.wait_ge(v_ready, NB)
            if i == KI:
                for n in range(NB):
                    pe.wait_ge(inner_ready[n], KI)
            for t in range(TB):
                c = slice(t * P, (t + 1) * P)
                mm = three_passes(nc, ps[:, first + t, :], in_hi[:, i % 2, c], in_lo[:, i % 2, c],
                                  d_hi[:, i % 2, :], d_lo[:, i % 2, :], m == 0, m == KI - 1)
            mm.then_inc(down_done, 1)

        def pe_turn(src, first):
            for t in range(NT):
                mm = nc.tensor.transpose(ps[:, first + t // 4, (t % 4) * P:(t % 4 + 1) * P],
                                         src[:, t * P:(t + 1) * P], ident[:])
            mm.then_inc(turned, 1)

        def act_gate_up(act, m):
            act.wait_ge(gu_scaled, m + 1)
            if m >= 2:
                act.wait_ge(gate_up_done[NB - 1], m - 1)
            nc.scalar.activation(gu_hi[:, m % 2, :], gu_w[:, m % 2, :], ACT.Copy).then_inc(gu_hi_ready, 1)

        def act_down(act, i):
            act.wait_ge(d_scaled, i + 1)
            if i >= 2:
                act.wait_ge(down_done, i - 1)
            nc.scalar.activation(d_hi[:, i % 2, :], d_w[:, i % 3, :], ACT.Copy).then_inc(d_hi_ready, 1)

        def act_in(act, i):
            n = i // KI
            act.wait_ge(inner_ready[n], i % KI + 1)
            if i >= 2:
                act.wait_ge(down_done, i - 1)
            nc.scalar.activation(in_hi[:, i % 2, :], gated[:, 0, :] if n == 0 else inner1[:, i % KI, :],
                                 ACT.Copy).then_inc(in_hi_ready, 1)

        def act_out(act, j):
            act.wait_ge(down_done, KI * (j // TB + 1))
            if j >= 4:
                act.wait_ge(g_stored[j % 4], 16 * (j // 4))
            bank = j + 4 if j < TB else j - TB
            nc.scalar.activation(g[:, j % 4, :], ps[:, bank, :], ACT.Silu).then_inc(g_ready, 1)

        def act_exp(act, n):
            act.wait_ge(v_ready, n + 1)
            if n:
                act.wait_ge(acs_ready, n * TB)
            nc.scalar.activation(av, v[:, n, :], ACT.Abs).then_inc(act_chain, 1)
            act.wait_ge(act_chain, n + 1)
            nc.scalar.activation(e, av, ACT.Exp, scale=-1.0).then_inc(e_ready, 1)

        def act_decay(act, n):
            for t in range(n * TB, (n + 1) * TB):
                act.wait_ge(acs_ready, t + 1)
                last = acs[:, (t + 1) * P - 1:(t + 1) * P]
                ins = nc.scalar.activation(decay[:, t * P:(t + 1) * P], acs[:, t * P:(t + 1) * P], ACT.Exp,
                                           bias=last, scale=-1.0)
            ins.then_inc(decay_ready, 1)
            for i, t in enumerate((n * TB + 1, n * TB + 2)):
                ins = nc.scalar.activation(lastdecay[:, 2 * n + i:2 * n + i + 1],
                                           acs[:, (t + 1) * P - 1:(t + 1) * P], ACT.Exp)
            ins.then_inc(decay_ready, 1)

        def dve_log_terms(link, n):
            dve = nc.vector
            dve.wait_ge(e_ready, n + 1)
            dve.tensor_scalar(u1, e, 1.0, None, ALU.add).then_inc(u1_ready, 1)
            dve.wait_ge(u1_ready, n + 1)
            link(dve.tensor_scalar(av, u1, -1.0, None, ALU.add))
            link(dve.tensor_scalar(z, av, 0.0, None, ALU.is_equal))
            link(dve.tensor_tensor(av, av, z, ALU.add))
            link(dve.reciprocal(step, av))
            link(dve.tensor_tensor(step, step, e, ALU.mult))
            link(dve.tensor_tensor(z, z, e, ALU.mult))

        def dve_dt(link, n):
            dve, c = nc.vector, slice(n * SEQ, (n + 1) * SEQ)
            dve.wait_ge(ln_ready, n + 1)
            link(dve.tensor_tensor(ln, ln, step, ALU.mult))
            link(dve.tensor_tensor(ln, ln, z, ALU.add))
            dve.scalar_tensor_tensor(dt[:, c], v[:, n, :], 0.0, ln, ALU.max, ALU.add).then_inc(dt_ready, 1)
            dve.wait_ge(dt_ready, n + 1)
            dve.wait_ge(aexp_ready, 1)
            link(dve.tensor_scalar(step, dt[:, c], aexp[:, 0:1], -1.0, ALU.mult, ALU.mult))
            dve.wait_ge(ones_ready, 1)
            for t in range(TB):
                at = slice((n * TB + t) * P, (n * TB + t + 1) * P)
                dve.tensor_tensor_scan(acs[:, at], ones[:], step[:, t * P:(t + 1) * P], 0.0, ALU.mult,
                                       ALU.add).then_inc(acs_ready, 1)

        def dve_decay(n):
            dve, c = nc.vector, slice(n * SEQ, (n + 1) * SEQ)
            dve.wait_ge(decay_ready, 2 * (n + 1))
            dve.tensor_tensor(decay[:, c], decay[:, c], dt[:, c], ALU.mult).then_inc(dd_ready, 1)
            for i in (2 * n, 2 * n + 1):
                dve.tensor_scalar(diag[:, i, :], ident[:], lastdecay[:, i:i + 1], None,
                                  ALU.mult).then_inc(diag_ready, 1)

        def dve_group():
            def banks(b):
                return ps[:, b:b + 2, :].rearrange("p b (t g h) -> p (b t) g h", t=4, g=GROUPS)

            def part(i):
                return group[:, :, i * NT * HG:(i + 1) * NT * HG].rearrange("p g (t h) -> p t g h", t=NT)
            dve = nc.vector
            for i, (at, bank) in enumerate(((0, 0), (2, 2), (1, 0))):
                dve.wait_ge(turned, i + 1)
                dve.tensor_copy(part(at), banks(bank)).then_inc(group_ready, 1)
            dve.wait_ge(turned, 4)
            dve.tensor_copy(group[:, :, 3 * NT * HG:].rearrange("p g (c h) -> p c g h", c=4),
                            ps[:, 2, :].rearrange("p (c g h) -> p c g h", c=4, g=GROUPS)).then_inc(group_ready, 1)

        def dve_in_lo(dve, i):
            dve.wait_ge(in_hi_ready, i + 1)
            nc.vector.tensor_tensor(in_lo[:, i % 2, :], gated[:, 0, :] if i < KI else inner1[:, i % KI, :],
                                    in_hi[:, i % 2, :].bitcast(F32), ALU.subtract).then_inc(in_lo_ready, 1)

        def dve_scale_gate_up(dve, m):
            dve.wait_ge(gu_loaded[m % 2], 32 * (m // 2 + 1))
            nc.vector.tensor_tensor(gu_w[:, m % 2, :], gu_q[:, m % 2, :], gu_w[:, m % 2, :],
                                    ALU.mult).then_inc(gu_scaled, 1)

        def dve_scale_down(dve, i):
            dve.wait_ge(d_loaded[i % 3], 32 * (i // 3 + 1))
            nc.vector.tensor_tensor(d_w[:, i % 3, :], d_q[:, i % 3, :], d_w[:, i % 3, :],
                                    ALU.mult).then_inc(d_scaled, 1)

        def dve_turned(dve, t):
            if t < NT:
                if t >= 2:
                    dve.wait_ge(h_turned, t - 1)
                dve.wait_ge(xn_ready, t + 1)
                nc.vector.tensor_scalar(h[:, t % 2, :], xn[:, t, :], rrms[:, t:t + 1], None,
                                        ALU.mult).then_inc(h_ready, 1)
                c = slice(t * P, (t + 1) * P)
                dve.wait_ge(xn_hi_ready, t + 1)
                nc.vector.tensor_tensor(xn_lo[:, :, c], ps[:, t % 2, :].rearrange("p (k c) -> p k c", k=KD),
                                        xn_hi[:, :, c].bitcast(F32), ALU.subtract).then_inc(xn_lo_ready, 1)
            if t:
                s = t - 1
                if s == 0:
                    dve.wait_ge(loaded, 64)
                dve.wait_ge(h_turned, s + 1)
                if s >= 2:
                    dve.wait_ge(h_lo_ready, s - 1)
                nc.vector.tensor_tensor(hw[:, s % 2], ps[:, 2 + s % 2, :].rearrange("p (k c) -> p k c", k=KD),
                                        normw[:].unsqueeze(2).to_broadcast((P, KD, P)), ALU.mult).then_inc(hw_ready, 1)


        block = ctx.enter_context(nc.Block())

        @block.sync
        def _(sp):
            def load_gate_up(m):
                if m >= 2:
                    sp.wait_ge(gu_lo_ready, m - 1)
                sp.dma_start(gu_q[:, m % 2, :], a["gu_q"][m]).then_inc(gu_loaded[m % 2], 16)
                sp.dma_start(gu_w[:, m % 2, :], a["gu_s"][m:m + 1, :].to_broadcast((P, GU))
                             ).then_inc(gu_loaded[m % 2], 16)

            def load_down(i):
                if i >= 3:
                    sp.wait_ge(d_lo_ready, i - 2)
                m = i % KI
                sp.dma_start(d_q[:, i % 3, :], a["d_q"][m]).then_inc(d_loaded[i % 3], 16)
                sp.dma_start(d_w[:, i % 3, :], a["d_s"][m:m + 1, :].to_broadcast((P, D))
                             ).then_inc(d_loaded[i % 3], 16)

            sp.dma_start(wdt[:], a["w_dt"]).then_inc(loaded, 16)
            sp.dma_start(normw[:], a["norm_w"]).then_inc(loaded, 16)
            sp.dma_start(dtb[:], a["dt_bias"]).then_inc(loaded, 16)
            sp.dma_start(alog[:], a["a_log"]).then_inc(loaded, 16)
            for m in range(KI):
                load_gate_up(m)
                load_down(m)
                if m == TURN_STEP:
                    sp.wait_ge(acs_ready, NT)
                    sp.dma_start(acs_dram, acs[:]).then_inc(stored, 16)
                if m == TURN_STEP + 2:
                    sp.wait_ge(group_ready, 4)
                    sp.dma_start(group_dram, group[:]).then_inc(stored, 16)
            for i in range(KI, 2 * KI):
                load_down(i)
                if KI + 2 <= i < KI + 2 + TB:
                    g_store(sp, i - KI - 2)
            for j in range(TB, NT):
                g_store(sp, j)
            for slot in g_stored:
                sp.wait_ge(slot, 16 * NT // 4)
            sp.wait_ge(stored, 32)

        @block.tensor
        def _(pe):
            for t in range(NT + 1):
                if t < NT:
                    pe.wait_ge(xn_ready, t + 1)
                    if t >= 2:
                        pe.wait_ge(xn_lo_ready, t - 1)
                    for k in range(KD):
                        mm = nc.tensor.transpose(ps[:, t % 2, k * P:(k + 1) * P], xn[:, t, k * P:(k + 1) * P],
                                                 ident[:])
                    mm.then_inc(xn_turned, 1)
                if t:
                    s = t - 1
                    pe.wait_ge(h_ready, s + 1)
                    if s >= 2:
                        pe.wait_ge(hw_ready, s - 1)
                    for k in range(KD):
                        mm = nc.tensor.transpose(ps[:, 2 + s % 2, k * P:(k + 1) * P],
                                                 h[:, s % 2, k * P:(k + 1) * P], ident[:])
                    mm.then_inc(h_turned, 1)
            pe.wait_ge(xn_lo_ready, NT)
            pe.wait_ge(hw_ready, NT)
            pe_gate_up(pe, 0)
            pe.wait_ge(wdt_split, 2)
            pe.wait_ge(h_lo_ready, NT)
            for n in range(NB):
                c = slice(n * SEQ, (n + 1) * SEQ)
                for k in range(KD):
                    mm = three_passes(nc, ps[:, 4 + n, :], wdt_hi[:, k, :], wdt_lo[:, k, :], h_hi[:, k, c],
                                      h_lo[:, k, c], k == 0, k == KD - 1)
                mm.then_inc(dt_proj, 1)
            for m in range(1, KI):
                if m == TURN_STEP:
                    for n in range(NB):
                        pe.wait_ge(inner_ready[n], m)
                    pe.wait_ge(dt_ready, NB)
                    pe_turn(dt, 0)
                    pe.wait_ge(acs_ready, NT)
                    pe_turn(acs, 2)
                    pe.wait_ge(dd_ready, NB)
                    pe.wait_ge(group_ready, 1)
                    pe_turn(decay, 0)
                    pe.wait_ge(diag_ready, 4)
                    pe.wait_ge(group_ready, 2)
                    mm = nc.tensor.matmul(ps[:, 2, :], ones[:], diag[:].rearrange("p c h -> p (c h)"),
                                          start=True, stop=True)
                    mm.then_inc(turned, 1)
                    pe_down(pe, m - 1)
                    pe.wait_ge(group_ready, 4)
                    pe_gate_up(pe, m)
                    continue
                pe_gate_up(pe, m)
                pe_down(pe, m - 1)
            for i in range(KI - 1, 2 * KI):
                pe_down(pe, i)

        @block.scalar
        def _(act):
            act.wait_ge(var_ready, 1)
            nc.scalar.activation(std[:], var_eps[:], ACT.Sqrt).then_inc(std_ready, 1)
            act.wait_ge(meansq_ready, 1)
            nc.scalar.activation(rms[:], meansq[:], ACT.Sqrt).then_inc(rms_ready, 1)
            act.wait_ge(loaded, 64)
            nc.scalar.activation(wdt_hi[:], wdt[:], ACT.Copy).then_inc(wdt_split, 1)
            for t in range(NT + 1):
                if t < NT:
                    act.wait_ge(xn_turned, t + 1)
                    nc.scalar.activation(xn_hi[:, :, t * P:(t + 1) * P],
                                         ps[:, t % 2, :].rearrange("p (k c) -> p k c", k=KD),
                                         ACT.Copy).then_inc(xn_hi_ready, 1)
                if t:
                    s = t - 1
                    act.wait_ge(hw_ready, s + 1)
                    nc.scalar.activation(h_hi[:, :, s * P:(s + 1) * P], hw[:, s % 2], ACT.Copy).then_inc(h_hi_ready, 1)
                if t == 5:
                    act_gate_up(act, 0)
            act_gate_up(act, 1)
            act_down(act, 0)
            act.wait_ge(loaded, 64)
            nc.scalar.activation(aexp[:], alog[:], ACT.Exp).then_inc(aexp_ready, 1)
            for m in range(KI):
                if m and m + 1 < KI:
                    act_gate_up(act, m + 1)
                if m:
                    act_down(act, m)
                for n in range(NB):
                    act.wait_ge(gate_up_done[n], m + 1)
                    if m:
                        act.wait_ge(in_lo_ready if n == 0 else inner_ready[1], m)
                    nc.scalar.activation(gated[:, n, :], ps[:, 2 * n, :], ACT.Silu).then_inc(silu_ready[n], 1)
                    if n == 0:
                        act_in(act, m)
                if m in (1, 3):
                    act.wait_ge(u1_ready, m // 2 + 1)
                    nc.scalar.activation(ln, u1, ACT.Ln).then_inc(ln_ready, 1)
                if m in (0, 2):
                    act_exp(act, m // 2)
                if m in (2, 4):
                    act_decay(act, m // 2 - 1)
            for i in range(KI, 2 * KI):
                act_down(act, i)
                act_in(act, i)
                if i < KI + TB:
                    act_out(act, i - KI)
            for j in range(TB, NT):
                act_out(act, j)

        @block.vector
        def _(dve):
            link = chain_on(dve, dve_chain)
            nc.vector.tensor_scalar(var_eps[:], mv[:, :, 1], EPS, None, ALU.add).then_inc(var_ready, 1)
            dve.wait_ge(std_ready, 1)
            link(nc.vector.reciprocal(rstd[:], std[:]))
            dve.wait_ge(x1_stored, 16 * NT)
            for t in range(2):
                nc.vector.tensor_scalar(xn[:, t, :], xn[:, t, :], mv[:, t, 0:1], rstd[:, t:t + 1],
                                        ALU.subtract, ALU.mult).then_inc(xn_ready, 1)
            link(nc.vector.tensor_tensor(meansq[:], rstd[:], rstd[:], ALU.mult))
            link(nc.vector.tensor_tensor(meansq[:], meansq[:], mv[:, :, 1], ALU.mult))
            nc.vector.tensor_scalar(meansq[:], meansq[:], EPS, None, ALU.add).then_inc(meansq_ready, 1)
            for t in range(2, NT):
                nc.vector.tensor_scalar(xn[:, t, :], xn[:, t, :], mv[:, t, 0:1], rstd[:, t:t + 1],
                                        ALU.subtract, ALU.mult).then_inc(xn_ready, 1)
                if t == 3:
                    dve.wait_ge(rms_ready, 1)
                    link(nc.vector.reciprocal(rrms[:], rms[:]))
                if t >= 3:
                    dve_turned(dve, t - 3)
                if t == 5:
                    dve_scale_gate_up(dve, 0)
            for t in range(NT - 3, NT + 1):
                dve_turned(dve, t)
            dve_scale_gate_up(dve, 1)
            dve_scale_down(dve, 0)
            for m in range(KI):
                if m in (1, 3):
                    dve_log_terms(link, m // 2)
                if m == TURN_STEP:
                    dve_group()
                for n in range(NB):
                    dve.wait_ge(silu_ready[n], m + 1)
                    nc.vector.tensor_tensor(gated[:, 0, :] if n == 0 else inner1[:, m, :], gated[:, n, :],
                                            ps[:, 2 * n + 1, :], ALU.mult).then_inc(inner_ready[n], 1)
                    if n == 0:
                        dve_in_lo(dve, m)
                if m == 0:
                    for n in range(NB):
                        dve.wait_ge(dt_proj, n + 1)
                        nc.vector.tensor_scalar(v[:, n, :], ps[:, 4 + n, :], dtb[:, 0:1], None,
                                                ALU.add).then_inc(v_ready, 1)
                if m + 2 < KI:
                    dve_scale_gate_up(dve, m + 2)
                dve_scale_down(dve, m + 1)
                if m in (1, 3):
                    dve_dt(link, m // 2)
                if m in (2, 4):
                    dve_decay(m // 2 - 1)
            for i in range(KI, 2 * KI):
                if i + 1 < 2 * KI:
                    dve_scale_down(dve, i + 1)
                dve_in_lo(dve, i)

        @block.gpsimd
        def _(pool):
            def rest_gate_up(m):
                pool.wait_ge(gu_hi_ready, m + 1)
                nc.gpsimd.tensor_tensor(gu_lo[:, m % 2, :], gu_w[:, m % 2, :], gu_hi[:, m % 2, :].bitcast(F32),
                                        ALU.subtract).then_inc(gu_lo_ready, 1)

            def rest_down(i):
                pool.wait_ge(d_hi_ready, i + 1)
                nc.gpsimd.tensor_tensor(d_lo[:, i % 2, :], d_w[:, i % 3, :], d_hi[:, i % 2, :].bitcast(F32),
                                        ALU.subtract).then_inc(d_lo_ready, 1)

            nc.gpsimd.memset(ones[:], 1.0).then_inc(ones_ready, 1)
            pool.wait_ge(wdt_split, 1)
            nc.gpsimd.tensor_tensor(wdt_lo[:], wdt[:], wdt_hi[:].bitcast(F32), ALU.subtract).then_inc(wdt_split, 1)
            for t in range(NT):
                c = slice(t * P, (t + 1) * P)
                pool.wait_ge(h_hi_ready, t + 1)
                nc.gpsimd.tensor_tensor(h_lo[:, :, c], hw[:, t % 2], h_hi[:, :, c].bitcast(F32),
                                        ALU.subtract).then_inc(h_lo_ready, 1)
                if t == 4:
                    rest_gate_up(0)
            for m in range(KI):
                if m + 1 < KI:
                    rest_gate_up(m + 1)
                rest_down(m)
            for i in range(KI, 2 * KI):
                rest_down(i)


BC_SLOT = 2
LOADS = [("HG", k) for k in range(BC_SLOT)] + [("BC", 0)] + [("HG", k) for k in range(BC_SLOT, KC)]
NLOAD = len(LOADS)
CONVS = [2 + k for k in range(BC_SLOT)] + [0, 1] + [2 + k for k in range(BC_SLOT, KC)]
NCONV = len(CONVS)


def slot_jobs(k):
    def ahead(i):
        return i // KC, i % KC
    jobs = [("ST", *ahead(k + 1)), ("DIAG", 0, k), ("OFF", 0, k), ("T", *ahead(k + 2))]
    if k == BC_SLOT:
        jobs += [("H", 1, CONVS.index(0)), ("H", 1, CONVS.index(1))]
    if k == 5:
        jobs += [("CB", 1, 0), ("BT", 1, 0)]
    return jobs + [("G", 1, k), ("H", 1, CONVS.index(2 + k))]


JOBS = [job for k in range(KC) for job in slot_jobs(k)]
PER = {"ST": KC, "DIAG": KC, "OFF": KC, "H": NCONV, "T": KC, "G": KC, "CB": 1, "BT": 1}
BANKS = 4
assert len(JOBS) % BANKS == 0


def mixer(nc, a, acc, ident, ones, h_hi, h_lo, group_dram, acs_dram, x1_dram, g_dram, out):
    with ExitStack() as ctx:
        sem = Sems(nc, ctx)

        def sb(name, shape, dt=F32):
            return ctx.enter_context(nc.sbuf_tensor(name, shape, dt))

        mask = sb("s_mask", [P, P])
        par = sb("s_par", [P, 2, 66])
        steps = sb("s_steps", [P, 2, 3, TB, HG])
        cdecay = sb("s_cdecay", [P, 2, 2, HG])
        skip4 = sb("s_skip4", [P, 2, KC])
        w_raw = sb("s_w_raw", [P, 2, 2 * KD * P])
        w_hi = sb("s_w_hi", [P, 2, 2 * KD * P], F32R)
        w_lo = sb("s_w_lo", [P, 2, 2 * KD * P], F32R)
        wo_raw = sb("s_wo_raw", [P, 2, D])
        wo_hi = sb("s_wo_hi", [P, 2, D], F32R)
        wo_lo = sb("s_wo_lo", [P, 2, D], F32R)
        cv = sb("s_cv", [P, 2, SEQ])
        th = sb("s_th", [P, 2, SEQ])
        tg = sb("s_tg", [P, SEQ])
        bT = sb("s_bT", [P, 2, SEQ])
        cT = sb("s_cT", [P, 2, SEQ])
        hid = sb("s_hid", [P, KC, SEQ])
        gate = sb("s_gate", [P, KC, SEQ])
        b_l = sb("s_b_l", [P, 2, TB - 1, NST])
        cbt = sb("s_cbt", [P, 2, TB, P])
        hdt = sb("s_hdt", [P, 2, TB, P])
        hdd = sb("s_hdd", [P, 2, TB - 1, P])
        state = sb("s_state", [P, 2, TB - 1, P])
        rows = sb("s_rows", [P, 4, SEQ])
        lm = sb("s_lm", [P, 4, SEQ])
        scale = sb("s_scale", [P, 2, 3 * P])
        ysum = sb("s_ysum", [P, 2, SEQ])
        yoff = sb("s_yoff", [P, 2, 3 * P])
        y_hi = sb("s_y_hi", [P, 2, SEQ], F32R)
        y_lo = sb("s_y_lo", [P, 2, SEQ], F32R)
        sq = sb("s_sq", [P, 2, SEQ])
        ssq = sb("s_ssq", [P, SEQ])
        meansq = sb("s_meansq", [P, TB])
        rms = sb("s_rms", [P, TB])
        rrms = sb("s_rrms", [P, TB])
        ps = ctx.enter_context(nc.psum_tensor("s_ps", [P, BANKS, 512], F32))
        ps_o = ctx.enter_context(nc.psum_tensor("s_ps_o", [P, TB, 512], F32))

        mask_loaded = sem("s_mask_loaded")
        par_loaded = [sem(f"s_par_loaded{b}") for b in range(2)]
        w_loaded = [sem(f"s_w_loaded{b}") for b in range(2)]
        wo_loaded = [sem(f"s_wo_loaded{b}") for b in range(2)]
        rows_loaded = [sem(f"s_rows_loaded{i}") for i in range(4)]
        done = {kind: sem(f"s_{kind.lower()}_done") for kind in PER}
        took = {kind: sem(f"s_{kind.lower()}_took") for kind in PER}
        ssq_done = sem("s_ssq_done")
        ssq_took = sem("s_ssq_took")
        op_done = sem("s_op_done")
        op_took = sem("s_op_took")
        w_hi_ready = sem("s_w_hi_ready")
        w_lo_ready = sem("s_w_lo_ready")
        wo_hi_ready = sem("s_wo_hi_ready")
        wo_lo_ready = sem("s_wo_lo_ready")
        skip_ready = sem("s_skip_ready")
        tap_ready = sem("s_tap_ready")
        conv_chain = sem("s_conv_chain")
        th_ready = sem("s_th_ready")
        tile_ready = sem("s_tile_ready")
        tg_ready = sem("s_tg_ready")
        state_chain = sem("s_state_chain")
        diff_ready = sem("s_diff_ready")
        exp_ready = sem("s_exp_ready")
        scale_ready = sem("s_scale_ready")
        m_ready = sem("s_m_ready")
        pool_chain = sem("s_pool_chain")
        y_ready = sem("s_y_ready")
        y_hi_ready = sem("s_y_hi_ready")
        y_lo_ready = sem("s_y_lo_ready")
        sq_ready = sem("s_sq_ready")
        ssq_ready = sem("s_ssq_ready")
        rms_ready = sem("s_rms_ready")
        rrms_ready = sem("s_rrms_ready")
        back = [sem(f"s_back{n}") for n in range(NB)]
        product_ready = sem("s_product_ready")
        out_ready = sem("s_out_ready")
        out_stored = sem("s_out_stored")

        class Unit:

            def __init__(self, g, b, first=False, last=False):
                self.g, self.b, self.u, self.first, self.last = g, b, 2 * g + b, first, last
                self.scans = not (isinstance(g, int) and g < 0)

            def ahead(self, n):
                if n == 1:
                    return Unit(self.g + self.b, 1 - self.b, first=not self.scans)
                return self if n == 0 else Unit(self.g - 1 + self.b, 1 - self.b)

            def at(self, per, i):
                return self.u * per + i + 1

        def exists(un, job):
            return not un.last if job[1] else un.scans

        def bank_free(pe, un, job):
            pos, owner = JOBS.index(job) - BANKS, un
            while True:
                if pos < 0:
                    if not owner.scans:
                        return
                    pos, owner = pos + len(JOBS), before(un)
                if exists(owner, JOBS[pos]):
                    kind, ahead, i = JOBS[pos]
                    u = (un.u if owner is un else un.u - 1) + ahead
                    pe.wait_ge(took[kind], u * PER[kind] + i + 1)
                    return
                pos -= BANKS

        def before(un):
            return Unit(-1, 1) if un.first else un.ahead(-1)

        def bank(job):
            return ps[:, JOBS.index(job) % BANKS, :]

        def load_slot(v, c):
            return (v.b + c) % 2, NLOAD * v.g + (NLOAD * v.b + c) // 2 + 1

        def loads_of(k):
            return [c for c in range(NLOAD) if LOADS[c] == ("HG", k) or k == BC_SLOT and LOADS[c][0] == "BC"]

        def loads_at_start(k):
            return loads_of(k) if k == 0 else [LOADS.index(("HG", k))] if k == BC_SLOT else []

        def loads_ahead(k):
            return [c for c in loads_of(k + 1) if c not in loads_at_start(k + 1)] if k + 1 < KC else []

        def conv_tile(v, i):
            j = CONVS[i]
            return bT[:, v.b, :] if j == 0 else cT[:, v.b, :] if j == 1 else hid[:, j - 2, :]

        def channel_tile_before(un, k):
            if not (un.scans if k == 0 else not un.last):
                return None
            i = CONVS.index(2 + (k - 1) % KC)
            return un.ahead(1 if k else 0), i, bank(("H", 1, i))

        UNITS = NB * GROUPS
        x1_b = w_raw[:].rearrange("p b (h d) -> p (b h) d", d=D)

        def ffn_b(t):
            return (cv if t % TB < 2 else th)[:, t % 2, :]

        def sp_back(sp, n):
            if n == 0:
                sp.wait_ge(w_lo_ready, UNITS * NLOAD)
            else:
                sp.wait_ge(out_ready, TB)
            sp.dma_start(x1_b, x1_dram[:, n * TB:(n + 1) * TB, :]).then_inc(back[n], 16)
            if n == 0:
                sp.wait_ge(tile_ready, UNITS * NCONV)
            sp.dma_start(cv[:], g_dram[:, n * TB:n * TB + 2, :]).then_inc(back[n], 16)
            sp.dma_start(th[:], g_dram[:, n * TB + 2:(n + 1) * TB, :]).then_inc(back[n], 16)

        def product(eng, tensor_tensor, t):
            eng.wait_ge(op_took, (UNITS - NB + t // TB) * TB + t % TB + 1)
            eng.wait_ge(back[t // TB], 48)
            tensor_tensor(acc[:, t, :], acc[:, t, :], ffn_b(t), ALU.mult).then_inc(product_ready, 1)

        def dve_total(dve, t):
            dve.wait_ge(product_ready, t + 1)
            dve.wait_ge(back[t // TB], 48)
            nc.vector.tensor_tensor(acc[:, t, :], acc[:, t, :], x1_b[:, t % TB, :], ALU.add).then_inc(out_ready, 1)

        def sp_out(sp, tiles):
            for t in tiles:
                sp.wait_ge(out_ready, t + 1)
                sp.dma_start(out[:, t, :], acc[:, t, :]).then_inc(out_stored, 16)

        def sp_params(sp, v, wait):
            if wait is not None:
                sp.wait_ge(y_hi_ready, wait)
                sp.wait_ge(y_lo_ready, wait)
            sp.dma_start(par[:, v.b], a["par"][:, bass.ds(v.g, 1), :].rearrange("p g c -> p (g c)")
                         ).then_inc(par_loaded[v.b], 16)
            src = group_dram[:, bass.ds(v.g, 1), 0:3 * NT * HG].rearrange("p g (s t h) -> p (g s) (t h)", s=3, t=NT)
            sp.dma_start(steps[:, v.b].rearrange("p s t h -> p s (t h)"),
                         src[:, :, v.b * TB * HG:(v.b + 1) * TB * HG]).then_inc(par_loaded[v.b], 16)
            at = 3 * NT * HG + v.b * 2 * HG
            sp.dma_start(cdecay[:, v.b].rearrange("p c h -> p (c h)"),
                         group_dram[:, bass.ds(v.g, 1), at:at + 2 * HG].rearrange("p g c -> p (g c)")
                         ).then_inc(par_loaded[v.b], 16)

        def sp_load(sp, v, c, free=True):
            slot, _ = load_slot(v, c)
            if free:
                sp.wait_ge(w_lo_ready, v.u * NLOAD + c - 1)
            sp.dma_start(w_raw[:, slot, :], a["w_in"][bass.ds(v.g * NLOAD + c, 1), :, :].rearrange("o p n -> (o p) n")
                         ).then_inc(w_loaded[slot], 16)

        def sp_rows(sp, v, k, free=True):
            for h in (2 * k, 2 * k + 1):
                if free:
                    sp.wait_ge(diff_ready, v.u * HG + h - 3)
                    sp.wait_ge(scale_ready, v.u * HG + h - 3)
                sp.dma_start(rows[:, h % 4, :], acs_dram[bass.ds(v.g * HG + h, 1), v.b * SEQ:(v.b + 1) * SEQ]
                             .to_broadcast((P, SEQ))).then_inc(rows_loaded[h % 4], 16)

        def sp_unit(sp, un):
            v = un.ahead(1)
            if not un.scans:
                sp.dma_start(mask[:], a["mask"]).then_inc(mask_loaded, 16)
            for k in range(KC):
                if un.scans:
                    if not (un.first and k < 2):
                        sp.wait_ge(wo_lo_ready, un.u * KC + k - 1)
                    sp.dma_start(wo_raw[:, k % 2, :], a["w_out"][bass.ds(un.g * KC + k, 1), :, :]
                                 .rearrange("o p n -> (o p) n")).then_inc(wo_loaded[k % 2], 16)
                job = ("T", *divmod(k + 2, KC))
                if exists(un, job):
                    sp_rows(sp, un.ahead(job[1]), job[2], free=un.scans)
                if not un.last:
                    for c in loads_of(k):
                        sp_load(sp, v, c, free=un.scans or c >= 2)
                    if k == 0:
                        sp_params(sp, v, None if un.first or not un.scans else un.u * KC)
                elif k == 1:
                    sp_back(sp, 0)

        def sp_last(sp):
            sp_out(sp, range(TB))
            sp_back(sp, 1)
            sp_out(sp, range(TB, NT))
            sp.wait_ge(out_stored, 16 * NT)

        def pe_project(pe, v, c, half, dst, kind):
            slot, _ = load_slot(v, c)
            pe.wait_ge(w_hi_ready, v.at(NLOAD, c))
            pe.wait_ge(w_lo_ready, v.at(NLOAD, c))
            cols = slice(v.b * SEQ, (v.b + 1) * SEQ)
            for k in range(KD):
                at = slice((half * KD + k) * P, (half * KD + k + 1) * P)
                mm = three_passes(nc, dst, w_hi[:, slot, at], w_lo[:, slot, at], h_hi[:, k, cols], h_lo[:, k, cols],
                                  k == 0, k == KD - 1)
            mm.then_inc(done[kind], 1)

        def pe_cb(pe, v, dst):
            pe.wait_ge(tile_ready, v.at(NCONV, CONVS.index(1)))
            for i in range(TB):
                c = slice(i * P, (i + 1) * P)
                mm = nc.tensor.matmul(dst[:, c], bT[:, v.b, c], cT[:, v.b, c], start=True, stop=True)
            mm.then_inc(done["CB"], 1)

        def pe_bt(pe, v, dst):
            for i in range(TB - 1):
                c = slice(i * P, (i + 1) * P)
                mm = nc.tensor.transpose(dst[:, c], bT[:, v.b, c], ident[:])
            mm.then_inc(done["BT"], 1)

        def pe_turn(pe, v, k, dst):
            pe.wait_ge(tile_ready, v.at(NCONV, CONVS.index(2 + k)))
            for i in range(TB):
                c = slice(i * P, (i + 1) * P)
                mm = nc.tensor.transpose(dst[:, c], hid[:, k, c], ident[:])
            mm.then_inc(done["T"], 1)

        def pe_state(pe, v, k, dst):
            pe.wait_ge(took["BT"], v.at(1, 0))
            pe.wait_ge(took["T"], v.at(KC, k))
            for i in range(TB - 1):
                mm = nc.tensor.matmul(dst[:, i * P:(i + 1) * P], b_l[:, v.b, i, :], hdd[:, k % 2, i, :],
                                      start=True, stop=True)
            mm.then_inc(done["ST"], 1)

        def pe_op(pe, v, k, tiles):
            if tiles[0] == 0:
                for s in (wo_hi_ready, wo_lo_ready, y_hi_ready, y_lo_ready):
                    pe.wait_ge(s, v.at(KC, k))
            for t in tiles:
                c = slice(t * P, (t + 1) * P)
                mm = three_passes(nc, ps_o[:, t, :], y_hi[:, k % 2, c], y_lo[:, k % 2, c], wo_hi[:, k % 2, :],
                                  wo_lo[:, k % 2, :], k == 0, k == KC - 1)
            if tiles[-1] == TB - 1:
                mm.then_inc(op_done, 1)

        def pe_ssq(pe, v, dst):
            pe.wait_ge(ssq_ready, v.at(KC - 1, KC - 2))
            for t in range(TB):
                mm = nc.tensor.matmul(dst[:, 3 * P + t:3 * P + t + 1], ssq[:, t * P:(t + 1) * P], ones[:, 0:1], start=True, stop=True)
            mm.then_inc(ssq_done, 1)

        def pe_unit(pe, un):
            prev = before(un)
            for k in range(KC):
                done_pair = (un, k - 1) if k else (prev, KC - 1)
                for job in slot_jobs(k):
                    kind, n, i = job
                    if exists(un, job):
                        v = un.ahead(n)
                        dst = bank(job)
                        bank_free(pe, un, job)
                        if kind == "CB":
                            pe_cb(pe, v, dst)
                        elif kind == "BT":
                            pe_bt(pe, v, dst)
                        elif kind == "ST":
                            pe_state(pe, v, i, dst)
                        elif kind == "T":
                            pe_turn(pe, v, i, dst)
                        elif kind == "H":
                            j = CONVS[i]
                            c, half = (LOADS.index(("BC", 0)), j) if j < 2 else (LOADS.index(("HG", j - 2)), 0)
                            pe_project(pe, v, c, half, dst, "H")
                        elif kind == "G":
                            pe_project(pe, v, LOADS.index(("HG", i)), 1, dst, "G")
                        elif kind == "DIAG":
                            pe.wait_ge(m_ready, v.at(HG, 2 * k + 1))
                            pe.wait_ge(took["T"], v.at(KC, k))
                            for e in range(2):
                                for j in range(TB):
                                    c = slice(j * P, (j + 1) * P)
                                    mm = nc.tensor.matmul(dst[e * HP:(e + 1) * HP, c],
                                                          hdt[:, k % 2, j, e * HP:(e + 1) * HP],
                                                          lm[:, (2 * k + e) % 4, c], start=True, stop=True)
                            mm.then_inc(done["DIAG"], 1)
                        else:
                            if k == 0 and not un.first:
                                pe_ssq(pe, prev, dst)
                            pe.wait_ge(took["ST"], v.at(KC, k))
                            for j in range(TB - 1):
                                mm = nc.tensor.matmul(dst[:, j * P:(j + 1) * P], state[:, k % 2, j, :],
                                                      cT[:, un.b, (j + 1) * P:(j + 2) * P], start=True, stop=True)
                            mm.then_inc(done["OFF"], 1)
                    if done_pair[0].scans and kind in ("DIAG", "OFF"):
                        if kind == "DIAG" and done_pair[1] == 0 and not un.first:
                            pe.wait_ge(op_took, un.u * TB)
                        pe_op(pe, *done_pair, (0, 1) if kind == "DIAG" else (2, 3))

        def pe_last(pe):
            v = Unit(GROUPS - 1, 1)
            pe_op(pe, v, KC - 1, (0, 1))
            pe_op(pe, v, KC - 1, (2, 3))
            pe.wait_ge(took["OFF"], v.at(KC, KC - 1))
            pe_ssq(pe, v, ps[:, 0, :])

        def act_w(act, v, c, first=False):
            slot, n = load_slot(v, c)
            act.wait_ge(w_loaded[slot], 16 * n)
            if not (first and c < 2):
                act_done(act, v, c - 2)
            nc.scalar.activation(w_hi[:, slot, :], w_raw[:, slot, :], ACT.Copy).then_inc(w_hi_ready, 1)

        def act_done(eng, v, c):
            u = v.u if c >= 0 else v.u - 1
            kind, k = LOADS[c % NLOAD]
            eng.wait_ge(done["H"], u * NCONV + CONVS.index(1 if kind == "BC" else 2 + k) + 1)

        def act_diff(act, v, k, first=False):
            if not first:
                act.wait_ge(done["DIAG"], v.u * KC + k - 1)
            for h in (2 * k, 2 * k + 1):
                act.wait_ge(rows_loaded[h % 4], 16 * (v.u * (HG // 4) + h // 4 + 1))
                for i in range(TB):
                    c = slice(i * P, (i + 1) * P)
                    ins = nc.scalar.activation(lm[:, h % 4, c], rows[:, h % 4, c], ACT.Relu,
                                               bias=steps[:, v.b, 2, i, h:h + 1], scale=-1.0)
                ins.then_inc(diff_ready, 1)

        def act_exps(act, v, k):
            for h in (2 * k, 2 * k + 1):
                act.wait_ge(diff_ready, v.at(HG, h))
                nc.scalar.activation(lm[:, h % 4, :], lm[:, h % 4, :], ACT.Exp, scale=-1.0).then_inc(exp_ready, 1)

        def act_scale(act, v, k, first=False):
            if not first:
                act.wait_ge(took["OFF"], v.u * KC + k - 1)
            for h in (2 * k, 2 * k + 1):
                e = h % 2
                nc.scalar.activation(scale[e * HP:(e + 1) * HP, k % 2, :], rows[e * HP:(e + 1) * HP, h % 4, P:],
                                     ACT.Exp).then_inc(scale_ready, 1)

        def act_tap(act, v, i, src):
            j = CONVS[i]
            act.wait_ge(done["H"], v.at(NCONV, i))
            act.wait_ge(par_loaded[v.b], 48 * (v.g + 1))
            if not v.first or i >= 2:
                act.wait_ge(tile_ready, v.u * NCONV + i - 1)
            nc.scalar.activation(cv[:, i % 2, :], src, ACT.Identity,
                                 bias=par[:, v.b, 40 + j:41 + j],
                                 scale=par[:, v.b, 4 * j + 3:4 * j + 4]).then_inc(tap_ready, 1)

        def act_tanh(act, v, i):
            act.wait_ge(took["H"], v.at(NCONV, i))
            nc.scalar.activation(th[:, i % 2, :], cv[:, i % 2, :], ACT.Tanh, scale=0.5).then_inc(th_ready, 1)

        def act_gate(act, v, k, src):
            act.wait_ge(done["G"], v.at(KC, k))
            if not v.first or k:
                act.wait_ge(took["G"], v.u * KC + k)
            nc.scalar.activation(tg[:], src, ACT.Tanh, scale=0.5).then_inc(tg_ready, 1)

        def act_y(act, un, k):
            act.wait_ge(y_ready, un.at(KC, k))
            if not (un.first and k < 2):
                act.wait_ge(op_done, un.u * KC + k - 1)
            nc.scalar.activation(y_hi[:, k % 2, :], ysum[:, k % 2, :], ACT.Copy,
                                 scale=par[:, un.b, 58 + k:59 + k]).then_inc(y_hi_ready, 1)

        def act_sq(act, un, k):
            if k >= 2:
                act.wait_ge(ssq_ready, un.u * (KC - 1) + max(k - 2, 1))
            elif not un.first:
                act.wait_ge(ssq_ready, un.u * (KC - 1))
            nc.scalar.activation(sq[:, k % 2, :], ysum[:, k % 2, :], ACT.Square).then_inc(sq_ready, 1)

        def act_wo(act, un, k):
            act.wait_ge(wo_loaded[k % 2], 16 * (un.u * (KC // 2) + k // 2 + 1))
            if not (un.first and k < 2):
                act.wait_ge(op_done, un.u * KC + k - 1)
            nc.scalar.activation(wo_hi[:, k % 2, :], wo_raw[:, k % 2, :], ACT.Copy).then_inc(wo_hi_ready, 1)

        def act_rms(act, v):
            act.wait_ge(ssq_took, v.at(1, 0))
            nc.scalar.activation(rms[:], meansq[:], ACT.Sqrt).then_inc(rms_ready, 1)

        def act_unit(act, un):
            v = un.ahead(1)
            b_at, c_at = CONVS.index(0), CONVS.index(1)
            for k in range(KC):
                tile = channel_tile_before(un, k)
                job = ("T", *divmod(k + 2, KC))
                two_on = (un.ahead(job[1]), job[2]) if exists(un, job) else None
                b_and_c = k == BC_SLOT and not un.last
                if tile:
                    act_tap(act, *tile)
                if not un.last:
                    for c in loads_at_start(k):
                        act_w(act, v, c, not un.scans)
                if not un.scans and not b_and_c:
                    for c in loads_ahead(k):
                        act_w(act, v, c, not un.scans)
                if two_on:
                    act_diff(act, *two_on, not un.scans)
                if tile:
                    act_tanh(act, *tile[:2])
                if k == 0 and un.scans and not un.first:
                    act_rms(act, un.ahead(-1))
                if two_on:
                    act_exps(act, *two_on)
                    act_scale(act, *two_on, not un.scans)
                if b_and_c:
                    act_tap(act, v, b_at, bank(("H", 1, b_at)))
                if un.scans:
                    act_wo(act, un, k)
                if k == 0 and not un.last:
                    act_gate(act, v, k, bank(("G", 1, k)))
                if un.scans and not un.last and not b_and_c:
                    for c in loads_ahead(k):
                        act_w(act, v, c, not un.scans)
                if un.scans:
                    act_y(act, un, k)
                if b_and_c:
                    act_tap(act, v, c_at, bank(("H", 1, c_at)))
                    act_tanh(act, v, b_at)
                if k and not un.last:
                    act_gate(act, v, k, bank(("G", 1, k)))
                if b_and_c:
                    for c in loads_ahead(k):
                        act_w(act, v, c, not un.scans)
                    act_tanh(act, v, c_at)
                if un.scans:
                    act_sq(act, un, k)

        def dve_state(dve, v, k, src, c):
            if c == 0:
                dve.wait_ge(done["ST"], v.at(KC, k))
                if k >= 2 or not v.first:
                    dve.wait_ge(done["OFF"], v.u * KC + k - 1)
                nc.vector.tensor_copy(state[:, k % 2, 0, :], src[:, 0:P]).then_inc(state_chain, 1)
                return
            dve.wait_ge(state_chain, (v.u * KC + k) * 2 + c)
            for e in range(2):
                h, cols = 2 * k + e, slice(e * HP, (e + 1) * HP)
                ins = nc.vector.scalar_tensor_tensor(
                    state[:, k % 2, c, cols], state[:, k % 2, c - 1, cols], cdecay[:, v.b, c - 1, h:h + 1],
                    src[:, c * P + e * HP:c * P + (e + 1) * HP], ALU.mult, ALU.add)
            ins.then_inc(state_chain if c == 1 else took["ST"], 1)

        def dve_turn(dve, v, k, src):
            dve.wait_ge(done["T"], v.at(KC, k))
            pair = slice(2 * k, 2 * k + 2)
            by_head = src.rearrange("p (c h e) -> p c h e", c=TB, h=2)
            nc.vector.tensor_tensor(hdd[:, k % 2].rearrange("p c (h e) -> p c h e", h=2), by_head[:, 0:TB - 1],
                                    steps[:, v.b, 1, 0:TB - 1, pair].unsqueeze(3).to_broadcast((P, TB - 1, 2, HP)),
                                    ALU.mult)
            nc.vector.tensor_tensor(hdt[:, k % 2].rearrange("p c (h e) -> p c h e", h=2), by_head,
                                    steps[:, v.b, 0, :, pair].unsqueeze(3).to_broadcast((P, TB, 2, HP)),
                                    ALU.mult).then_inc(took["T"], 1)

        def dve_m(dve, v, h):
            dve.wait_ge(exp_ready, v.at(HG, h))
            nc.vector.tensor_tensor(lm[:, h % 4, :], lm[:, h % 4, :], cbt[:, v.b].rearrange("p c i -> p (c i)"),
                                    ALU.mult).then_inc(m_ready, 1)

        def dve_conv(dve, v, i, src, d):
            j = CONVS[i]
            if d == 1:
                dve.wait_ge(tap_ready, v.at(NCONV, i))
            else:
                dve.wait_ge(conv_chain, (v.u * NCONV + i) * 2 + d - 1)
            dst = cv[:, i % 2, d:]
            nc.vector.scalar_tensor_tensor(dst, src[:, 0:SEQ - d], par[:, v.b, 4 * j + 3 - d:4 * j + 4 - d],
                                           dst, ALU.mult, ALU.add).then_inc(conv_chain if d < 3 else took["H"], 1)

        def dve_silu(dve, v, i):
            dve.wait_ge(th_ready, v.at(NCONV, i))
            nc.vector.scalar_tensor_tensor(conv_tile(v, i), th[:, i % 2, :], 1.0, cv[:, i % 2, :], ALU.add,
                                           ALU.mult).then_inc(tile_ready, 1)

        def dve_gate(dve, v, k, src):
            dve.wait_ge(tg_ready, v.at(KC, k))
            if not v.first:
                dve.wait_ge(y_ready, (v.u - 1) * KC + k + 1)
            nc.vector.scalar_tensor_tensor(gate[:, k, :], tg[:], 1.0, src, ALU.add, ALU.mult).then_inc(took["G"], 1)

        def dve_cb(dve, v, src):
            dve.wait_ge(done["CB"], v.at(1, 0))
            nc.vector.tensor_tensor(cbt[:, v.b], src.rearrange("p (c i) -> p c i", c=TB),
                                    mask[:].unsqueeze(1).to_broadcast((P, TB, P)), ALU.mult).then_inc(took["CB"], 1)

        def dve_bt(dve, v, src):
            dve.wait_ge(done["BT"], v.at(1, 0))
            nc.vector.tensor_copy(b_l[:, v.b].rearrange("p c n -> p (c n)"), src[:, 0:3 * P]).then_inc(took["BT"], 1)

        def dve_skip(dve, v):
            dve.wait_ge(par_loaded[v.b], 48 * (v.g + 1))
            nc.vector.tensor_scalar(skip4[:, v.b], par[:, v.b, 50:58], 4.0, None, ALU.mult).then_inc(skip_ready, 1)

        def dve_y_lo(dve, un, k):
            dve.wait_ge(y_hi_ready, un.at(KC, k))
            nc.vector.scalar_tensor_tensor(y_lo[:, k % 2, :], ysum[:, k % 2, :], par[:, un.b, 58 + k:59 + k],
                                           y_hi[:, k % 2, :].bitcast(F32), ALU.mult,
                                           ALU.subtract).then_inc(y_lo_ready, 1)

        def dve_ssq(dve, v, src):
            dve.wait_ge(ssq_done, v.at(1, 0))
            nc.vector.tensor_scalar(meansq[:], src[:, 3 * P:3 * P + TB], 1.0 / CG, 256 * EPS, ALU.mult,
                                    ALU.add).then_inc(ssq_took, 1)

        def dve_out(dve, v):
            dve.wait_ge(rms_ready, v.at(1, 0))
            nc.vector.reciprocal(rrms[:], rms[:]).then_inc(rrms_ready, 1)
            dve.wait_ge(rrms_ready, v.at(1, 0))
            dve.wait_ge(op_done, v.at(KC, KC - 1))
            for t in range(TB):
                nc.vector.scalar_tensor_tensor(acc[:, v.b * TB + t, :], ps_o[:, t, :], rrms[:, t:t + 1],
                                               acc[:, v.b * TB + t, :], ALU.mult, ALU.add).then_inc(op_took, 1)

        def dve_y(dve, un, k):
            dve.wait_ge(done["DIAG"], un.at(KC, k))
            if not (un.first and k < 2):
                dve.wait_ge(sq_ready, un.u * KC + k - 1)
                dve.wait_ge(y_lo_ready, un.u * KC + k - 1)
            dve.wait_ge(skip_ready, un.at(1, 0))
            nc.vector.scalar_tensor_tensor(ysum[:, k % 2, :], hid[:, k, :], skip4[:, un.b, k:k + 1],
                                           bank(("DIAG", 0, k)), ALU.mult, ALU.add).then_inc(took["DIAG"], 1)
            dve.wait_ge(done["OFF"], un.at(KC, k))
            dve.wait_ge(scale_ready, un.at(HG, 2 * k + 1))
            if k == 0 and not un.first:
                dve_ssq(dve, un.ahead(-1), bank(("OFF", 0, 0)))
            nc.vector.tensor_tensor(yoff[:, k % 2, :], bank(("OFF", 0, k))[:, 0:3 * P], scale[:, k % 2, :],
                                    ALU.mult).then_inc(took["OFF"], 1)

        def dve_unit(dve, un):
            v = un.ahead(1)
            b_at, c_at = CONVS.index(0), CONVS.index(1)
            if not un.scans:
                dve.wait_ge(mask_loaded, 16)
            for k in range(KC):
                st_job, turn_job = ("ST", *divmod(k + 1, KC)), ("T", *divmod(k + 2, KC))
                tile = channel_tile_before(un, k)
                for c in range(TB - 1):
                    if exists(un, st_job):
                        after = un.ahead(st_job[1]), st_job[2]
                        if c < 2:
                            dve_m(dve, after[0], 2 * after[1] + c)
                        dve_state(dve, *after, bank(st_job), c)
                    if tile:
                        dve_conv(dve, *tile, c + 1)
                if un.scans:
                    dve_y(dve, un, k)
                if tile:
                    dve_silu(dve, *tile[:2])
                if k == 0 and un.scans and not un.first:
                    dve_out(dve, un.ahead(-1))
                if exists(un, turn_job):
                    dve_turn(dve, un.ahead(turn_job[1]), turn_job[2], bank(turn_job))
                if not un.last:
                    if k == 5:
                        dve_cb(dve, v, bank(("CB", 1, 0)))
                        dve_bt(dve, v, bank(("BT", 1, 0)))
                    if k == 3:
                        dve_skip(dve, v)
                if k == BC_SLOT and not un.last:
                    for d in (1, 2, 3):
                        dve_conv(dve, v, b_at, bank(("H", 1, b_at)), d)
                    if un.scans:
                        dve_y_lo(dve, un, k)
                    dve_conv(dve, v, c_at, bank(("H", 1, c_at)), 1)
                    dve_silu(dve, v, b_at)
                    dve_conv(dve, v, c_at, bank(("H", 1, c_at)), 2)
                    dve_gate(dve, v, k, bank(("G", 1, k)))
                    dve_conv(dve, v, c_at, bank(("H", 1, c_at)), 3)
                    dve_silu(dve, v, c_at)
                else:
                    if not un.last:
                        dve_gate(dve, v, k, bank(("G", 1, k)))
                    if un.scans:
                        dve_y_lo(dve, un, k)
                    if un.last and 3 <= k < 3 + TB:
                        dve_total(dve, k - 3)

        def dve_last(dve):
            v = Unit(GROUPS - 1, 1)
            dve_ssq(dve, v, ps[:, 0, :])
            dve_out(dve, v)
            for t in range(TB, NT):
                product(dve, nc.vector.tensor_tensor, t)
            for t in range(TB, NT):
                dve_total(dve, t)

        def pool_w(pool, v, c):
            slot, _ = load_slot(v, c)
            pool.wait_ge(w_hi_ready, v.at(NLOAD, c))
            nc.gpsimd.tensor_tensor(w_lo[:, slot, :], w_raw[:, slot, :], w_hi[:, slot, :].bitcast(F32),
                                    ALU.subtract).then_inc(w_lo_ready, 1)

        def pool_sum(pool, un, k):
            pool.wait_ge(sq_ready, un.at(KC, k))
            if k > 1:
                pool.wait_ge(ssq_ready, un.u * (KC - 1) + k - 1)
            elif not un.first:
                pool.wait_ge(ssq_done, un.u)
            nc.gpsimd.tensor_tensor(ssq[:], sq[:, 0, :] if k == 1 else ssq[:], sq[:, k % 2, :],
                                    ALU.add).then_inc(ssq_ready, 1)

        def pool_y(pool, un, k):
            pool.wait_ge(took["OFF"], un.at(KC, k))
            nc.gpsimd.tensor_tensor(ysum[:, k % 2, P:], ysum[:, k % 2, P:], yoff[:, k % 2, :],
                                    ALU.add).then_inc(pool_chain, 1)
            pool.wait_ge(pool_chain, un.at(KC, k))
            nc.gpsimd.tensor_tensor(ysum[:, k % 2, :], ysum[:, k % 2, :], gate[:, k, :],
                                    ALU.mult).then_inc(y_ready, 1)
            pool.wait_ge(wo_hi_ready, un.at(KC, k))
            nc.gpsimd.tensor_tensor(wo_lo[:, k % 2, :], wo_raw[:, k % 2, :], wo_hi[:, k % 2, :].bitcast(F32),
                                    ALU.subtract).then_inc(wo_lo_ready, 1)

        def pool_unit(pool, un):
            v = un.ahead(1)
            for k in range(KC):
                if un.scans:
                    if k > 1:
                        pool_sum(pool, un, k - 1)
                    elif k == 0 and not un.first:
                        pool_sum(pool, un.ahead(-1), KC - 1)
                if not un.last:
                    for c in loads_at_start(k):
                        pool_w(pool, v, c)
                if un.scans:
                    pool_y(pool, un, k)
                if not un.last:
                    for c in loads_ahead(k):
                        pool_w(pool, v, c)
                elif 2 <= k < 2 + TB:
                    product(pool, nc.gpsimd.tensor_tensor, k - 2)
            if un.last:
                pool_sum(pool, un, KC - 1)

        def schedule(eng, unit, end):
            unit(eng, Unit(-1, 1))
            unit(eng, Unit(0, 0, first=True))
            with eng.Fori(0, GROUPS - 1) as g:
                unit(eng, Unit(g, 1))
                unit(eng, Unit(g + 1, 0))
            unit(eng, Unit(GROUPS - 1, 1, last=True))
            if end:
                end(eng)

        with nc.Block() as block:
            @block.sync
            def _(sp):
                schedule(sp, sp_unit, sp_last)

            @block.tensor
            def _(pe):
                schedule(pe, pe_unit, pe_last)

            @block.scalar
            def _(act):
                schedule(act, act_unit, lambda e: act_rms(e, Unit(GROUPS - 1, 1)))

            @block.vector
            def _(dve):
                schedule(dve, dve_unit, dve_last)

            @block.gpsimd
            def _(pool):
                schedule(pool, pool_unit, None)


def program(nc, a, out):
    with ExitStack() as ctx:
        def sb(name, shape, dt=F32):
            return ctx.enter_context(nc.sbuf_tensor(name, shape, dt))

        def dram(name, shape):
            return nc.dram_tensor(name, shape, F32, kind="Internal").ap()

        xs = sb("xs", [P, NT, D])
        ident = sb("ident", [P, P])
        table = dram("table", [T, 2 * D])
        x1_dram = dram("x1_dram", [P, NT, D])
        g_dram = dram("g_dram", [P, NT, D])
        acs_dram = dram("acs_dram", [HEADS, T])
        group_dram = dram("group_dram", [P, GROUPS, GROUP_N])
        x1_mv = sb("x1_mv", [P, NT, 2])
        x1_stored = Sems(nc, ctx)("x1_stored")
        layer0(nc, a, xs, x1_mv, ident, x1_dram, x1_stored, table)
        ones = sb("ones", [P, P])
        h_hi = sb("h_hi", [P, KD, T], F32R)
        h_lo = sb("h_lo", [P, KD, T], F32R)
        layer1_inputs(nc, a, xs, x1_mv, x1_stored, ident, ones, h_hi, h_lo, group_dram, acs_dram, g_dram)
        mixer(nc, a, xs, ident, ones, h_hi, h_lo, group_dram, acs_dram, x1_dram, g_dram,
              out.rearrange("(t p) d -> p t d", p=P))


def shape_tables(np):
    t = np.arange(D)
    f = np.arange(D // 2)
    ang = 2 * np.pi * ((t[:, None] * f[None, :]) % D) / D
    cos, sin = np.cos(ang), np.sin(ang)
    sin[:, 0] = np.cos(np.pi * t)
    dft = np.concatenate([cos, sin], 1)
    weight = np.full(D // 2, 2.0 / D)
    weight[0] = 1.0 / D
    tau = np.minimum(t, D - t)
    ci = np.cos(2 * np.pi * ((f[:, None] * tau[None, :]) % D) / D) * weight[:, None]
    si = ci.copy()
    si[0] = np.cos(np.pi * tau) / D
    idft = np.concatenate([ci, si], 0)

    def lay(m):
        return np.ascontiguousarray(m.reshape(KD, P, -1).transpose(1, 0, 2)).astype(np.float32)
    row = np.arange(T).reshape(NT, P).T[:, :, None] * (2 * D)
    return {"ident": np.eye(P, dtype=np.float32), "mask": np.triu(np.ones((P, P), np.float32)), "dft": lay(dft), "idft": lay(idft),
            "rowbase": np.broadcast_to(row, (P, NT, 8)).astype(np.uint32)}


def kernel(**inputs):
    import numpy as np
    import concourse.bacc as bacc
    from concourse.bass_utils import run_bass_kernel_spmd

    def c(v):
        return np.ascontiguousarray(v)

    i = {k: np.asarray(v) for k, v in inputs.items()}
    arrays = {
        "x": c(i["L0_attn_x"].reshape(T, D)),
        "gate_w": c(i["L0_ffn_gate_w"]), "up_w": c(i["L0_ffn_up_w"]), "down_w": c(i["L0_ffn_down_w"]),
        "fc1_w": c(i["L0_ffn_fc1_w"]), "fc2_w": c(i["L0_ffn_fc2_w"]), "expert_w": c(i["L0_ffn_expert_w"]),
        "gamma": c(i["L0_ffn_ln_gamma"].reshape(1, D)), "beta": c(i["L0_ffn_ln_beta"].reshape(1, D)),
    }
    w_in = i["L1_attn_in_proj_w"].reshape(-1, P, D)
    order = [t for g in range(GROUPS)
             for kind, k in LOADS
             for t in ((GROUPS * KC + g * KC + k, g * KC + k) if kind == "HG"
                       else (2 * GROUPS * KC + g, (2 * KC + 1) * GROUPS + g))]
    tiles = w_in[order].reshape(-1, 2, P, KD, P)
    arrays["w_in"] = c(tiles.transpose(0, 4, 1, 3, 2).reshape(-1, P, 2 * KD * P))
    arrays["w_dt"] = c(w_in[-1].reshape(P, KD, P).transpose(2, 1, 0))
    arrays["w_out"] = c(i["L1_attn_out_proj_w"].reshape(D, GROUPS, KC, P).transpose(1, 2, 3, 0).reshape(
        GROUPS * KC, P, D))
    arrays["norm_w"] = c(i["L1_attn_norm_w"].reshape(KD, P).T)
    arrays["dt_bias"] = c(i["L1_attn_dt_bias"].reshape(P, 1))
    arrays["a_log"] = c(i["L1_attn_A_log"].reshape(P, 1))
    cw, cb = i["L1_attn_conv_w"].reshape(-1, P, CONV), i["L1_attn_conv_b"].reshape(-1, P)
    skip = np.repeat(i["L1_attn_Dp"], HP).reshape(GROUPS, KC, P)
    gn = i["L1_attn_gnorm_w"].reshape(GROUPS, KC, P)
    par = []
    for g in range(GROUPS):
        own = [GROUPS * KC + g, GROUPS * KC + GROUPS + g] + [g * KC + k for k in range(KC)]
        par.append(np.concatenate([cw[own].transpose(1, 0, 2).reshape(P, -1), cb[own].T, skip[g].T, gn[g].T], 1))
    arrays["par"] = c(np.stack(par, 1))

    def steps(m):
        return m.reshape(KI, P, KD, P).transpose(0, 3, 2, 1)
    arrays["gu_q"] = c(np.stack([steps(i[f"L1_ffn_{n}_q"]) for n in ("gate", "up")], 2).reshape(KI, P, GU))
    arrays["gu_s"] = c(np.stack([i[f"L1_ffn_{n}_s"].reshape(KI, P, KD).transpose(0, 2, 1) for n in ("gate", "up")],
                                1).reshape(KI, GU))
    arrays["d_q"] = c(i["L1_ffn_down_q"].T.reshape(KI, P, D))
    arrays["d_s"] = c(i["L1_ffn_down_s"].T)
    arrays.update(shape_tables(np))
    nc = bacc.Bacc("TRN2", target_bir_lowering=False, num_devices=1)
    a = {k: nc.dram_tensor(f"in_{k}", v.shape, mybir.dt.from_np(v.dtype), kind="ExternalInput").ap()
         for k, v in arrays.items()}
    out = nc.dram_tensor("out", (T, D), F32, kind="ExternalOutput").ap()
    program(nc, a, out)
    r = run_bass_kernel_spmd(nc, [{f"in_{k}": v for k, v in arrays.items()}], core_ids=[0])
    return r.results[0]["out"].reshape(NB, SEQ, D)
```
